# Optimizing a Trainium2 kernel written in Bass

```python
import numpy as np
import jax
import jax.numpy as jnp

def _softmax(x, axis=-1):
    return jax.nn.softmax(x, axis=axis)

def _gelu(x):
    return jax.nn.gelu(x, approximate=True)

def _silu(x):
    return jax.nn.silu(x)

def _sigmoid(x):
    return jax.nn.sigmoid(x)

def _layernorm(x, axis=-1, eps=1e-05):
    m = jnp.mean(x, axis=axis, keepdims=True)
    v = jnp.var(x, axis=axis, keepdims=True)
    return (x - m) / jnp.sqrt(v + eps)

def _scatter_add(tgt, idx, src, axis=0):
    return tgt.at[idx].add(src)

def _segment_sum(src, seg, n):
    return jax.ops.segment_sum(src, seg, n)
kernel_name = 'mk_hybrid_d2_jaxref_r8_8602c6'

def setup_inputs(seed: int=0):
    np.random.seed(seed)
    _w = jnp.asarray

    def _L0_attn_a_setup():
        import jax, jax.numpy as jnp
        import numpy as np
        H = 4
        DK = 128
        DV = 32
        LOW_RANK = 16
        GATE_NORM = 16.0
        CHUNK = 64
        EPS = 1e-05

        def _gla_chunk(q, k, v, gk):
            B, T, _, _ = q.shape
            NC, C = (T // CHUNK, CHUNK)
            scale = DK ** (-0.5)

            def chunks(a):
                return a.reshape(B, NC, C, H, a.shape[-1]).transpose(1, 0, 3, 2, 4)
            qc, kc, vc, gc = (chunks(q), chunks(k), chunks(v), chunks(gk))
            G = jnp.cumsum(gc, axis=-2)
            qg = qc * jnp.exp(G) * scale
            k_intra = kc * jnp.exp(-G)
            kg = kc * jnp.exp(G[..., -1:, :] - G)
            g_last = jnp.exp(G[..., -1, :])
            A = jnp.einsum('nbhik,nbhjk->nbhij', qg, k_intra)
            A = jnp.where(jnp.tril(jnp.ones((C, C), bool)), A, 0.0)
            o_intra = jnp.einsum('nbhij,nbhjv->nbhiv', A, vc)

            def step(S, inp):
                qg_, kg_, v_, gl_, oi_ = inp
                o = oi_ + jnp.einsum('bhck,bhkv->bhcv', qg_, S)
                S = S * gl_[..., :, None] + jnp.einsum('bhck,bhcv->bhkv', kg_, v_)
                return (S, o)
            S0 = jnp.zeros((B, H, DK, DV), q.dtype)
            _, o = jax.lax.scan(step, S0, (qg, kg, vc, g_last, o_intra))
            return o.transpose(1, 0, 3, 2, 4).reshape(B, T, H, DV)
        key = jax.random.key(seed)
        ks = jax.random.split(key, 10)
        Dm = 128
        Kd, Vd = (H * DK, H * DV)

        def lin(k, fan_in, fan_out):
            return jax.random.normal(k, (fan_in, fan_out), jnp.float32) * fan_in ** (-0.5)
        return {'x': jax.random.normal(ks[0], (4, 256, Dm), jnp.float32), 'Wq': lin(ks[1], Dm, Kd), 'Wk': lin(ks[2], Dm, Kd), 'Wv': lin(ks[3], Dm, Vd), 'Wg': lin(ks[4], Dm, Vd), 'Wgk1': lin(ks[5], Dm, LOW_RANK), 'Wgk2': lin(ks[6], LOW_RANK, Kd), 'bgk2': jnp.zeros((Kd,), jnp.float32), 'Wo': lin(ks[7], Vd, Dm), 'gnw': jnp.ones((DV,), jnp.float32)}
    _L0_attn_a_in = _L0_attn_a_setup()

    def _L0_attn_b_setup():
        import jax, jax.numpy as jnp
        import numpy as np
        key = jax.random.key(seed)
        k_u, k_lam, k_B, k_C = jax.random.split(key, 4)
        batch, seq_len, d_model, N = (4, 512, 128, 64)
        return {'u': jax.random.normal(k_u, (batch, seq_len, d_model), dtype=jnp.float32), 'Lambda': jax.random.normal(k_lam, (N,), dtype=jnp.float32), 'log_dt': jnp.zeros((1,), dtype=jnp.float32), 'B': jax.random.normal(k_B, (N, d_model), dtype=jnp.float32), 'C': jax.random.normal(k_C, (d_model, N), dtype=jnp.float32), 'D': jnp.zeros((d_model,), dtype=jnp.float32)}
    _L0_attn_b_in = _L0_attn_b_setup()

    def _L0_ffn_setup():
        import jax, jax.numpy as jnp
        import numpy as np
        D_IN, D_HID = (128, 512)

        def _ternary(key, shape):
            return jax.random.randint(key, shape, -1, 2).astype(jnp.float32)

        def _tlin(x, w, s):
            return jnp.einsum('bsi,oi->bso', x, w) * s
        key = jax.random.key(seed)
        ks = jax.random.split(key, 12)
        inv = lambda fan: 1.0 / np.sqrt(fan).astype(np.float32)
        return {'x': jax.random.normal(ks[0], (4, 256, D_IN), dtype=jnp.float32), 'w1_w': _ternary(ks[1], (D_HID, D_IN)), 'w1_s': jax.random.uniform(ks[2], (D_HID,), dtype=jnp.float32) * inv(D_IN), 'w2_w': _ternary(ks[3], (D_HID, D_IN)), 'w2_s': jax.random.uniform(ks[4], (D_HID,), dtype=jnp.float32) * inv(D_IN), 'h1_w': _ternary(ks[5], (D_HID, D_HID)), 'h1_s': jax.random.uniform(ks[6], (D_HID,), dtype=jnp.float32) * inv(D_HID), 'h2_w': _ternary(ks[7], (D_HID, D_HID)), 'h2_s': jax.random.uniform(ks[8], (D_HID,), dtype=jnp.float32) * inv(D_HID), 'w3_w': _ternary(ks[9], (D_IN, D_HID)), 'w3_s': jax.random.uniform(ks[10], (D_IN,), dtype=jnp.float32) * inv(D_HID)}
    _L0_ffn_in = _L0_ffn_setup()

    def _L1_attn_a_setup():
        import jax, jax.numpy as jnp
        import numpy as np
        B, L = (2, 128)
        D_MODEL, D_CKV, D_CQ = (128, 32, 64)
        N_HEAD, D_HEAD, D_ROPE = (8, 64, 32)
        N_IDX_HEAD = 4
        K_TS, LW = (96, 64)
        ROPE_BASE = 10000.0

        def _pope(x, angles):
            cos, sin = (jnp.cos(angles), jnp.sin(angles))
            mu1, mu2 = jnp.split(jax.nn.softplus(x), 2, axis=-1)
            return jnp.concatenate([mu1 * cos - mu2 * sin, mu1 * sin + mu2 * cos], axis=-1)

        def _forward(x, W_dkv, W_uk, W_uv, W_dq, W_uq, W_qr, W_kr, W_out, idx_wq, idx_wk, idx_w, raw_delta):
            B_, L_, _ = x.shape
            c_kv = x @ W_dkv
            q_i = (x @ idx_wq).reshape(B_, L_, N_IDX_HEAD, D_HEAD)
            k_i = x @ idx_wk
            s_i = jax.nn.relu(jnp.einsum('bthd,bsd->bths', q_i, k_i))
            I = jnp.einsum('bths,h->bts', s_i, idx_w)
            qpos = jnp.arange(L_)[:, None]
            kpos = jnp.arange(L_)[None, :]
            local = (kpos >= qpos - LW + 1) & (kpos <= qpos)
            causal = kpos > qpos
            I = jnp.where(local[None], jnp.inf, I)
            I = jnp.where(causal[None], -jnp.inf, I)
            kk = min(K_TS, L_)
            _, idx = jax.lax.top_k(I, kk)
            bi = jnp.arange(B_)[:, None, None]
            key_c = (c_kv @ W_uk)[bi, idx].reshape(B_, L_, kk, N_HEAD, D_HEAD)
            value = (c_kv @ W_uv)[bi, idx].reshape(B_, L_, kk, N_HEAD, D_HEAD)
            c_q = x @ W_dq
            query_c = (c_q @ W_uq).reshape(B_, L_, N_HEAD, D_HEAD)
            half = D_ROPE // 2
            theta = 1.0 / ROPE_BASE ** (2.0 * jnp.arange(half, dtype=jnp.float32) / D_ROPE)
            delta = -2.0 * jnp.pi * jax.nn.sigmoid(raw_delta)
            angles_q = jnp.arange(L_, dtype=jnp.float32)[:, None] * theta[None, :] + delta
            query_r = _pope((c_q @ W_qr).reshape(B_, L_, N_HEAD, D_ROPE), angles_q[None, :, None, :])
            kr_sel = (x @ W_kr)[bi, idx]
            angles_k = jnp.arange(kk, dtype=jnp.float32)[:, None] * theta[None, :] + delta
            key_r = _pope(kr_sel, angles_k[None, None, :, :])
            scale = (D_HEAD + D_ROPE) ** (-0.5)
            q_c = query_c.transpose(0, 2, 1, 3)
            q_r = query_r.transpose(0, 2, 1, 3)
            k_c = key_c.transpose(0, 3, 1, 2, 4)
            v = value.transpose(0, 3, 1, 2, 4)
            scores = (jnp.einsum('bhld,bhlkd->bhlk', q_c, k_c) + jnp.einsum('bhld,blkd->bhlk', q_r, key_r)) * scale
            attn = jax.nn.softmax(scores.astype(jnp.float32), axis=-1).astype(v.dtype)
            out = jnp.einsum('bhlk,bhlkd->bhld', attn, v)
            out = out.transpose(0, 2, 1, 3).reshape(B_, L_, N_HEAD * D_HEAD)
            return out @ W_out
        key = jax.random.key(seed)
        ks = jax.random.split(key, 14)

        def w(k, shape, fan_in):
            return jax.random.normal(k, shape, dtype=jnp.float32) * fan_in ** (-0.5)
        return {'x': jax.random.normal(ks[0], (B, L, D_MODEL), dtype=jnp.float32), 'W_dkv': w(ks[1], (D_MODEL, D_CKV), D_MODEL), 'W_uk': w(ks[2], (D_CKV, N_HEAD * D_HEAD), D_CKV), 'W_uv': w(ks[3], (D_CKV, N_HEAD * D_HEAD), D_CKV), 'W_dq': w(ks[4], (D_MODEL, D_CQ), D_MODEL), 'W_uq': w(ks[5], (D_CQ, N_HEAD * D_HEAD), D_CQ), 'W_qr': w(ks[6], (D_CQ, N_HEAD * D_ROPE), D_CQ), 'W_kr': w(ks[7], (D_MODEL, D_ROPE), D_MODEL), 'W_out': w(ks[8], (N_HEAD * D_HEAD, D_MODEL), N_HEAD * D_HEAD), 'idx_wq': w(ks[9], (D_MODEL, N_IDX_HEAD * D_HEAD), D_MODEL), 'idx_wk': w(ks[10], (D_MODEL, D_HEAD), D_MODEL), 'idx_w': jnp.ones((N_IDX_HEAD,), dtype=jnp.float32), 'raw_delta': jax.random.normal(ks[11], (D_ROPE // 2,), dtype=jnp.float32) * 0.1}
    _L1_attn_a_in = _L1_attn_a_setup()

    def _L1_attn_b_setup():
        import jax, jax.numpy as jnp
        import numpy as np
        EPS = 1e-06
        N_HEADS = 16

        def _heads(t, B, N, H, Dk):
            return t.reshape(B, N, H, Dk).transpose(0, 2, 1, 3)
        key = jax.random.key(seed)
        ks = jax.random.split(key, 5)
        B, N, D = (64, 64, 128)
        x = jax.random.normal(ks[0], (B, N, D), dtype=jnp.float32)
        s = 0.02
        W_q = jax.random.normal(ks[1], (D, D), dtype=jnp.float32) * s
        W_k = jax.random.normal(ks[2], (D, D), dtype=jnp.float32) * s
        W_v = jax.random.normal(ks[3], (D, D), dtype=jnp.float32) * s
        W_o = jax.random.normal(ks[4], (D, D), dtype=jnp.float32) * s
        z = jnp.zeros((D,), dtype=jnp.float32)
        return {'x': x, 'W_q': W_q, 'b_q': z, 'W_k': W_k, 'b_k': z, 'W_v': W_v, 'b_v': z, 'W_o': W_o, 'b_o': z}
    _L1_attn_b_in = _L1_attn_b_setup()

    def _L1_ffn_setup():
        import jax, jax.numpy as jnp
        import numpy as np
        DIM = 128
        HIDDEN = 384
        SCALE = 1.0 / 127.0

        def _dequant(w_int, dtype):
            return w_int.astype(dtype) * jnp.asarray(SCALE, dtype)
        key = jax.random.key(seed)
        k_x, k_g, k_u, k_d = jax.random.split(key, 4)
        x = jax.random.normal(k_x, (4, 256, DIM), dtype=jnp.float32)
        w_gate = jax.random.randint(k_g, (HIDDEN, DIM), -127, 128, dtype=jnp.int32)
        w_up = jax.random.randint(k_u, (HIDDEN, DIM), -127, 128, dtype=jnp.int32)
        w_down = jax.random.randint(k_d, (DIM, HIDDEN), -127, 128, dtype=jnp.int32)
        return {'x': x, 'w_gate': w_gate, 'w_up': w_up, 'w_down': w_down}
    _L1_ffn_in = _L1_ffn_setup()
    _d = {'L0_attn_a_x': _L0_attn_a_in['x'], 'L0_attn_a_Wq': _L0_attn_a_in['Wq'], 'L0_attn_a_Wk': _L0_attn_a_in['Wk'], 'L0_attn_a_Wv': _L0_attn_a_in['Wv'], 'L0_attn_a_Wg': _L0_attn_a_in['Wg'], 'L0_attn_a_Wgk1': _L0_attn_a_in['Wgk1'], 'L0_attn_a_Wgk2': _L0_attn_a_in['Wgk2'], 'L0_attn_a_bgk2': _L0_attn_a_in['bgk2'], 'L0_attn_a_Wo': _L0_attn_a_in['Wo'], 'L0_attn_a_gnw': _L0_attn_a_in['gnw'], 'L0_attn_b_Lambda': _L0_attn_b_in['Lambda'], 'L0_attn_b_log_dt': _L0_attn_b_in['log_dt'], 'L0_attn_b_B': _L0_attn_b_in['B'], 'L0_attn_b_C': _L0_attn_b_in['C'], 'L0_attn_b_D': _L0_attn_b_in['D'], 'L0_ffn_w1_w': _L0_ffn_in['w1_w'], 'L0_ffn_w1_s': _L0_ffn_in['w1_s'], 'L0_ffn_w2_w': _L0_ffn_in['w2_w'], 'L0_ffn_w2_s': _L0_ffn_in['w2_s'], 'L0_ffn_h1_w': _L0_ffn_in['h1_w'], 'L0_ffn_h1_s': _L0_ffn_in['h1_s'], 'L0_ffn_h2_w': _L0_ffn_in['h2_w'], 'L0_ffn_h2_s': _L0_ffn_in['h2_s'], 'L0_ffn_w3_w': _L0_ffn_in['w3_w'], 'L0_ffn_w3_s': _L0_ffn_in['w3_s'], 'L1_attn_a_W_dkv': _L1_attn_a_in['W_dkv'], 'L1_attn_a_W_uk': _L1_attn_a_in['W_uk'], 'L1_attn_a_W_uv': _L1_attn_a_in['W_uv'], 'L1_attn_a_W_dq': _L1_attn_a_in['W_dq'], 'L1_attn_a_W_uq': _L1_attn_a_in['W_uq'], 'L1_attn_a_W_qr': _L1_attn_a_in['W_qr'], 'L1_attn_a_W_kr': _L1_attn_a_in['W_kr'], 'L1_attn_a_W_out': _L1_attn_a_in['W_out'], 'L1_attn_a_idx_wq': _L1_attn_a_in['idx_wq'], 'L1_attn_a_idx_wk': _L1_attn_a_in['idx_wk'], 'L1_attn_a_idx_w': _L1_attn_a_in['idx_w'], 'L1_attn_a_raw_delta': _L1_attn_a_in['raw_delta'], 'L1_attn_b_W_q': _L1_attn_b_in['W_q'], 'L1_attn_b_b_q': _L1_attn_b_in['b_q'], 'L1_attn_b_W_k': _L1_attn_b_in['W_k'], 'L1_attn_b_b_k': _L1_attn_b_in['b_k'], 'L1_attn_b_W_v': _L1_attn_b_in['W_v'], 'L1_attn_b_b_v': _L1_attn_b_in['b_v'], 'L1_attn_b_W_o': _L1_attn_b_in['W_o'], 'L1_attn_b_b_o': _L1_attn_b_in['b_o'], 'L1_ffn_w_gate': _L1_ffn_in['w_gate'], 'L1_ffn_w_up': _L1_ffn_in['w_up'], 'L1_ffn_w_down': _L1_ffn_in['w_down']}
    _x0 = _d['L0_attn_a_x']
    _d['L0_attn_a_x'] = jax.random.normal(jax.random.fold_in(jax.random.key(seed), 1), (1, 2048, 128), dtype=_x0.dtype)
    del _x0
    return _d

def reference(L0_attn_a_x, L0_attn_a_Wq, L0_attn_a_Wk, L0_attn_a_Wv, L0_attn_a_Wg, L0_attn_a_Wgk1, L0_attn_a_Wgk2, L0_attn_a_bgk2, L0_attn_a_Wo, L0_attn_a_gnw, L0_attn_b_Lambda, L0_attn_b_log_dt, L0_attn_b_B, L0_attn_b_C, L0_attn_b_D, L0_ffn_w1_w, L0_ffn_w1_s, L0_ffn_w2_w, L0_ffn_w2_s, L0_ffn_h1_w, L0_ffn_h1_s, L0_ffn_h2_w, L0_ffn_h2_s, L0_ffn_w3_w, L0_ffn_w3_s, L1_attn_a_W_dkv, L1_attn_a_W_uk, L1_attn_a_W_uv, L1_attn_a_W_dq, L1_attn_a_W_uq, L1_attn_a_W_qr, L1_attn_a_W_kr, L1_attn_a_W_out, L1_attn_a_idx_wq, L1_attn_a_idx_wk, L1_attn_a_idx_w, L1_attn_a_raw_delta, L1_attn_b_W_q, L1_attn_b_b_q, L1_attn_b_W_k, L1_attn_b_b_k, L1_attn_b_W_v, L1_attn_b_b_v, L1_attn_b_W_o, L1_attn_b_b_o, L1_ffn_w_gate, L1_ffn_w_up, L1_ffn_w_down):

    def _L0_attn_a_ref(x, Wq, Wk, Wv, Wg, Wgk1, Wgk2, bgk2, Wo, gnw):
        import jax, jax.numpy as jnp
        import numpy as np
        H = 4
        DK = 128
        DV = 32
        LOW_RANK = 16
        GATE_NORM = 16.0
        CHUNK = 64
        EPS = 1e-05

        def _gla_chunk(q, k, v, gk):
            B, T, _, _ = q.shape
            NC, C = (T // CHUNK, CHUNK)
            scale = DK ** (-0.5)

            def chunks(a):
                return a.reshape(B, NC, C, H, a.shape[-1]).transpose(1, 0, 3, 2, 4)
            qc, kc, vc, gc = (chunks(q), chunks(k), chunks(v), chunks(gk))
            G = jnp.cumsum(gc, axis=-2)
            qg = qc * jnp.exp(G) * scale
            k_intra = kc * jnp.exp(-G)
            kg = kc * jnp.exp(G[..., -1:, :] - G)
            g_last = jnp.exp(G[..., -1, :])
            A = jnp.einsum('nbhik,nbhjk->nbhij', qg, k_intra)
            A = jnp.where(jnp.tril(jnp.ones((C, C), bool)), A, 0.0)
            o_intra = jnp.einsum('nbhij,nbhjv->nbhiv', A, vc)

            def step(S, inp):
                qg_, kg_, v_, gl_, oi_ = inp
                o = oi_ + jnp.einsum('bhck,bhkv->bhcv', qg_, S)
                S = S * gl_[..., :, None] + jnp.einsum('bhck,bhcv->bhkv', kg_, v_)
                return (S, o)
            S0 = jnp.zeros((B, H, DK, DV), q.dtype)
            _, o = jax.lax.scan(step, S0, (qg, kg, vc, g_last, o_intra))
            return o.transpose(1, 0, 3, 2, 4).reshape(B, T, H, DV)
        B, T, Dm = x.shape
        q = (x @ Wq).reshape(B, T, H, DK)
        k = (x @ Wk).reshape(B, T, H, DK)
        v = (x @ Wv).reshape(B, T, H, DV)
        gk = jax.nn.log_sigmoid(x @ Wgk1 @ Wgk2 + bgk2) / GATE_NORM
        gk = gk.reshape(B, T, H, DK)
        o = _gla_chunk(q, k, v, gk)
        g = (x @ Wg).reshape(B, T, H, DV)
        o = o * jax.lax.rsqrt(jnp.mean(o * o, axis=-1, keepdims=True) + EPS) * gnw
        o = o * (g * jax.nn.sigmoid(g))
        return o.reshape(B, T, H * DV) @ Wo

    def _L0_attn_b_ref(u, Lambda, log_dt, B, C, D):
        import jax, jax.numpy as jnp
        import numpy as np
        dt = jnp.exp(log_dt)
        a = jnp.exp(-dt * jnp.exp(Lambda))
        Bu = jnp.einsum('bld,nd->bln', u, B)

        def step(x, bu_t):
            x = a * x + bu_t
            return (x, x)
        x0 = jnp.zeros((u.shape[0], Lambda.shape[0]), dtype=u.dtype)
        _, xs = jax.lax.scan(step, x0, jnp.swapaxes(Bu, 0, 1))
        xs = jnp.swapaxes(xs, 0, 1)
        return jnp.einsum('bln,dn->bld', xs, C) + D * u

    def _L0_ffn_ref(x, w1_w, w1_s, w2_w, w2_s, h1_w, h1_s, h2_w, h2_s, w3_w, w3_s):
        import jax, jax.numpy as jnp
        import numpy as np
        D_IN, D_HID = (128, 512)

        def _ternary(key, shape):
            return jax.random.randint(key, shape, -1, 2).astype(jnp.float32)

        def _tlin(x, w, s):
            return jnp.einsum('bsi,oi->bso', x, w) * s
        h = jax.nn.silu(_tlin(x, w1_w, w1_s)) * _tlin(x, w2_w, w2_s)
        h = jax.nn.gelu(_tlin(h, h1_w, h1_s), approximate=False)
        h = jax.nn.gelu(_tlin(h, h2_w, h2_s), approximate=False)
        return _tlin(h, w3_w, w3_s)

    def _L1_attn_a_ref(x, W_dkv, W_uk, W_uv, W_dq, W_uq, W_qr, W_kr, W_out, idx_wq, idx_wk, idx_w, raw_delta):
        import jax, jax.numpy as jnp
        import numpy as np
        B, L = (2, 128)
        D_MODEL, D_CKV, D_CQ = (128, 32, 64)
        N_HEAD, D_HEAD, D_ROPE = (8, 64, 32)
        N_IDX_HEAD = 4
        K_TS, LW = (96, 64)
        ROPE_BASE = 10000.0

        def _pope(x, angles):
            cos, sin = (jnp.cos(angles), jnp.sin(angles))
            mu1, mu2 = jnp.split(jax.nn.softplus(x), 2, axis=-1)
            return jnp.concatenate([mu1 * cos - mu2 * sin, mu1 * sin + mu2 * cos], axis=-1)

        def _forward(x, W_dkv, W_uk, W_uv, W_dq, W_uq, W_qr, W_kr, W_out, idx_wq, idx_wk, idx_w, raw_delta):
            B_, L_, _ = x.shape
            c_kv = x @ W_dkv
            q_i = (x @ idx_wq).reshape(B_, L_, N_IDX_HEAD, D_HEAD)
            k_i = x @ idx_wk
            s_i = jax.nn.relu(jnp.einsum('bthd,bsd->bths', q_i, k_i))
            I = jnp.einsum('bths,h->bts', s_i, idx_w)
            qpos = jnp.arange(L_)[:, None]
            kpos = jnp.arange(L_)[None, :]
            local = (kpos >= qpos - LW + 1) & (kpos <= qpos)
            causal = kpos > qpos
            I = jnp.where(local[None], jnp.inf, I)
            I = jnp.where(causal[None], -jnp.inf, I)
            kk = min(K_TS, L_)
            _, idx = jax.lax.top_k(I, kk)
            bi = jnp.arange(B_)[:, None, None]
            key_c = (c_kv @ W_uk)[bi, idx].reshape(B_, L_, kk, N_HEAD, D_HEAD)
            value = (c_kv @ W_uv)[bi, idx].reshape(B_, L_, kk, N_HEAD, D_HEAD)
            c_q = x @ W_dq
            query_c = (c_q @ W_uq).reshape(B_, L_, N_HEAD, D_HEAD)
            half = D_ROPE // 2
            theta = 1.0 / ROPE_BASE ** (2.0 * jnp.arange(half, dtype=jnp.float32) / D_ROPE)
            delta = -2.0 * jnp.pi * jax.nn.sigmoid(raw_delta)
            angles_q = jnp.arange(L_, dtype=jnp.float32)[:, None] * theta[None, :] + delta
            query_r = _pope((c_q @ W_qr).reshape(B_, L_, N_HEAD, D_ROPE), angles_q[None, :, None, :])
            kr_sel = (x @ W_kr)[bi, idx]
            angles_k = jnp.arange(kk, dtype=jnp.float32)[:, None] * theta[None, :] + delta
            key_r = _pope(kr_sel, angles_k[None, None, :, :])
            scale = (D_HEAD + D_ROPE) ** (-0.5)
            q_c = query_c.transpose(0, 2, 1, 3)
            q_r = query_r.transpose(0, 2, 1, 3)
            k_c = key_c.transpose(0, 3, 1, 2, 4)
            v = value.transpose(0, 3, 1, 2, 4)
            scores = (jnp.einsum('bhld,bhlkd->bhlk', q_c, k_c) + jnp.einsum('bhld,blkd->bhlk', q_r, key_r)) * scale
            attn = jax.nn.softmax(scores.astype(jnp.float32), axis=-1).astype(v.dtype)
            out = jnp.einsum('bhlk,bhlkd->bhld', attn, v)
            out = out.transpose(0, 2, 1, 3).reshape(B_, L_, N_HEAD * D_HEAD)
            return out @ W_out
        return _forward(x, W_dkv, W_uk, W_uv, W_dq, W_uq, W_qr, W_kr, W_out, idx_wq, idx_wk, idx_w, raw_delta)

    def _L1_attn_b_ref(x, W_q, b_q, W_k, b_k, W_v, b_v, W_o, b_o):
        import jax, jax.numpy as jnp
        import numpy as np
        EPS = 1e-06
        N_HEADS = 16

        def _heads(t, B, N, H, Dk):
            return t.reshape(B, N, H, Dk).transpose(0, 2, 1, 3)
        B, N, Dm = x.shape
        H = N_HEADS
        Dk = Dm // H
        q = _heads(x @ W_q.T + b_q, B, N, H, Dk)
        k = _heads(x @ W_k.T + b_k, B, N, H, Dk)
        v = _heads(x @ W_v.T + b_v, B, N, H, Dk)
        dec = jnp.exp(-jnp.arange(N, dtype=jnp.float32) / N)[None, None, :, None]
        qf = jax.nn.relu(q) * dec
        kf = jax.nn.relu(k) * dec
        KV = jnp.einsum('bhnd,bhne->bhde', kf, v)
        Ksum = kf.sum(axis=2)
        denom = jnp.einsum('bhnd,bhd->bhn', qf, Ksum) + EPS
        out = jnp.einsum('bhnd,bhde->bhne', qf, KV) / denom[..., None]
        out = out.transpose(0, 2, 1, 3).reshape(B, N, Dm)
        return out @ W_o.T + b_o

    def _L1_ffn_ref(x, w_gate, w_up, w_down):
        import jax, jax.numpy as jnp
        import numpy as np
        DIM = 128
        HIDDEN = 384
        SCALE = 1.0 / 127.0

        def _dequant(w_int, dtype):
            return w_int.astype(dtype) * jnp.asarray(SCALE, dtype)
        wg = _dequant(w_gate, x.dtype)
        wu = _dequant(w_up, x.dtype)
        wd = _dequant(w_down, x.dtype)
        gate = jnp.einsum('bsd,hd->bsh', x, wg)
        up = jnp.einsum('bsd,hd->bsh', x, wu)
        h = jax.nn.silu(gate) * up
        return jnp.einsum('bsh,dh->bsd', h, wd)
    x = L0_attn_a_x
    x = x + _L0_attn_a_ref(_layernorm(x, axis=-1), L0_attn_a_Wq, L0_attn_a_Wk, L0_attn_a_Wv, L0_attn_a_Wg, L0_attn_a_Wgk1, L0_attn_a_Wgk2, L0_attn_a_bgk2, L0_attn_a_Wo, L0_attn_a_gnw)
    x = x + _L0_ffn_ref(_layernorm(x, axis=-1), L0_ffn_w1_w, L0_ffn_w1_s, L0_ffn_w2_w, L0_ffn_w2_s, L0_ffn_h1_w, L0_ffn_h1_s, L0_ffn_h2_w, L0_ffn_h2_s, L0_ffn_w3_w, L0_ffn_w3_s)
    x = x + _L0_attn_b_ref(_layernorm(x, axis=-1), L0_attn_b_Lambda, L0_attn_b_log_dt, L0_attn_b_B, L0_attn_b_C, L0_attn_b_D)
    x = x + _L0_ffn_ref(_layernorm(x, axis=-1), L0_ffn_w1_w, L0_ffn_w1_s, L0_ffn_w2_w, L0_ffn_w2_s, L0_ffn_h1_w, L0_ffn_h1_s, L0_ffn_h2_w, L0_ffn_h2_s, L0_ffn_w3_w, L0_ffn_w3_s)
    x = x + _L1_attn_a_ref(_layernorm(x, axis=-1), L1_attn_a_W_dkv, L1_attn_a_W_uk, L1_attn_a_W_uv, L1_attn_a_W_dq, L1_attn_a_W_uq, L1_attn_a_W_qr, L1_attn_a_W_kr, L1_attn_a_W_out, L1_attn_a_idx_wq, L1_attn_a_idx_wk, L1_attn_a_idx_w, L1_attn_a_raw_delta)
    x = x + _L1_ffn_ref(_layernorm(x, axis=-1), L1_ffn_w_gate, L1_ffn_w_up, L1_ffn_w_down)
    x = x + _L1_attn_b_ref(_layernorm(x, axis=-1), L1_attn_b_W_q, L1_attn_b_b_q, L1_attn_b_W_k, L1_attn_b_b_k, L1_attn_b_W_v, L1_attn_b_b_v, L1_attn_b_W_o, L1_attn_b_b_o)
    x = x + _L1_ffn_ref(_layernorm(x, axis=-1), L1_ffn_w_gate, L1_ffn_w_up, L1_ffn_w_down)
    return x

_drawn_inputs = setup_inputs


def setup_inputs(seed=0):
    import zlib

    import numpy as np

    out = dict(_drawn_inputs(seed))
    spreads = {'L0_attn_a_bgk2': (0.0, 0.1),
     'L0_attn_a_gnw': (1.0, 0.2),
     'L0_attn_b_D': (0.0, 0.1),
     'L1_attn_a_idx_w': (1.0, 0.2),
     'L1_attn_b_b_q': (0.0, 0.1),
     'L1_attn_b_b_k': (0.0, 0.1),
     'L1_attn_b_b_v': (0.0, 0.1),
     'L1_attn_b_b_o': (0.0, 0.1)}
    factors = {}
    for name, (base, spread) in spreads.items():
        noise = np.random.default_rng([zlib.crc32(name.encode()), seed]).standard_normal(out[name].shape)
        drawn = base * np.exp(spread * noise) if base else spread * noise
        out[name] = jnp.asarray(drawn.astype(out[name].dtype))
    for name, factor in factors.items():
        out[name] = (out[name] * factor).astype(out[name].dtype)
    return out
```

```python
from contextlib import ExitStack

import numpy as np

import concourse.bass as bass
from concourse import mybir

F32 = mybir.dt.float32
I32 = mybir.dt.int32
U32 = mybir.dt.uint32
ALU = mybir.AluOpType
ACT = mybir.ActivationFunctionType

P = 128
T = 2048
C = 512
NCH = T // C
NT = T // P
EPS_LN = 1e-5
LN0 = 2
STORES_K, STORES_Q = 16, 96
EPS_LIN = 1e-6
GH, GDK, GDV, GCHUNK = 4, 128, 32, 64
NH, DR, DC, DCQ, DH = 8, 32, 32, 64, 64
NIH = 4
KTOP, LW = 96, 64
JG = KTOP - LW
ROW = 2 * DR + DC
SCALE = (DH + DR) ** -0.5
GQ = 16
NG = P // GQ
WIN = LW + GQ
KEYS = GQ * JG + WIN
NEG = -1e30
LOWEST = -3e38
TAKEN = -3.3e38
HID = 512
NM = HID // P
HID2 = 384
NM2 = HID2 // P
LH, LDK = 16, 8


def shape_tables():
    f32 = np.float32
    t = {}
    t["ident"] = np.eye(P, dtype=f32)
    t["center"] = (np.eye(P) - 1.0 / P).astype(f32)
    t["mean_all"] = np.full((P, P), 1.0 / P, f32)
    same = np.arange(P)[:, None] // GDV == np.arange(P)[None, :] // GDV
    t["mean_head"] = (same / GDV).astype(f32)
    t["same_head"] = (np.arange(P)[:, None] // LDK == np.arange(P)[None, :] // LDK).astype(f32)
    j, i = np.arange(P)[:, None], np.arange(P)[None, :]
    t["gla_mask"] = ((j <= i) & (j // GCHUNK == i // GCHUNK)).astype(f32)
    t["scan_keep"] = np.tile((np.arange(P) % GCHUNK != 0).astype(f32), (P, GH))
    cols = np.zeros((P, 4), f32)
    cols[:, 0] = EPS_LN
    cols[:, 1] = 1.0
    t["cols"] = cols
    half = DR // 2
    theta = 1.0 / 10000.0 ** (2.0 * np.arange(half) / DR)
    pos = np.arange(T)
    q_g = theta[:, None] * pos[None, :]
    q_l = theta[:, None] * (pos + np.maximum(pos - (LW - 1), 0))[None, :]
    for name, a in (("qg", q_g), ("ql", q_l)):
        t["cos_" + name] = np.tile(np.cos(a), (NH, 1)).astype(f32)
        t["sin_" + name] = np.tile(np.sin(a), (NH, 1)).astype(f32)
    c, s = np.cos(q_g), np.sin(q_g)
    t["key_rope"] = np.concatenate([c, c, -s, s]).astype(f32)
    a = (LW + np.arange(JG))[:, None] * theta[None, :]
    row = np.concatenate([np.cos(a), np.cos(a), -np.sin(a), np.sin(a), np.ones((JG, DC))], axis=1)
    t["rank_rope"] = np.tile(row, (P // JG, 1)).astype(f32)
    q = np.arange(P) % GQ
    own = (np.arange(GQ * JG) // JG)[None, :] == q[:, None]
    x = np.arange(WIN)[None, :]
    near = (x >= 1 + q[:, None]) & (x <= LW + q[:, None])
    first = np.broadcast_to(x < LW, (P, WIN))
    t["score_mask"] = np.where(np.concatenate([own, near], 1), 0, NEG).astype(f32)
    t["score_mask_first"] = np.where(np.concatenate([own, first], 1), 0, NEG).astype(f32)
    p, s = np.arange(P)[:, None], np.arange(KTOP)[None, :]
    past, local = s <= p - LW, (s <= p) & (s > p - LW)
    local = local | ((p < LW) & (s < LW))
    t["index_mask_first"] = np.where(local, LOWEST, np.where(past, 0, NEG)).astype(f32)
    t["index_mask"] = np.where(np.arange(P)[None, :] <= p, 0, LOWEST).astype(f32)
    dec = np.exp(-np.arange(T, dtype=f32) / f32(T)).astype(f32)
    t["decay_row"] = np.broadcast_to(dec, (P, T))
    t["decay_col"] = dec.reshape(NT, P).T
    t["ones_row"] = np.ones((1, P), f32)
    return t


TABLES = ["ident", "center", "mean_all", "mean_head", "same_head", "gla_mask", "scan_keep", "cols", "cos_qg",
          "sin_qg", "cos_ql", "sin_ql", "key_rope", "rank_rope", "score_mask", "score_mask_first",
          "index_mask_first", "index_mask", "decay_row", "decay_col", "ones_row"]


class Steps:

    def __init__(self, eng, sem):
        self.eng, self.sem, self.base, self.loop, self.k = eng, sem, 0, 0, 0

    def enter(self, i, per):
        self.loop, self.k = i * per, 0

    def leave(self, per, times):
        assert self.k == per, (self.k, per)
        self.base, self.loop, self.k = self.base + per * times, 0, 0

    def did(self, ins):
        self.k += 1
        ins.then_inc(self.sem, 1)
        self.eng.wait_ge(self.sem, self.base + self.loop + self.k)


def hybrid_kernel(nc, d, out):
    with ExitStack() as ctx:
        def sem(name):
            return ctx.enter_context(nc.semaphore(name))

        def sb(name, shape, dt=F32):
            return ctx.enter_context(nc.sbuf_tensor(name, shape, dt))

        def dram(name, shape):
            return nc.dram_tensor(name, shape, F32, kind="Internal").ap()

        bank2 = [ctx.enter_context(nc.psum_tensor(f"bank{2 * i}_{2 * i + 1}", [P, 2 * C], F32)) for i in range(4)]
        bank = [bank2[i // 2][:, (i % 2) * C:(i % 2) * C + C] for i in range(8)]

        x = sb("x", [P, T])
        xn = sb("xn", [P, T])
        LOAD = {}

        def load(name, dt=F32):
            LOAD[name] = sb(name, list(d[name].shape), dt)
            return LOAD[name]

        ident, center, mean_all, mean_head = load("ident"), load("center"), load("mean_all"), load("mean_head")
        same_head, gla_mask, scan_keep, cols = load("same_head"), load("gla_mask"), load("scan_keep"), load("cols")
        rank_rope, ones_row = load("rank_rope"), load("ones_row")
        score_mask, score_mask_first = load("score_mask"), load("score_mask_first")
        index_mask, index_mask_first, decay_col = load("index_mask"), load("index_mask_first"), load("decay_col")
        eps_col, one_col = cols[:, 0:1], cols[:, 1:2]
        gWv, gWg, gWo, Wgk1, Wgk2 = (load(n) for n in ("gWv", "gWg", "gWo", "Wgk1", "Wgk2"))
        bgk2, gnw = load("bgk2"), load("gnw")
        lam, log_dt, sBT, sCT, sD = (load(n) for n in ("lam", "log_dt", "sBT", "sCT", "sD"))
        w1, w2, h1, h2, w3 = (load(n) for n in ("w1", "w2", "h1", "h2", "w3"))
        w1s, w2s, h1s, h2s, w3s = (load(n) for n in ("w1s", "w2s", "h1s", "h2s", "w3s"))
        Wkeys, Wdq, Wqr1, Wqr2 = (load(n) for n in ("Wkeys", "Wdq", "Wqr1", "Wqr2"))
        Wiq, Wik, iw = (load(n) for n in ("Wiq", "Wik", "iw"))
        lWqT, lWkvT, lWoT, lbq, lbkv, lbo = (load(n) for n in ("lWqT", "lWkvT", "lWoT", "lbq", "lbkv", "lbo"))
        gate_w, up_w, down_w = (sb(n, [P, HID2]) for n in ("gate_w", "up_w", "down_w"))

        ARENA = 33 * 1024
        arena = sb("arena", [P, ARENA])
        at = [0]

        def part(*shape, parts=P):
            n = int(np.prod(shape))
            assert at[0] + n <= ARENA, (at[0], n)
            v = arena[0:parts, at[0]:at[0] + n]
            at[0] += n
            if len(shape) == 2:
                v = v.rearrange("p (a b) -> p a b", a=shape[0])
            return v

        sq, sd = part(2, C), part(2, C)
        LAYER = at[0]
        gWq, gWk = part(GH * GDK), part(GH * GDK)
        xs_t, r_sb = part(P), part(P, parts=16)
        zb, ab, lg, Gc = (part(GH, P) for _ in range(4))
        eG, emG, qg, kI, kIT, AT = (part(GH, P) for _ in range(6))
        vt, S, S_in = part(P), part(P), part(P)
        eg, egr = part(P), part(P)
        oT, gate = part(T), part(T)
        o_sq, o_sd = part(C), part(C)
        at[0] = LAYER
        fa, fb = part(NM, C), part(NM, C)
        at[0] = LAYER
        a_exp, a_dt, a_neg, a_dec, carry = (part(1, parts=64) for _ in range(5))
        keep, states = part(C, parts=64), part(T, parts=64)
        at[0] = LAYER
        KL, ki = part(T, parts=ROW), part(T)
        qi = part(2, T)
        Muv = part(NH, P, parts=DC)
        TOPK = at[0]
        WuqT, WukT = part(NH, DCQ, parts=DH), part(NH, DC, parts=DH)
        WuvT, Wout = part(NH, DC, parts=DH), part(NH, P, parts=DH)
        Mq = part(NH * DC, parts=DCQ)
        key_rope = part(C, parts=2 * DR)
        rope_tab = part(4, C)
        cq, raw, rows = part(C, parts=DCQ), part(C, parts=ROW), part(4, ROW)
        k_abs = part(C, parts=2 * DR)
        q_abs, mu = part(2, C), part(2, C)
        rot = part(4, C)
        rot_t = part(2, C)
        qt_sb = part(2, C)
        at[0] = TOPK
        I_s = part(1, T)
        relu = part(4, C)
        top8 = part(JG)
        idx_f = part(JG)
        G = [part(P // 4, ROW) for _ in range(2)]
        QL_in, QG_in = part(NH, P, parts=ROW), part(NH, P, parts=ROW)
        QL, QG = part(NG, P, parts=ROW), part(NG, P, parts=ROW)
        Vloc = [part(NG, DC, parts=WIN) for _ in range(2)]
        GR = [part(4, ROW) for _ in range(2)]
        GT = [part(C, parts=ROW) for _ in range(2)]
        Sm = [part(KEYS) for _ in range(2)]
        Pr = [part(KEYS) for _ in range(2)]
        PTg, PTl = part(C), part(P, parts=WIN)
        mx, nb, ssum, rsum = (part(2) for _ in range(4))
        O_sb = part(DC)
        OT = [part(NH, P, parts=DC) for _ in range(2)]
        at[0] = LAYER
        decay_row = part(T)
        qf = part(T)
        xs_c = part(C)
        lk4, lv4 = part(4, P), part(4, P + 1)
        KV, KVm, Den = part(P + 1), part(P), part(P)
        lq = part(C)
        den, rden, lo = part(C), part(C), part(C)
        at[0] = LAYER
        ia = part(NM2, C)
        gate_i, up_i, down_i = (sb(n, [P, HID2], I32) for n in ("gate_i", "up_i", "down_i"))
        idx_u = sb("idx_u", [P, 2, JG], U32)
        idx_T = [sb(f"idx_T{b}", [P, P // 4], U32) for b in range(2)]

        key_table = dram("key_table", (T, ROW))
        q_rot = {n: dram("q_" + n, (2, P, T)) for n in ("l", "g")}
        q_lat = dram("q_lat", (NH * DC, T))

        (s_tab, s_gla, s_ssm, s_ffn, s_tk, s_lin, s_int) = (
            sem("loaded_" + n) for n in ("tables", "gla", "ssm", "ffn", "topk", "lin", "int"))
        x_loaded, x_ready = sem("x_loaded"), sem("x_ready")
        ln_centered, ln_squared, ln_var, ln_sd, ln_applied = (
            sem("ln_" + n) for n in ("centered", "squared", "var", "sd", "applied"))
        dve_step, act_step, pool_step, pe_step = sem("dve_step"), sem("act_step"), sem("pool_step"), sem("pe_step")

        LOADS = {
            s_tab: ["ident", "center", "mean_all", "cols"],
            s_gla: ["gWv", "gWg", "gWo", "Wgk1", "Wgk2", "bgk2", "gnw", "mean_head", "gla_mask", "scan_keep"],
            s_ffn: ["w1", "w2", "h1", "h2", "w3", "w1s", "w2s", "h1s", "h2s", "w3s"],
            s_ssm: ["lam", "log_dt", "sBT", "sCT", "sD"],
            s_tk: ["Wkeys", "Wdq", "Wqr1", "Wqr2", "Wiq", "Wik", "iw", "rank_rope", "score_mask",
                   "score_mask_first", "index_mask", "index_mask_first"],
            s_lin: ["lWqT", "lWkvT", "lWoT", "lbq", "lbkv", "lbo", "same_head", "decay_col", "ones_row"],
        }
        assert {n for v in LOADS.values() for n in v} == set(LOAD)
        N_TAB, N_GLA, N_FFN, N_SSM, N_TK, N_LIN = (16 * len(v) for v in LOADS.values())

        (g_xs, g_r, g_rs, g_zqk, g_vg, g_lnz, g_G, g_exp, g_eg, g_qk, g_kT, g_kTs, g_A, g_AT, g_vts, g_o, g_dS,
         g_S, g_out, g_osq, g_oms, g_osd, g_on, g_y) = (
            sem("gla_" + n) for n in (
                "tile_staged", "lowrank", "lowrank_copied", "projected", "vg_projected", "log_gate", "cumulated",
                "decays", "gate_exp", "scaled", "k_turned", "k_turned_copied", "scores", "scores_masked",
                "v_copied", "read_out", "state_add", "state_ready", "tile_done", "squared", "mean_sq", "rms",
                "normed", "projected_out"))
        g_zb = sem("gla_gate_biased")
        f_up, f_silu, f_gated, f_h1, f_g1, f_h2, f_g2, f_down = (
            sem("ffn_" + n) for n in ("up", "silu", "gated", "hidden1", "gelu1", "hidden2", "gelu2", "down"))
        ss_a, ss_u, ss_x, ss_y = (sem("ssm_" + n) for n in ("decay_ready", "inputs", "states", "outputs"))
        (t_w, t_wm, t_wc, t_wdone, t_cq, t_cqs, t_raw, t_kln, t_rawd, t_kl, t_rows, t_rowss, t_iq, t_iqs, t_qp,
         t_qln, t_rot, t_qlat, t_qlats, t_tab) = (
            sem("topk_" + n) for n in (
                "weights", "merged", "merged_copied", "setup_done", "cq", "cq_copied", "raw_keys", "key_log",
                "keys_ready", "local_keys", "key_rows", "key_rows_copied", "index_proj", "index_copied",
                "query_proj", "query_log", "rotated", "q_latent", "q_latent_copied", "rope_tables"))
        t_store_k, t_store_q = sem("topk_keys_stored"), sem("topk_queries_stored")
        (i_s, i_relu, i_used, i_done, i_perm, i_idx) = (
            sem("index_" + n) for n in ("scores", "relu", "relu_used", "picked", "permuted", "ready"))
        gathered = [sem(f"gathered{b}") for b in range(2)]
        q_loaded, a_q = sem("queries_loaded"), sem("queries_regrouped")
        v_loaded = [sem(f"local_values_loaded{b}") for b in range(2)]
        (a_rot, a_gt, a_gts, a_s, a_max, a_exp_s, a_pt, a_pts, a_ptl, a_pv, a_o, a_ot, a_otc, a_y, a_x) = (
            sem("attn_" + n) for n in (
                "rows_rotated", "rows_turned", "rows_turned_copied", "scores", "max", "probs", "probs_turned",
                "probs_copied", "local_probs_copied", "values", "normed", "out_turned", "out_copied", "projected",
                "added"))
        (l_q, l_qr, l_qf, l_xs, l_kv, l_kvs, l_KV, l_KVa, l_W, l_nd, l_o, l_y, l_in) = (
            sem("lin_" + n) for n in (
                "q", "q_relu", "q_features", "chunk_staged", "kv", "kv_features", "outer", "outer_added",
                "weights_ready", "num_den", "normed", "projected", "decay_loaded"))
        n_w, n_up, n_silu, n_gated, n_down = (
            sem("int_" + n) for n in ("weights_ready", "up", "silu", "gated", "down"))
        stored = sem("stored")

        L_GLA, L_FFN0, L_SSM, L_FFN1, L_TOPK, L_INT0, L_LIN, L_INT1 = range(8)

        def chunk(a, c):
            return a[:, bass.ds(c * C, C)]

        block = ctx.enter_context(nc.Block())

        @block.sync
        def _(sp):
            sp.dma_start(x[:, :], d["xT"]).then_inc(x_loaded, 16)
            for s, names in LOADS.items():
                for n in names:
                    sp.dma_start(LOAD[n][:], d[n]).then_inc(s, 16)
                if s is s_gla:
                    sp.dma_start(gWq, d["gWq"]).then_inc(s, 16)
                    sp.dma_start(gWk, d["gWk"]).then_inc(s, 16)
            for n, dst in (("gate_i", gate_i), ("up_i", up_i), ("down_i", down_i)):
                sp.dma_start(dst[:], d[n]).then_inc(s_int, 16)

            sp.wait_ge(x_ready, 4 * L_TOPK + 4)
            for n, dst in (("WuqT", WuqT), ("WukT", WukT), ("WuvT", WuvT), ("Wout", Wout)):
                sp.dma_start(dst, d[n]).then_inc(t_w, 16)
            with sp.Fori(0, NCH) as c:
                sp.wait_ge(t_rot, c + 1)
                for k, n in enumerate(("cos_ql", "sin_ql", "cos_qg", "sin_qg")):
                    sp.dma_start(rope_tab[:, k, :], chunk(d[n], c)).then_inc(t_tab, 16)
                sp.dma_start(key_rope, chunk(d["key_rope"], c)).then_inc(t_tab, 16)
                sp.wait_ge(t_rowss, c + 1)
                sp.dma_start(key_table[bass.ds(c * C, C), :].rearrange("(b p) r -> p b r", p=P), rows)\
                    .then_inc(t_store_k, 16)
                sp.wait_ge(t_qlats, 2 * c + 2)
                for k in range(2):
                    sp.dma_start(chunk(q_lat[k * P:k * P + P, :], c), qt_sb[:, k, :]).then_inc(t_store_q, 16)
                sp.wait_ge(t_rot, c + 2)
                for k, n in enumerate("llgg"):
                    sp.dma_start(chunk(q_rot[n][k % 2], c), rot[:, k, :]).then_inc(t_store_q, 16)
            sp.wait_ge(t_store_q, STORES_Q * (NCH + 1))
            sp.wait_ge(t_store_k, STORES_K * (NCH + 1))
            sp.wait_ge(t_rot, NCH + 1)
            for i in range(NT):
                b = i % 2
                if i >= 1:
                    sp.wait_ge(a_q, i)
                half = DR // 2
                for dst, n in ((QL_in, "l"), (QG_in, "g")):
                    for r in range(4):
                        src = q_rot[n][r % 2][:, i * P:(i + 1) * P].rearrange("(h f) t -> f h t", f=half)
                        sp.dma_start(dst[r * half:(r + 1) * half], src).then_inc(q_loaded, 16)
                    src = q_lat[:, i * P:(i + 1) * P].rearrange("(h c) t -> c h t", c=DC)
                    sp.dma_start(dst[2 * DR:ROW], src).then_inc(q_loaded, 16)
                if i >= 2:
                    sp.wait_ge(a_pv, NG * (i - 1))
                for g in range(NG):
                    s0 = max(i * P + g * GQ - LW, 0)
                    sp.dma_start(Vloc[b][:, g, :], key_table[s0:s0 + WIN, 2 * DR:ROW]).then_inc(v_loaded[b], 16)

            sp.wait_ge(x_ready, 4 * L_LIN + 4)
            sp.dma_start(decay_row, d["decay_row"]).then_inc(l_in, 16)
            with sp.Fori(0, NCH) as c:
                sp.wait_ge(x_ready, 4 * L_INT1 + 5 + c)
                sp.dma_start(chunk(out, c), chunk(x, c)).then_inc(stored, 16)
            sp.wait_ge(stored, 16 * NCH)

        @block.gpsimd
        def _(pool):
            pool.wait_ge(t_store_k, STORES_K * (NCH + 1))
            pool.wait_ge(t_rot, NCH + 1)
            for i in range(NT):
                b = i % 2
                pool.wait_ge(i_idx, i + 1)
                if i >= 2:
                    pool.wait_ge(a_pv, NG * (i - 1))
                for q in range(P // 4):
                    pool.indirect_dma_start(
                        out=G[b][:, q, :], out_offset=None, in_=key_table,
                        in_offset=bass.IndirectOffsetOnAxis(ap=idx_T[b][:, q:q + 1], axis=0),
                    ).then_inc(gathered[b], 16)

        @block.tensor
        def _(pe):
            def mm(out_, lhsT, rhs, start=True, stop=True, **kw):
                return pe.matmul(out_, lhsT, rhs, start=start, stop=stop, **kw)

            def layer_norm(k):
                with pe.Fori(0, 2) as r:
                    for u in range(2):
                        n = 4 * k + r * 2 + u
                        pe.wait_ge(x_ready, n + 1)
                        pe.wait_ge(ln_applied, LN0 + n - 1)
                        mm(bank[4 + u], center[:], chunk(x, r * 2 + u)).then_inc(ln_centered, 1)
                    for u in range(2):
                        pe.wait_ge(ln_squared, 4 * k + r * 2 + u + 1)
                        mm(bank[6 + u], mean_all[:], sq[:, u, :]).then_inc(ln_var, 1)

            def gla():
                pe.wait_ge(s_gla, N_GLA + 32)
                pe.wait_ge(ln_applied, LN0 + 4 * L_GLA + 4)
                with pe.Fori(0, NT) as i:
                    pe.wait_ge(g_xs, i + 1)
                    pe.wait_ge(g_out, i + 1)
                    mm(bank[0][0:16, 0:P], Wgk1[:], xs_t).then_inc(g_r, 1)
                    for h in range(GH):
                        mm(bank[2][:, h * P:h * P + P], gWq[:, h * GDK:(h + 1) * GDK], xs_t)
                        mm(bank[3][:, h * P:h * P + P], gWk[:, h * GDK:(h + 1) * GDK], xs_t)
                    mm(bank[7][:, 256:384], gWg[:], xs_t)
                    mm(bank[7][:, 384:512], xs_t, gWv[:]).then_inc(g_vg, 1)
                    pe.wait_ge(g_rs, i + 1)
                    for h in range(GH):
                        last = mm(bank[1][:, h * P:h * P + P], Wgk2[:, h * GDK:(h + 1) * GDK], r_sb)
                    last.then_inc(g_zqk, 1)
                    pe.wait_ge(g_qk, i + 1)
                    for h in range(GH):
                        last = mm(bank[5][:, h * P:h * P + P], kI[:, h, :], qg[:, h, :])
                    last.then_inc(g_A, 1)
                    for h in range(GH):
                        last = pe.transpose(bank[4][:, h * P:h * P + P], kI[:, h, :], ident[:])
                    last.then_inc(g_kT, 1)
                    pe.wait_ge(g_AT, i + 1)
                    pe.wait_ge(g_vts, i + 1)
                    for h in range(GH):
                        mm(bank[6][GDV * h:GDV * h + GDV, 0:P], vt[:, GDV * h:GDV * h + GDV], AT[:, h, :],
                           stop=False, tile_position=(0, GDV * h), skip_group_check=True)
                    for half in range(2):
                        lo_, hi_ = half * GCHUNK, (half + 1) * GCHUNK
                        pe.wait_ge(g_S, i * 2 + half + 1)
                        for h in range(GH):
                            last = mm(bank[6][GDV * h:GDV * h + GDV, lo_:hi_], S[:, GDV * h:GDV * h + GDV],
                                      qg[:, h, lo_:hi_], start=False, stop=True, tile_position=(0, GDV * h),
                                      skip_group_check=True)
                        if half == 1:
                            last.then_inc(g_o, 1)
                        if half == 0:
                            pe.wait_ge(g_kTs, i + 1)
                        for h in range(GH):
                            last = mm(bank[7][:, half * P + GDV * h:half * P + GDV * h + GDV],
                                      kIT[lo_:hi_, h, :], vt[lo_:hi_, GDV * h:GDV * h + GDV])
                        last.then_inc(g_dS, 1)
                with pe.Fori(0, NCH) as c:
                    pe.wait_ge(g_osq, c + 1)
                    mm(bank[0], mean_head[:], o_sq).then_inc(g_oms, 1)
                    pe.wait_ge(g_on, c + 1)
                    mm(bank[1], gWo[:], chunk(oT, c)).then_inc(g_y, 1)

            def ffn(layer, k):
                pe.wait_ge(s_ffn, N_FFN)
                with pe.Fori(0, NCH) as c:
                    n = 4 * k + c
                    pe.wait_ge(ln_applied, LN0 + 4 * layer + 1 + c)
                    pe.wait_ge(x_ready, 4 * layer + 4 + c)
                    for m in range(NM):
                        if m >= 2:
                            pe.wait_ge(f_gated, 4 * n + m - 1)
                        mm(bank[2 * (m % 2)], w1[:, m * P:m * P + P], chunk(xn, c))
                        mm(bank[2 * (m % 2) + 1], w2[:, m * P:m * P + P], chunk(xn, c)).then_inc(f_up, 1)
                    pe.wait_ge(f_gated, 4 * n + NM)
                    for m in range(NM):
                        for kk in range(NM):
                            last = mm(bank[m], h1[:, kk, m * P:m * P + P], fa[:, kk, :], kk == 0, kk == NM - 1)
                        last.then_inc(f_h1, 1)
                    for m in range(NM):
                        pe.wait_ge(f_g1, 4 * n + NM)
                        for kk in range(NM):
                            last = mm(bank[m], h2[:, kk, m * P:m * P + P], fb[:, kk, :], kk == 0, kk == NM - 1)
                        last.then_inc(f_h2, 1)
                    pe.wait_ge(f_g2, 4 * n + NM)
                    for kk in range(NM):
                        last = mm(bank[0], w3[:, kk, :], fa[:, kk, :], kk == 0, kk == NM - 1)
                    last.then_inc(f_down, 1)

            def ssm():
                pe.wait_ge(s_ssm, N_SSM)
                with pe.Fori(0, NCH) as c:
                    pe.wait_ge(ln_applied, LN0 + 4 * L_SSM + 1 + c)
                    pe.wait_ge(x_ready, 4 * L_SSM + 4 + c)
                    mm(bank[0][0:64, :], sBT[:], chunk(xn, c)).then_inc(ss_u, 1)
                    pe.wait_ge(ss_x, c + 1)
                    mm(bank[1], sCT[:], chunk(states, c)).then_inc(ss_y, 1)

            def topk_setup():
                pe.wait_ge(s_tk, N_TK)
                pe.wait_ge(t_w, 64)
                pe.wait_ge(x_ready, 4 * L_TOPK + 4)
                for h in range(NH):
                    last = mm(bank[0][0:DCQ, h * DC:(h + 1) * DC], WuqT[:, h, :], WukT[:, h, :])
                for h in range(NH):
                    last = mm(bank[1 + h // 4][0:DC, (h % 4) * P:(h % 4 + 1) * P], WuvT[:, h, :], Wout[:, h, :])
                last.then_inc(t_wm, 1)
                pe.wait_ge(t_wc, 3)
                pe.wait_ge(ln_applied, LN0 + 4 * L_TOPK + 4)
                with pe.Fori(0, NCH) as c:
                    pe.wait_ge(t_rot, c + 1)
                    mm(bank[0][0:DCQ, :], Wdq[:], chunk(xn, c)).then_inc(t_cq, 1)
                    mm(bank[1][0:ROW, :], Wkeys[:], chunk(xn, c)).then_inc(t_raw, 1)
                    mm(bank[2], Wiq[:, 0:P], chunk(xn, c))
                    mm(bank[3], Wiq[:, P:2 * P], chunk(xn, c))
                    mm(bank[4], Wik[:], chunk(xn, c)).then_inc(t_iq, 1)
                    pe.wait_ge(t_cqs, c + 1)
                    mm(bank[5], Wqr1[:], cq)
                    mm(bank[6], Wqr2[:], cq).then_inc(t_qp, 1)
                    mm(bank[7], Mq[:, 0:P], cq).then_inc(t_qlat, 1)
                    mm(bank[0], Mq[:, P:2 * P], cq).then_inc(t_qlat, 1)
                    pe.wait_ge(t_rawd, c + 1)
                    for j in range(4):
                        last = pe.transpose(bank[1][:, j * ROW:(j + 1) * ROW], raw[:, j * P:(j + 1) * P],
                                            ident[0:ROW, 0:ROW])
                    last.then_inc(t_rows, 1)

            units = [0]

            def index_scores(i):
                W = KTOP if i == 0 else i * P + P - LW
                for s0 in range(0, W, C):
                    w = min(C, W - s0)
                    for h in range(NIH):
                        if units[0] >= 1:
                            pe.wait_ge(i_relu, units[0])
                        if i >= 1 and s0 == 0 and h == 0:
                            pe.wait_ge(i_idx, i)
                        if i >= 2 and s0 == 0 and h == 0:
                            pe.wait_ge(a_x, i - 1)
                        lo_ = 64 * (h % 2)
                        mm(bank[7][:, 0:w], qi[lo_:lo_ + 64, h // 2, i * P:(i + 1) * P],
                           ki[lo_:lo_ + 64, s0:s0 + w]).then_inc(i_s, 1)
                        units[0] += 1

            def index_turn(i):
                pe.wait_ge(i_done, i + 1)
                pe.wait_ge(i_relu, units[0])
                for tq in range(4):
                    last = mm(bank[7][JG * tq:JG * tq + JG, 0:P // 4], idx_f, ident[:, tq:P:4],
                              tile_position=(0, JG * tq), skip_group_check=True)
                last.then_inc(i_perm, 1)

            def rows_turn(n):
                i, g = n // NG, n % NG
                pe.wait_ge(a_rot, n + 1)
                if n >= 1:
                    pe.wait_ge(a_gts, n)
                for j in range(4):
                    last = pe.transpose(bank[4][0:ROW, j * P:(j + 1) * P], GR[n % 2][:, j, :], ident[:])
                last.then_inc(a_gt, 1)

            def scores(n):
                i, g = n // NG, n % NG
                b = i % 2
                pe.wait_ge(a_gts, n + 1)
                if g == 0:
                    pe.wait_ge(a_q, i + 1)
                if n >= 2:
                    pe.wait_ge(a_max, n - 1)
                s0 = max(i * P + g * GQ - LW, 0)
                sp_ = bank2[n % 2]
                mm(sp_[:, 0:C], QG[:, g, :], GT[n % 2])
                mm(sp_[:, C:KEYS], QL[:, g, :], KL[:, s0:s0 + WIN]).then_inc(a_s, 1)

            def probs_turn(n):
                pe.wait_ge(a_exp_s, n + 1)
                if n >= 1:
                    pe.wait_ge(a_pts, n)
                    pe.wait_ge(a_o, n)
                for j in range(4):
                    pe.transpose(bank[5][:, j * P:(j + 1) * P], Pr[n % 2][:, j * P:(j + 1) * P], ident[:])
                pe.transpose(bank[6][0:WIN, 0:P], Pr[n % 2][:, C:KEYS], ident[:]).then_inc(a_pt, 1)

            def values(n):
                i, g = n // NG, n % NG
                b = i % 2
                if g == 0:
                    pe.wait_ge(v_loaded[b], 16 * NG * (i // 2 + 1))
                pe.wait_ge(a_pts, n + 1)
                pe.wait_ge(a_ptl, n + 1)
                for j in range(4):
                    mm(bank[6][:, 128:128 + DC], PTg[:, j * P:(j + 1) * P], G[b][:, g * 4 + j, 2 * DR:ROW],
                       j == 0, False, skip_group_check=True)
                mm(bank[6][:, 128:128 + DC], PTl, Vloc[b][:, g, :], False, True,
                   skip_group_check=True).then_inc(a_pv, 1)

            def out_turn(n):
                pe.wait_ge(a_o, n + 1)
                if n >= 1:
                    pe.wait_ge(a_otc, n)
                if n % NG == 0:
                    pe.wait_ge(i_idx, min(n // NG + 2, NT))
                pe.transpose(bank[7][0:DC, 256:384], O_sb, ident[:]).then_inc(a_ot, 1)

            def out_project(i):
                pe.wait_ge(a_otc, NG * (i + 1))
                if i >= 1:
                    pe.wait_ge(a_x, i)
                for h in range(NH):
                    last = mm(bank[7][:, 384:512], Muv[:, h, :], OT[i % 2][:, h, :], h == 0, h == NH - 1,
                              skip_group_check=True)
                last.then_inc(a_y, 1)

            def topk():
                pe.wait_ge(t_rot, NCH + 1)
                for i in range(NT + 1):
                    if i < NT:
                        index_scores(i)
                        index_turn(i)
                    if i >= 1:
                        n0 = NG * (i - 1)
                        rows_turn(n0)
                        for k in range(NG + 2):
                            if k < NG:
                                scores(n0 + k)
                            if k + 1 < NG:
                                rows_turn(n0 + k + 1)
                            if 1 <= k <= NG:
                                probs_turn(n0 + k - 1)
                                values(n0 + k - 1)
                            if k >= 2:
                                out_turn(n0 + k - 2)
                        out_project(i - 1)
                pe.wait_ge(a_x, NT)

            def int_ffn(layer, k):
                pe.wait_ge(n_w, 3)
                with pe.Fori(0, NCH) as c:
                    n = 4 * k + c
                    pe.wait_ge(ln_applied, LN0 + 4 * layer + 1 + c)
                    pe.wait_ge(x_ready, 4 * layer + 4 + c)
                    for m in range(NM2):
                        if m >= 2:
                            pe.wait_ge(n_gated, NM2 * n + m - 1)
                        mm(bank[2 * (m % 2)], gate_w[:, m * P:m * P + P], chunk(xn, c))
                        mm(bank[2 * (m % 2) + 1], up_w[:, m * P:m * P + P], chunk(xn, c)).then_inc(n_up, 1)
                    pe.wait_ge(n_gated, NM2 * n + NM2)
                    for m in range(NM2):
                        last = mm(bank[0], down_w[:, m * P:m * P + P], ia[:, m, :], m == 0, m == NM2 - 1)
                    last.then_inc(n_down, 1)

            def linear_attention():
                pe.wait_ge(s_lin, N_LIN)
                pe.wait_ge(ln_applied, LN0 + 4 * L_LIN + 4)
                with pe.Fori(0, NCH) as c:
                    pe.wait_ge(l_KVa, c + 1)
                    mm(bank[0], lWqT[:], chunk(xn, c)).then_inc(l_q, 1)
                    pe.wait_ge(l_xs, c + 1)
                    for j in range(4):
                        if j >= 2:
                            pe.wait_ge(l_kvs, 4 * c + j - 1)
                        mm(bank[1 + j % 2][:, 0:2 * P], xs_c[:, j * P:(j + 1) * P], lWkvT[:], True, False)
                        mm(bank[1 + j % 2][:, 0:2 * P], ones_row[:], lbkv[:], False, True).then_inc(l_kv, 1)
                    pe.wait_ge(l_kvs, 4 * c + 4)
                    for j in range(4):
                        last = mm(bank[3][:, 0:P + 1], lk4[:, j, :], lv4[:, j, :], j == 0, j == 3)
                    last.then_inc(l_KV, 1)
                pe.wait_ge(l_W, 2)
                with pe.Fori(0, NCH) as c:
                    pe.wait_ge(x_ready, 4 * L_LIN + 4 + c)
                    mm(bank[0], KVm, chunk(qf, c))
                    mm(bank[1], Den, chunk(qf, c)).then_inc(l_nd, 1)
                    pe.wait_ge(l_o, c + 1)
                    mm(bank[2], lWoT[:], lo).then_inc(l_y, 1)

            pe.wait_ge(s_tab, N_TAB)
            layer_norm(L_GLA)
            gla()
            layer_norm(L_FFN0)
            ffn(L_FFN0, 0)
            layer_norm(L_SSM)
            ssm()
            layer_norm(L_FFN1)
            ffn(L_FFN1, 1)
            layer_norm(L_TOPK)
            topk_setup()
            topk()
            layer_norm(L_INT0)
            int_ffn(L_INT0, 0)
            layer_norm(L_LIN)
            linear_attention()
            layer_norm(L_INT1)
            int_ffn(L_INT1, 1)

        @block.scalar
        def _(act):
            steps = Steps(act, act_step)
            fn = nc.scalar.activation

            def layer_norm(k):
                with act.Fori(0, 2) as r:
                    for u in range(2):
                        act.wait_ge(ln_centered, 4 * k + r * 2 + u + 1)
                        fn(sq[:, u, :], bank[4 + u], ACT.Square).then_inc(ln_squared, 1)
                    for u in range(2):
                        act.wait_ge(ln_var, 4 * k + r * 2 + u + 1)
                        fn(sd[:, u, :], bank[6 + u], ACT.Sqrt, bias=eps_col).then_inc(ln_sd, 1)

            def softplus_neg_abs(dst, done, parts=P):
                steps.did(fn(dst, dst, ACT.Exp, scale=-1.0))
                fn(dst, dst, ACT.Ln, bias=one_col[0:parts]).then_inc(done, 1)

            def gla():
                with act.Fori(0, NT) as i:
                    steps.enter(i, 2)
                    act.wait_ge(g_r, i + 1)
                    fn(r_sb, bank[0][0:16, 0:P], ACT.Copy).then_inc(g_rs, 1)
                    act.wait_ge(g_zb, i + 1)
                    steps.did(fn(ab, zb, ACT.Abs))
                    softplus_neg_abs(ab, g_lnz)
                    act.wait_ge(g_vts, i + 1)
                    fn(eg, bank[7][:, 256:384], ACT.Exp, scale=-1.0).then_inc(g_eg, 1)
                    act.wait_ge(g_G, i + 1)
                    fn(eG, Gc, ACT.Exp, scale=1.0 / 16)
                    fn(emG, Gc, ACT.Exp, scale=-1.0 / 16).then_inc(g_exp, 1)
                    act.wait_ge(g_kT, i + 1)
                    fn(kIT, bank[4].rearrange("p (h d) -> p h d", h=GH), ACT.Copy).then_inc(g_kTs, 1)
                steps.leave(2, NT)
                act.wait_ge(g_out, NT + 1)
                with act.Fori(0, NCH) as c:
                    fn(o_sq, chunk(oT, c), ACT.Square).then_inc(g_osq, 1)
                    act.wait_ge(g_oms, c + 1)
                    fn(o_sd, bank[0], ACT.Sqrt, bias=eps_col).then_inc(g_osd, 1)

            def ffn(layer, k):
                act.wait_ge(s_ffn, N_FFN)
                act.wait_ge(x_ready, 4 * layer + 4)
                with act.Fori(0, NCH) as c:
                    n = 4 * k + c
                    for m in range(NM):
                        act.wait_ge(f_up, 4 * n + m + 1)
                        fn(fb[:, m, :], bank[2 * (m % 2)], ACT.Silu, scale=w1s[:, m:m + 1]).then_inc(f_silu, 1)
                    for m in range(NM):
                        act.wait_ge(f_h1, 4 * n + m + 1)
                        fn(fb[:, m, :], bank[m], ACT.Gelu, scale=h1s[:, m:m + 1]).then_inc(f_g1, 1)
                    for m in range(NM):
                        act.wait_ge(f_h2, 4 * n + m + 1)
                        fn(fa[:, m, :], bank[m], ACT.Gelu, scale=h2s[:, m:m + 1]).then_inc(f_g2, 1)

            def ssm():
                act.wait_ge(s_ssm, N_SSM)
                act.wait_ge(x_ready, 4 * L_SSM + 4)
                fn(a_exp, lam[:], ACT.Exp)
                fn(a_dt, log_dt[:], ACT.Exp).then_inc(ss_a, 1)
                act.wait_ge(ss_a, 2)
                fn(a_dec, a_neg, ACT.Exp, scale=-1.0).then_inc(ss_a, 1)

            def topk_setup():
                act.wait_ge(t_wm, 1)
                fn(Mq, bank[0][0:DCQ, 0:NH * DC], ACT.Copy).then_inc(t_wc, 1)
                for a in range(2):
                    fn(Muv[:, 4 * a:4 * a + 4, :], bank[1 + a][0:DC, :].rearrange("c (h d) -> c h d", h=4),
                       ACT.Copy).then_inc(t_wc, 1)
                with act.Fori(0, NCH) as c:
                    steps.enter(c, 4)
                    act.wait_ge(t_cq, c + 1)
                    fn(cq, bank[0][0:DCQ, :], ACT.Copy).then_inc(t_cqs, 1)
                    act.wait_ge(t_raw, c + 1)
                    steps.did(fn(k_abs, bank[1][0:2 * DR, :], ACT.Abs))
                    softplus_neg_abs(k_abs, t_kln, 2 * DR)
                    act.wait_ge(t_iq, c + 1)
                    fn(chunk(qi[:, 0, :], c), bank[2], ACT.Copy)
                    fn(chunk(qi[:, 1, :], c), bank[3], ACT.Copy)
                    fn(chunk(ki, c), bank[4], ACT.Copy).then_inc(t_iqs, 1)
                    act.wait_ge(t_qp, c + 1)
                    fn(q_abs[:, 0, :], bank[5], ACT.Abs)
                    steps.did(fn(q_abs[:, 1, :], bank[6], ACT.Abs))
                    softplus_neg_abs(q_abs, t_qln)
                    act.wait_ge(t_store_q, STORES_Q * (c + 1))
                    act.wait_ge(t_qlat, 2 * c + 1)
                    fn(qt_sb[:, 0, :], bank[7], ACT.Copy).then_inc(t_qlats, 1)
                    act.wait_ge(t_qlat, 2 * c + 2)
                    fn(qt_sb[:, 1, :], bank[0], ACT.Copy).then_inc(t_qlats, 1)
                    act.wait_ge(t_store_k, STORES_K * (c + 1))
                    act.wait_ge(t_rows, c + 1)
                    fn(rows, bank[1][:, 0:4 * ROW].rearrange("p (b r) -> p b r", b=4), ACT.Copy)\
                        .then_inc(t_rowss, 1)
                steps.leave(4, NCH)

            units = [0]

            def index_relu(i):
                W = KTOP if i == 0 else i * P + P - LW
                for s0 in range(0, W, C):
                    w = min(C, W - s0)
                    for h in range(NIH):
                        u = units[0]
                        act.wait_ge(i_s, u + 1)
                        if u >= 4:
                            act.wait_ge(i_used, u - 3)
                        fn(relu[:, u % 4, 0:w], bank[7][:, 0:w], ACT.Relu).then_inc(i_relu, 1)
                        units[0] += 1

            def queries_regroup(i):
                act.wait_ge(q_loaded, 160 * (i + 1))
                if i >= 1:
                    act.wait_ge(a_s, NG * i)
                for dst, src in ((QL, QL_in), (QG, QG_in)):
                    last = fn(dst.rearrange("r g (h t) -> r g h t", h=NH),
                              src.rearrange("r h (g t) -> r g h t", g=NG), ACT.Copy)
                last.then_inc(a_q, 1)

            def rows_copy(n):
                act.wait_ge(a_gt, n + 1)
                if n >= 2:
                    act.wait_ge(a_s, n - 1)
                fn(GT[n % 2], bank[4][0:ROW, :], ACT.Copy).then_inc(a_gts, 1)

            def probs(n):
                act.wait_ge(a_max, n + 1)
                if n >= 2:
                    act.wait_ge(a_pt, n - 1)
                    act.wait_ge(a_o, n - 1)
                fn(Pr[n % 2], Sm[n % 2], ACT.Exp, scale=SCALE, bias=nb[:, n % 2:n % 2 + 1],
                   accum_out=ssum[:, n % 2:n % 2 + 1]).then_inc(a_exp_s, 1)

            def probs_copy(n):
                act.wait_ge(a_pt, n + 1)
                fn(PTg, bank[5], ACT.Copy).then_inc(a_pts, 1)

            def topk():
                act.wait_ge(t_rot, NCH + 1)
                act.wait_ge(t_store_q, STORES_Q * (NCH + 1))
                act.wait_ge(t_store_k, STORES_K * (NCH + 1))
                for i in range(NT + 1):
                    if i < NT:
                        index_relu(i)
                    if i >= 1:
                        n0 = NG * (i - 1)
                        queries_regroup(i - 1)
                        rows_copy(n0)
                        for k in range(NG + 1):
                            if k + 1 < NG:
                                rows_copy(n0 + k + 1)
                            if k >= 1:
                                probs_copy(n0 + k - 1)
                            if k < NG:
                                probs(n0 + k)

            def int_ffn(layer, k):
                act.wait_ge(x_ready, 4 * layer + 4)
                with act.Fori(0, NCH) as c:
                    n = 4 * k + c
                    for m in range(NM2):
                        act.wait_ge(n_up, NM2 * n + m + 1)
                        fn(ia[:, m, :], bank[2 * (m % 2)], ACT.Silu).then_inc(n_silu, 1)

            def linear_attention():
                act.wait_ge(x_ready, 4 * L_LIN + 4)
                with act.Fori(0, NCH) as c:
                    act.wait_ge(l_q, c + 1)
                    fn(lq, bank[0], ACT.Relu, bias=lbq[:]).then_inc(l_qr, 1)

            act.wait_ge(s_tab, N_TAB)
            layer_norm(L_GLA)
            gla()
            layer_norm(L_FFN0)
            ffn(L_FFN0, 0)
            layer_norm(L_SSM)
            ssm()
            layer_norm(L_FFN1)
            ffn(L_FFN1, 1)
            layer_norm(L_TOPK)
            topk_setup()
            topk()
            layer_norm(L_INT0)
            int_ffn(L_INT0, 0)
            layer_norm(L_LIN)
            linear_attention()
            layer_norm(L_INT1)
            int_ffn(L_INT1, 1)

        @block.vector
        def _(dve):
            v = nc.vector
            steps = Steps(dve, dve_step)

            def layer_norm(k):
                with dve.Fori(0, 2) as r:
                    steps.enter(r, 2)
                    for u in range(2):
                        dve.wait_ge(ln_sd, 4 * k + r * 2 + u + 1)
                        steps.did(v.reciprocal(sd[:, u, :], sd[:, u, :]))
                        v.tensor_tensor(chunk(xn, r * 2 + u), bank[4 + u], sd[:, u, :], ALU.mult)\
                            .then_inc(ln_applied, 1)
                steps.leave(2, 2)

            def heads(a, n=GH):
                return a.rearrange("p (h t) -> p h t", h=n)

            def gla():
                dve.wait_ge(s_gla, N_GLA + 32)
                v.memset(S, 0.0).then_inc(g_S, 1)
                with dve.Fori(0, NT) as i:
                    steps.enter(i, 5)
                    dve.wait_ge(ln_applied, LN0 + 4 * L_GLA + 4)
                    dve.wait_ge(g_vg, i + 1)
                    v.tensor_copy(xs_t, xn[:, bass.ds(i * P, P)]).then_inc(g_xs, 1)
                    dve.wait_ge(g_zqk, i + 1)
                    v.tensor_tensor(zb, heads(bank[1]), bgk2[:].unsqueeze(2).to_broadcast([P, GH, P]), ALU.add)\
                        .then_inc(g_zb, 1)
                    dve.wait_ge(g_vg, i + 2)
                    v.tensor_copy(vt, bank[7][:, 384:512]).then_inc(g_vts, 1)
                    dve.wait_ge(g_lnz, i + 1)
                    dve.wait_ge(g_zb, i + 1)
                    steps.did(v.scalar_tensor_tensor(zb, zb, 0.0, ab, ALU.min, ALU.subtract))
                    v.tensor_tensor_scan(Gc.rearrange("p h t -> p (h t)"), scan_keep[:],
                                         zb.rearrange("p h t -> p (h t)"), 0.0, ALU.mult, ALU.add)\
                        .then_inc(g_G, 1)
                    dve.wait_ge(g_exp, i + 1)
                    v.scalar_tensor_tensor(qg, heads(bank[2]), GDK ** -0.5, eG, ALU.mult, ALU.mult)
                    v.tensor_tensor(kI, heads(bank[3]), emG, ALU.mult).then_inc(g_qk, 1)
                    dve.wait_ge(g_eg, i + 1)
                    steps.did(v.tensor_scalar(egr, eg, 1.0, None, ALU.add))
                    steps.did(v.reciprocal(egr, egr))
                    v.tensor_tensor(gate[:, bass.ds(i * P, P)], bank[7][:, 256:384], egr, ALU.mult)
                    dve.wait_ge(g_A, i + 1)
                    v.tensor_tensor(AT, heads(bank[5]), gla_mask[:].unsqueeze(1).to_broadcast([P, GH, P]),
                                    ALU.mult).then_inc(g_AT, 1)
                    for half in range(2):
                        dve.wait_ge(g_dS, 2 * i + half + 1)
                        dve.wait_ge(g_S, 2 * i + half + 1)
                        steps.did(v.tensor_tensor(S_in, S, bank[7][:, half * P:half * P + P], ALU.add))
                        end = (half + 1) * GCHUNK - 1
                        v.tensor_tensor(heads(S), heads(S_in), eG[:, :, end:end + 1].to_broadcast([P, GH, GDV]),
                                        ALU.mult).then_inc(g_S, 1)
                    dve.wait_ge(g_o, i + 1)
                    v.tensor_copy(oT[:, bass.ds(i * P, P)], bank[6][:, 0:P]).then_inc(g_out, 1)
                steps.leave(5, NT)
                with dve.Fori(0, NCH) as c:
                    steps.enter(c, 2)
                    dve.wait_ge(g_osd, c + 1)
                    steps.did(v.reciprocal(o_sd, o_sd))
                    steps.did(v.tensor_tensor(chunk(oT, c), chunk(oT, c), o_sd, ALU.mult))
                    v.scalar_tensor_tensor(chunk(oT, c), chunk(oT, c), gnw[:], chunk(gate, c), ALU.mult, ALU.mult)\
                        .then_inc(g_on, 1)
                    dve.wait_ge(g_y, c + 1)
                    v.tensor_tensor(chunk(x, c), chunk(x, c), bank[1], ALU.add).then_inc(x_ready, 1)
                steps.leave(2, NCH)

            def ffn(layer, k):
                dve.wait_ge(s_ffn, N_FFN)
                with dve.Fori(0, NCH) as c:
                    n = 4 * k + c
                    for m in range(NM):
                        dve.wait_ge(f_silu, 4 * n + m + 1)
                        v.scalar_tensor_tensor(fa[:, m, :], bank[2 * (m % 2) + 1], w2s[:, m:m + 1], fb[:, m, :],
                                               ALU.mult, ALU.mult).then_inc(f_gated, 1)
                    dve.wait_ge(f_down, n + 1)
                    v.scalar_tensor_tensor(chunk(x, c), bank[0], w3s[:], chunk(x, c), ALU.mult, ALU.add)\
                        .then_inc(x_ready, 1)

            def ssm():
                dve.wait_ge(s_ssm, N_SSM)
                dve.wait_ge(ss_a, 1)
                v.tensor_tensor(a_neg, a_exp, a_dt, ALU.mult).then_inc(ss_a, 1)
                steps.did(v.memset(keep, 1.0))
                dve.wait_ge(ss_a, 3)
                steps.did(v.tensor_scalar(keep, keep, a_dec, None, ALU.mult))
                steps.did(v.memset(carry, 0.0))
                steps.leave(3, 1)
                with dve.Fori(0, NCH) as c:
                    steps.enter(c, 2)
                    dve.wait_ge(ss_u, c + 1)
                    v.tensor_tensor_scan(chunk(states, c), keep, bank[0][0:64, :], carry, ALU.mult, ALU.add)\
                        .then_inc(ss_x, 1)
                    dve.wait_ge(ss_x, c + 1)
                    steps.did(v.tensor_copy(carry, states[:, bass.ds(c * C + C - 1, 1)]))
                    dve.wait_ge(ln_applied, LN0 + 4 * L_SSM + 4)
                    steps.did(v.scalar_tensor_tensor(chunk(x, c), chunk(xn, c), sD[:], chunk(x, c),
                                                     ALU.mult, ALU.add))
                    dve.wait_ge(ss_y, c + 1)
                    v.tensor_tensor(chunk(x, c), chunk(x, c), bank[1], ALU.add).then_inc(x_ready, 1)
                steps.leave(2, NCH)

            def topk_setup():
                with dve.Fori(0, NCH) as c:
                    steps.enter(c, 13)
                    dve.wait_ge(t_kln, c + 1)
                    v.scalar_tensor_tensor(raw[0:2 * DR, :], bank[1][0:2 * DR, :], 0.0, k_abs, ALU.max, ALU.add)
                    v.tensor_copy(raw[2 * DR:ROW, :], bank[1][2 * DR:ROW, :]).then_inc(t_rawd, 1)
                    dve.wait_ge(t_rawd, c + 1)
                    dve.wait_ge(t_tab, 80 * (c + 1))
                    v.tensor_tensor(chunk(KL[0:2 * DR, :], c), raw[0:2 * DR, :], key_rope, ALU.mult)
                    v.tensor_copy(chunk(KL[2 * DR:ROW, :], c), raw[2 * DR:ROW, :])
                    dve.wait_ge(t_qln, c + 1)
                    steps.did(v.scalar_tensor_tensor(mu[:, 0, :], bank[5], 0.0, q_abs[:, 0, :], ALU.max, ALU.add))
                    steps.did(v.scalar_tensor_tensor(mu[:, 1, :], bank[6], 0.0, q_abs[:, 1, :], ALU.max, ALU.add))
                    dve.wait_ge(t_store_q, STORES_Q * (c + 1))
                    for k in range(2):
                        cos, sin = rope_tab[:, 2 * k, :], rope_tab[:, 2 * k + 1, :]
                        for b, (f0, f1, op) in enumerate(((cos, sin, ALU.subtract), (sin, cos, ALU.add))):
                            steps.did(v.tensor_tensor(rot_t[:, 0, :], mu[:, 0, :], f0, ALU.mult))
                            steps.did(v.tensor_tensor(rot_t[:, 1, :], mu[:, 1, :], f1, ALU.mult))
                            if k == 1 and b == 1:
                                dve.wait_ge(t_iqs, c + 1)
                                dve.wait_ge(t_qlats, 2 * c + 2)
                                dve.wait_ge(t_rowss, c + 1)
                            last = v.tensor_tensor(rot[:, 2 * k + b, :], rot_t[:, 0, :], rot_t[:, 1, :], op)
                            if k == 1 and b == 1:
                                last.then_inc(t_rot, 1)
                                dve.wait_ge(t_rot, c + 2)
                            else:
                                steps.did(last)
                steps.leave(13, NCH)

            units = [0]

            def pick(i):
                W = KTOP if i == 0 else i * P + P - LW
                sc = I_s[:, 0, 0:W]
                for s0 in range(0, W, C):
                    w = min(C, W - s0)
                    for h in range(NIH):
                        u = units[0]
                        dve.wait_ge(i_relu, u + 1)
                        r_, s_ = relu[:, u % 4, 0:w], sc[:, s0:s0 + w]
                        if h == 0:
                            ins = v.tensor_scalar(s_, r_, iw[:, 0:1], None, ALU.mult)
                        else:
                            dve.wait_ge(i_used, u)
                            ins = v.scalar_tensor_tensor(s_, r_, iw[:, h:h + 1], s_, ALU.mult, ALU.add)
                        ins.then_inc(i_used, 1)
                        units[0] += 1
                dve.wait_ge(i_used, units[0])
                if i == 0:
                    steps.did(v.tensor_tensor(sc, sc, index_mask_first[:], ALU.add))
                else:
                    steps.did(v.tensor_tensor(sc[:, W - P:W], sc[:, W - P:W], index_mask[:], ALU.add))
                for r in range(JG // 8):
                    best = top8[:, 8 * r:8 * r + 8]
                    steps.did(v.max(best, sc))
                    steps.did(v.max_index(idx_u[:, i % 2, 8 * r:8 * r + 8], best, sc))
                    if r < JG // 8 - 1:
                        steps.did(v.match_replace(sc, best, sc, TAKEN))
                if i >= 1:
                    dve.wait_ge(i_perm, i)
                v.tensor_copy(idx_f, idx_u[:, i % 2, :]).then_inc(i_done, 1)
                dve.wait_ge(i_perm, i + 1)
                if i >= 2:
                    dve.wait_ge(gathered[i % 2], 16 * (P // 4) * (i // 2))
                v.tensor_copy(idx_T[i % 2][:], bank[7][:, 0:P // 4]).then_inc(i_idx, 1)

            def rows_rotate(n):
                i, g = n // NG, n % NG
                if g == 0:
                    dve.wait_ge(gathered[i % 2], 16 * (P // 4) * (i // 2 + 1))
                if n >= 2:
                    dve.wait_ge(a_gt, n - 1)
                v.tensor_tensor(GR[n % 2], G[i % 2][:, 4 * g:4 * g + 4, :],
                                rank_rope[:].unsqueeze(1).to_broadcast([P, 4, ROW]), ALU.mult).then_inc(a_rot, 1)

            def row_max(n):
                i, g = n // NG, n % NG
                b = n % 2
                dve.wait_ge(a_s, n + 1)
                if n >= 2:
                    dve.wait_ge(a_exp_s, n - 1)
                mask = score_mask_first if i * P + g * GQ < LW else score_mask
                steps.did(v.tensor_tensor_reduce(out=Sm[b], in0=bank2[b][:, 0:KEYS], in1=mask[:], scale=1.0,
                                                 scalar=LOWEST, op0=ALU.add, op1=ALU.max,
                                                 accum_out=mx[:, b:b + 1]))
                v.tensor_scalar(nb[:, b:b + 1], mx[:, b:b + 1], -SCALE, None, ALU.mult).then_inc(a_max, 1)

            def local_probs_copy(n):
                dve.wait_ge(a_pt, n + 1)
                v.tensor_copy(PTl, bank[6][0:WIN, 0:P]).then_inc(a_ptl, 1)

            def out_norm(n):
                b = n % 2
                dve.wait_ge(a_exp_s, n + 1)
                steps.did(v.reciprocal(rsum[:, b:b + 1], ssum[:, b:b + 1]))
                dve.wait_ge(a_pv, n + 1)
                if n >= 1:
                    dve.wait_ge(a_ot, n)
                v.tensor_scalar(O_sb, bank[6][:, 128:128 + DC], rsum[:, b:b + 1], None, ALU.mult).then_inc(a_o, 1)

            def out_copy(n):
                i, g = n // NG, n % NG
                dve.wait_ge(a_ot, n + 1)
                v.tensor_copy(OT[i % 2][:, :, g * GQ:(g + 1) * GQ],
                              bank[7][0:DC, 256:384].rearrange("c (h t) -> c h t", h=NH)).then_inc(a_otc, 1)

            def topk():
                dve.wait_ge(s_tk, N_TK)
                dve.wait_ge(t_store_q, STORES_Q * (NCH + 1))
                dve.wait_ge(t_store_k, STORES_K * (NCH + 1))
                for i in range(NT + 1):
                    if i < NT:
                        pick(i)
                    if i >= 1:
                        n0 = NG * (i - 1)
                        rows_rotate(n0)
                        for k in range(NG + 2):
                            if k + 1 < NG:
                                rows_rotate(n0 + k + 1)
                            if k < NG:
                                row_max(n0 + k)
                            if 1 <= k <= NG:
                                local_probs_copy(n0 + k - 1)
                                out_norm(n0 + k - 1)
                            if k >= 2:
                                out_copy(n0 + k - 2)
                        dve.wait_ge(a_y, i)
                        xt = x[:, (i - 1) * P:i * P]
                        ins = v.tensor_tensor(xt, xt, bank[7][:, 384:512], ALU.add).then_inc(a_x, 1)
                        if i % 4 == 0:
                            dve.wait_ge(a_x, i)
                            v.engine_nop().then_inc(x_ready, 1)
                steps.leave(steps.k, 1)

            def int_weights():
                dve.wait_ge(s_int, 48)
                for dst, src in ((gate_w, gate_i), (up_w, up_i), (down_w, down_i)):
                    v.tensor_scalar(dst[:], src[:], float(np.float32(1.0 / 127.0)), None, ALU.mult)\
                        .then_inc(n_w, 1)

            def int_ffn(layer, k):
                with dve.Fori(0, NCH) as c:
                    n = 4 * k + c
                    for m in range(NM2):
                        dve.wait_ge(n_silu, NM2 * n + m + 1)
                        v.tensor_tensor(ia[:, m, :], ia[:, m, :], bank[2 * (m % 2) + 1], ALU.mult)\
                            .then_inc(n_gated, 1)
                    dve.wait_ge(n_down, n + 1)
                    v.tensor_tensor(chunk(x, c), chunk(x, c), bank[0], ALU.add).then_inc(x_ready, 1)

            def linear_attention():
                dve.wait_ge(s_lin, N_LIN)
                dve.wait_ge(ln_applied, LN0 + 4 * L_LIN + 4)
                steps.did(v.memset(KV, 0.0))
                steps.did(v.memset(lv4, 1.0))
                steps.leave(2, 1)
                dve.wait_ge(l_in, 16)
                with dve.Fori(0, NCH) as c:
                    v.tensor_copy(xs_c, chunk(xn, c)).then_inc(l_xs, 1)
                    dve.wait_ge(l_qr, c + 1)
                    v.tensor_tensor(chunk(qf, c), lq, chunk(decay_row, c), ALU.mult)
                    for j in range(4):
                        dve.wait_ge(l_kv, 4 * c + j + 1)
                        kv = bank[1 + j % 2]
                        v.tensor_scalar(lk4[:, j, :], kv[:, 0:P], 0.0, decay_col[:, bass.ds(4 * c + j, 1)],
                                        ALU.max, ALU.mult)
                        v.tensor_copy(lv4[:, j, 0:P], kv[:, P:2 * P]).then_inc(l_kvs, 1)
                    dve.wait_ge(l_KV, c + 1)
                    v.tensor_tensor(KV, KV, bank[3][:, 0:P + 1], ALU.add).then_inc(l_KVa, 1)
                    dve.wait_ge(l_KVa, c + 2)
                v.tensor_tensor(KVm, KV[:, 0:P], same_head[:], ALU.mult).then_inc(l_W, 1)
                v.tensor_scalar(Den, same_head[:], KV[:, P:P + 1], None, ALU.mult).then_inc(l_W, 1)
                with dve.Fori(0, NCH) as c:
                    steps.enter(c, 2)
                    dve.wait_ge(l_nd, c + 1)
                    steps.did(v.tensor_scalar(den, bank[1], EPS_LIN, None, ALU.add))
                    steps.did(v.reciprocal(rden, den))
                    v.tensor_tensor(lo, bank[0], rden, ALU.mult).then_inc(l_o, 1)
                    dve.wait_ge(l_y, c + 1)
                    v.scalar_tensor_tensor(chunk(x, c), bank[2], lbo[:], chunk(x, c), ALU.add, ALU.add)\
                        .then_inc(x_ready, 1)
                steps.leave(2, NCH)

            v.engine_nop().then_inc(ln_applied, LN0)
            for s, free in ((g_out, 1), (g_vg, 1), (t_rot, 1), (t_store_k, STORES_K), (t_store_q, STORES_Q),
                            (l_KVa, 1)):
                v.engine_nop().then_inc(s, free)
            dve.wait_ge(x_loaded, 16)
            v.engine_nop().then_inc(x_ready, 4)
            int_weights()
            layer_norm(L_GLA)
            gla()
            layer_norm(L_FFN0)
            ffn(L_FFN0, 0)
            layer_norm(L_SSM)
            ssm()
            layer_norm(L_FFN1)
            ffn(L_FFN1, 1)
            layer_norm(L_TOPK)
            topk_setup()
            topk()
            layer_norm(L_INT0)
            int_ffn(L_INT0, 0)
            layer_norm(L_LIN)
            linear_attention()
            layer_norm(L_INT1)
            int_ffn(L_INT1, 1)


def lay_out(i):
    A, B, F, K, L, N = "L0_attn_a_", "L0_attn_b_", "L0_ffn_", "L1_attn_a_", "L1_attn_b_", "L1_ffn_"

    def fold(w):
        return w.reshape(-1, P, w.shape[1]).transpose(1, 0, 2)

    def col(w):
        return w.reshape(-1, P).T

    d = {"xT": i[A + "x"][0].T}
    for n in ("Wq", "Wk", "Wv", "Wg", "Wo"):
        d["g" + n] = i[A + n]
    d["Wgk1"], d["Wgk2"], d["bgk2"] = i[A + "Wgk1"], i[A + "Wgk2"], col(i[A + "bgk2"])
    d["gnw"] = np.tile(i[A + "gnw"], GH)[:, None]
    d["lam"] = i[B + "Lambda"][:, None]
    d["log_dt"] = np.tile(i[B + "log_dt"], 64)[:, None]
    d["sBT"], d["sCT"], d["sD"] = i[B + "B"].T, i[B + "C"].T, i[B + "D"][:, None]
    d["w1"], d["w2"] = i[F + "w1_w"].T, i[F + "w2_w"].T
    for n in ("h1", "h2", "w3"):
        d[n] = fold(i[F + n + "_w"].T)
    for n in ("w1", "w2", "h1", "h2", "w3"):
        d[n + "s"] = col(i[F + n + "_s"])
    half = DR // 2
    kr = i[K + "W_kr"]
    d["Wkeys"] = np.concatenate([kr, kr[:, half:], kr[:, :half], i[K + "W_dkv"]], axis=1)
    d["Wdq"] = i[K + "W_dq"]
    qr = i[K + "W_qr"].reshape(DCQ, NH, DR)
    d["Wqr1"], d["Wqr2"] = qr[:, :, :half].reshape(DCQ, P), qr[:, :, half:].reshape(DCQ, P)
    for n, w in (("WuqT", "W_uq"), ("WukT", "W_uk"), ("WuvT", "W_uv")):
        d[n] = i[K + w].reshape(-1, NH, DH).transpose(2, 1, 0)
    d["Wout"] = i[K + "W_out"].reshape(NH, DH, P).transpose(1, 0, 2)
    d["Wiq"] = i[K + "idx_wq"]
    d["Wik"] = np.concatenate([i[K + "idx_wk"]] * 2, axis=1)
    d["iw"] = np.tile(i[K + "idx_w"][None, :], (P, 1))
    d["lWqT"], d["lWoT"] = i[L + "W_q"].T, i[L + "W_o"].T
    d["lWkvT"] = np.concatenate([i[L + "W_k"].T, i[L + "W_v"].T], axis=1)
    d["lbkv"] = np.concatenate([i[L + "b_k"], i[L + "b_v"]])[None, :]
    d["lbq"], d["lbo"] = i[L + "b_q"][:, None], i[L + "b_o"][:, None]
    d["gate_i"], d["up_i"] = i[N + "w_gate"].T, i[N + "w_up"].T
    d["down_i"] = fold(i[N + "w_down"].T).reshape(P, HID2)
    return d


def kernel(**inputs):
    import concourse.bacc as bacc
    from concourse.bass_utils import run_bass_kernel_spmd

    nc = bacc.Bacc("TRN2", target_bir_lowering=False, num_devices=1)
    arrays = {n: np.ascontiguousarray(a) for n, a in
              {**lay_out({n: np.asarray(a) for n, a in inputs.items()}), **shape_tables()}.items()}
    aps = {n: nc.dram_tensor("in_" + n, a.shape, mybir.dt.from_np(a.dtype), kind="ExternalInput").ap()
           for n, a in arrays.items()}
    out = nc.dram_tensor("out", (P, T), F32, kind="ExternalOutput").ap()
    hybrid_kernel(nc, aps, out)
    r = run_bass_kernel_spmd(nc, [{"in_" + n: a for n, a in arrays.items()}], core_ids=[0])
    return np.ascontiguousarray(r.results[0]["out"].T)[None]
```

```python
from contextlib import ExitStack

import numpy as np

import concourse.bass as bass
from concourse import mybir

F32 = mybir.dt.float32
I32 = mybir.dt.int32
U32 = mybir.dt.uint32
ALU = mybir.AluOpType
ACT = mybir.ActivationFunctionType

P = 128
T = 2048
C = 512
NCH = T // C
NT = T // P
EPS_LN = 1e-5
LN0 = 2
STORES_K, STORES_Q = 16, 96
EPS_LIN = 1e-6
GH, GDK, GDV, GCHUNK = 4, 128, 32, 64
NH, DR, DC, DCQ, DH = 8, 32, 32, 64, 64
NIH = 4
KTOP, LW = 96, 64
JG = KTOP - LW
ROW = 2 * DR + DC
SCALE = (DH + DR) ** -0.5
GQ = 16
NG = P // GQ
WIN = LW + GQ
QD = P // JG
KEYS = P + WIN
NEG = -1e30
LOWEST = -3e38
TAKEN = -3.3e38
HID = 512
NM = HID // P
HID2 = 384
NM2 = HID2 // P
LH, LDK = 16, 8


def shape_tables():
    f32 = np.float32
    t = {}
    t["ident"] = np.eye(P, dtype=f32)
    t["center"] = (np.eye(P) - 1.0 / P).astype(f32)
    t["mean_all"] = np.full((P, P), 1.0 / P, f32)
    same = np.arange(P)[:, None] // GDV == np.arange(P)[None, :] // GDV
    t["mean_head"] = (same / GDV).astype(f32)
    t["same_head"] = (np.arange(P)[:, None] // LDK == np.arange(P)[None, :] // LDK).astype(f32)
    j, i = np.arange(P)[:, None], np.arange(P)[None, :]
    t["gla_mask"] = ((j <= i) & (j // GCHUNK == i // GCHUNK)).astype(f32)
    t["scan_keep"] = np.tile((np.arange(P) % GCHUNK != 0).astype(f32), (P, GH))
    cols = np.zeros((P, 4), f32)
    cols[:, 0] = EPS_LN
    cols[:, 1] = 1.0
    t["cols"] = cols
    half = DR // 2
    theta = 1.0 / 10000.0 ** (2.0 * np.arange(half) / DR)
    pos = np.arange(T)
    q_g = theta[:, None] * pos[None, :]
    q_l = theta[:, None] * (pos + np.maximum(pos - (LW - 1), 0))[None, :]
    for name, a in (("qg", q_g), ("ql", q_l)):
        t["cos_" + name] = np.tile(np.cos(a), (NH, 1)).astype(f32)
        t["sin_" + name] = np.tile(np.sin(a), (NH, 1)).astype(f32)
    c, s = np.cos(q_g), np.sin(q_g)
    t["key_rope"] = np.concatenate([c, c, -s, s]).astype(f32)
    a = (LW + np.arange(JG))[:, None] * theta[None, :]
    row = np.concatenate([np.cos(a), np.cos(a), -np.sin(a), np.sin(a), np.ones((JG, DC))], axis=1)
    t["rank_rope"] = np.tile(row, (P // JG, 1)).astype(f32)
    r = np.arange(P)
    tq, q = r % QD, r // (NH * QD) * QD + r % QD
    own = (np.arange(P) // JG)[None, :] == tq[:, None]
    x = np.arange(WIN)[None, :]
    near = (x >= 1 + q[:, None]) & (x <= LW + q[:, None])
    first = np.broadcast_to(x < LW, (P, WIN))
    t["score_mask"] = np.where(np.concatenate([own, near], 1), 0, NEG).astype(f32)
    t["score_mask_first"] = np.where(np.concatenate([own, first], 1), 0, NEG).astype(f32)
    p, s = np.arange(P)[:, None], np.arange(KTOP)[None, :]
    past, local = s <= p - LW, (s <= p) & (s > p - LW)
    local = local | ((p < LW) & (s < LW))
    t["index_mask_first"] = np.where(local, LOWEST, np.where(past, 0, NEG)).astype(f32)
    t["index_mask"] = np.where(np.arange(P)[None, :] <= p, 0, LOWEST).astype(f32)
    dec = np.exp(-np.arange(T, dtype=f32) / f32(T)).astype(f32)
    t["decay_row"] = np.broadcast_to(dec, (P, T))
    t["decay_col"] = dec.reshape(NT, P).T
    t["ones_row"] = np.ones((1, P), f32)
    return t


TABLES = ["ident", "center", "mean_all", "mean_head", "same_head", "gla_mask", "scan_keep", "cols", "cos_qg",
          "sin_qg", "cos_ql", "sin_ql", "key_rope", "rank_rope", "score_mask", "score_mask_first",
          "index_mask_first", "index_mask", "decay_row", "decay_col", "ones_row"]


class Steps:

    def __init__(self, eng, sem):
        self.eng, self.sem, self.base, self.loop, self.k = eng, sem, 0, 0, 0

    def enter(self, i, per):
        self.loop, self.k = i * per, 0

    def leave(self, per, times):
        assert self.k == per, (self.k, per)
        self.base, self.loop, self.k = self.base + per * times, 0, 0

    def did(self, ins):
        self.k += 1
        ins.then_inc(self.sem, 1)
        self.eng.wait_ge(self.sem, self.base + self.loop + self.k)


def hybrid_kernel(nc, d, out):
    with ExitStack() as ctx:
        def sem(name):
            return ctx.enter_context(nc.semaphore(name))

        def sb(name, shape, dt=F32):
            return ctx.enter_context(nc.sbuf_tensor(name, shape, dt))

        def dram(name, shape):
            return nc.dram_tensor(name, shape, F32, kind="Internal").ap()

        bank2 = [ctx.enter_context(nc.psum_tensor(f"bank{2 * i}_{2 * i + 1}", [P, 2 * C], F32)) for i in range(4)]
        bank = [bank2[i // 2][:, (i % 2) * C:(i % 2) * C + C] for i in range(8)]

        x = sb("x", [P, T])
        xn = sb("xn", [P, T])
        LOAD = {}

        def load(name, dt=F32):
            LOAD[name] = sb(name, list(d[name].shape), dt)
            return LOAD[name]

        ident, center, mean_all, mean_head = load("ident"), load("center"), load("mean_all"), load("mean_head")
        same_head, gla_mask, scan_keep, cols = load("same_head"), load("gla_mask"), load("scan_keep"), load("cols")
        rank_rope, ones_row = load("rank_rope"), load("ones_row")
        score_mask, score_mask_first = load("score_mask"), load("score_mask_first")
        index_mask, index_mask_first, decay_col = load("index_mask"), load("index_mask_first"), load("decay_col")
        eps_col, one_col = cols[:, 0:1], cols[:, 1:2]
        gWv, gWg, gWo, Wgk1, Wgk2 = (load(n) for n in ("gWv", "gWg", "gWo", "Wgk1", "Wgk2"))
        bgk2, gnw = load("bgk2"), load("gnw")
        lam, log_dt, sBT, sCT, sD = (load(n) for n in ("lam", "log_dt", "sBT", "sCT", "sD"))
        w1, w2, h1, h2, w3 = (load(n) for n in ("w1", "w2", "h1", "h2", "w3"))
        w1s, w2s, h1s, h2s, w3s = (load(n) for n in ("w1s", "w2s", "h1s", "h2s", "w3s"))
        Wkeys, Wdq, Wqr1, Wqr2 = (load(n) for n in ("Wkeys", "Wdq", "Wqr1", "Wqr2"))
        Wiq, Wik, iw = (load(n) for n in ("Wiq", "Wik", "iw"))
        lWqT, lWkvT, lWoT, lbq, lbkv, lbo = (load(n) for n in ("lWqT", "lWkvT", "lWoT", "lbq", "lbkv", "lbo"))
        gate_w, up_w, down_w = (sb(n, [P, HID2]) for n in ("gate_w", "up_w", "down_w"))

        ARENA = 33 * 1024
        arena = sb("arena", [P, ARENA])
        at = [0]

        def part(*shape, parts=P):
            n = int(np.prod(shape))
            assert at[0] + n <= ARENA, (at[0], n)
            v = arena[0:parts, at[0]:at[0] + n]
            at[0] += n
            if len(shape) == 2:
                v = v.rearrange("p (a b) -> p a b", a=shape[0])
            return v

        sq, sd = part(2, C), part(2, C)
        LAYER = at[0]
        gWq, gWk = part(GH * GDK), part(GH * GDK)
        xs_t, r_sb = part(P), part(P, parts=16)
        zb, ab, lg, Gc = (part(GH, P) for _ in range(4))
        eG, emG, qg, kI, kIT, AT = (part(GH, P) for _ in range(6))
        vt, S, S_in = part(P), part(P), part(P)
        eg, egr = part(P), part(P)
        oT, gate = part(T), part(T)
        o_sq, o_sd = part(C), part(C)
        at[0] = LAYER
        fa, fb = part(NM, C), part(NM, C)
        at[0] = LAYER
        a_exp, a_dt, a_neg, a_dec, carry = (part(1, parts=64) for _ in range(5))
        keep, states = part(C, parts=64), part(T, parts=64)
        at[0] = LAYER
        KL, ki = part(T, parts=ROW), part(T)
        qi = part(2, T)
        Muv = part(NH, P, parts=DC)
        TOPK = at[0]
        WuqT, WukT = part(NH, DCQ, parts=DH), part(NH, DC, parts=DH)
        WuvT, Wout = part(NH, DC, parts=DH), part(NH, P, parts=DH)
        Mq = part(NH * DC, parts=DCQ)
        key_rope = part(C, parts=2 * DR)
        rope_tab = part(4, C)
        cq, raw, rows = part(C, parts=DCQ), part(C, parts=ROW), part(4, ROW)
        k_abs = part(C, parts=2 * DR)
        q_abs, mu = part(2, C), part(2, C)
        rot = part(4, C)
        rot_t = part(2, C)
        qt_sb = part(2, C)
        at[0] = TOPK
        I_s = part(2, T)
        relu = part(4, C)
        top8 = part(JG)
        idx_f = part(JG)
        G = [part(P // 4, ROW) for _ in range(2)]
        QL_in, QG_in = part(NH, P, parts=ROW), part(NH, P, parts=ROW)
        QL, QG = part(NG, P, parts=ROW), part(NG, P, parts=ROW)
        Vloc = [part(NG, DC, parts=WIN) for _ in range(2)]
        GR = [part(4, ROW) for _ in range(2)]
        GT = [part(C, parts=ROW) for _ in range(2)]
        Sm = [part(KEYS) for _ in range(2)]
        Pr = [part(KEYS) for _ in range(2)]
        PTg = [part(P) for _ in range(2)]
        PTl = [part(P, parts=WIN) for _ in range(2)]
        mx, nb, ssum, rsum = (part(2) for _ in range(4))
        OT = [part(NH, P, parts=DC) for _ in range(2)]
        at[0] = LAYER
        decay_row = part(T)
        qf = part(T)
        xs_c = part(C)
        lk4, lv4 = part(4, P), part(4, P + 1)
        KV, KVm, Den = part(P + 1), part(P), part(P)
        lq = part(C)
        den, rden, lo = part(C), part(C), part(C)
        at[0] = LAYER
        ia = part(NM2, C)
        gate_i, up_i, down_i = (sb(n, [P, HID2], I32) for n in ("gate_i", "up_i", "down_i"))
        idx_u = sb("idx_u", [P, JG], U32)
        idx_T = sb("idx_T", [P, NT, P // 4], U32)

        key_table = dram("key_table", (T, ROW))
        q_rot = {n: dram("q_" + n, (2, P, T)) for n in ("l", "g")}
        q_lat = dram("q_lat", (NH * DC, T))

        (s_tab, s_gla, s_ssm, s_ffn, s_tk, s_lin, s_int) = (
            sem("loaded_" + n) for n in ("tables", "gla", "ssm", "ffn", "topk", "lin", "int"))
        x_loaded, x_ready = sem("x_loaded"), sem("x_ready")
        ln_centered, ln_squared, ln_var, ln_sd, ln_applied = (
            sem("ln_" + n) for n in ("centered", "squared", "var", "sd", "applied"))
        dve_step, act_step, pool_step, pe_step = sem("dve_step"), sem("act_step"), sem("pool_step"), sem("pe_step")

        LOADS = {
            s_tab: ["ident", "center", "mean_all", "cols"],
            s_gla: ["gWv", "gWg", "gWo", "Wgk1", "Wgk2", "bgk2", "gnw", "mean_head", "gla_mask", "scan_keep"],
            s_ffn: ["w1", "w2", "h1", "h2", "w3", "w1s", "w2s", "h1s", "h2s", "w3s"],
            s_ssm: ["lam", "log_dt", "sBT", "sCT", "sD"],
            s_tk: ["Wkeys", "Wdq", "Wqr1", "Wqr2", "Wiq", "Wik", "iw", "rank_rope", "score_mask",
                   "score_mask_first", "index_mask", "index_mask_first"],
            s_lin: ["lWqT", "lWkvT", "lWoT", "lbq", "lbkv", "lbo", "same_head", "decay_col", "ones_row"],
        }
        assert {n for v in LOADS.values() for n in v} == set(LOAD)
        N_TAB, N_GLA, N_FFN, N_SSM, N_TK, N_LIN = (16 * len(v) for v in LOADS.values())

        (g_xs, g_r, g_rs, g_zqk, g_vg, g_lnz, g_G, g_exp, g_eg, g_qk, g_kT, g_kTs, g_A, g_AT, g_vts, g_o, g_dS,
         g_S, g_out, g_osq, g_oms, g_osd, g_on, g_y) = (
            sem("gla_" + n) for n in (
                "tile_staged", "lowrank", "lowrank_copied", "projected", "vg_projected", "log_gate", "cumulated",
                "decays", "gate_exp", "scaled", "k_turned", "k_turned_copied", "scores", "scores_masked",
                "v_copied", "read_out", "state_add", "state_ready", "tile_done", "squared", "mean_sq", "rms",
                "normed", "projected_out"))
        g_zb = sem("gla_gate_biased")
        f_up, f_silu, f_gated, f_h1, f_g1, f_h2, f_g2, f_down = (
            sem("ffn_" + n) for n in ("up", "silu", "gated", "hidden1", "gelu1", "hidden2", "gelu2", "down"))
        ss_a, ss_u, ss_x, ss_y = (sem("ssm_" + n) for n in ("decay_ready", "inputs", "states", "outputs"))
        (t_w, t_wm, t_wc, t_wdone, t_cq, t_cqs, t_raw, t_kln, t_rawd, t_kl, t_rows, t_rowss, t_iq, t_iqs, t_qp,
         t_qln, t_rot, t_qlat, t_qlats, t_tab) = (
            sem("topk_" + n) for n in (
                "weights", "merged", "merged_copied", "setup_done", "cq", "cq_copied", "raw_keys", "key_log",
                "keys_ready", "local_keys", "key_rows", "key_rows_copied", "index_proj", "index_copied",
                "query_proj", "query_log", "rotated", "q_latent", "q_latent_copied", "rope_tables"))
        t_store_k, t_store_q = sem("topk_keys_stored"), sem("topk_queries_stored")
        (i_s, i_relu, i_used, i_done, i_perm, i_idx) = (
            sem("index_" + n) for n in ("scores", "relu", "relu_used", "picked", "permuted", "ready"))
        gathered = [[sem(f"gathered{b}_{g}") for g in range(NG)] for b in range(2)]
        q_loaded, a_q = sem("queries_loaded"), sem("queries_regrouped")
        v_loaded = [sem(f"local_values_loaded{b}") for b in range(2)]
        (a_rot, a_gt, a_gts, a_s, a_max, a_exp_s, a_pt, a_pts, a_pv, a_pn, a_otc, a_y, a_x) = (
            sem("attn_" + n) for n in (
                "rows_rotated", "rows_turned", "rows_turned_copied", "scores", "max", "probs", "probs_turned",
                "probs_copied", "values", "probs_normed", "out_copied", "projected",
                "added"))
        (l_q, l_qr, l_qf, l_xs, l_kv, l_kvs, l_KV, l_KVa, l_W, l_nd, l_o, l_y, l_in) = (
            sem("lin_" + n) for n in (
                "q", "q_relu", "q_features", "chunk_staged", "kv", "kv_features", "outer", "outer_added",
                "weights_ready", "num_den", "normed", "projected", "decay_loaded"))
        n_w, n_up, n_silu, n_gated, n_down = (
            sem("int_" + n) for n in ("weights_ready", "up", "silu", "gated", "down"))
        stored = sem("stored")

        ATTN_LAG = NG
        PICK_SLOTS = NG * NT - 6
        SLOTS = NG * NT + ATTN_LAG + 4

        def index_width(i):
            return KTOP if i == 0 else i * P + P - LW

        def index_units(i):
            W = index_width(i)
            return [(s0, min(C, W - s0), h) for s0 in range(0, W, C) for h in range(NIH)]

        UNITS_BEFORE = [sum(len(index_units(k)) for k in range(i)) for i in range(NT + 1)]
        N_ROUNDS = JG // 8

        SUMS = [[((i, "sum", u), w + 60) for u, (_, w, _) in enumerate(index_units(i))] for i in range(NT)] + [[]]
        PICKS = [[((i, "mask", 0), 190)] +
                 [((i, what, r), index_width(i) + 60) for r in range(N_ROUNDS) for what in ("max", "index", "drop")
                  if (what, r) != ("drop", N_ROUNDS - 1)] +
                 [((i, "turn", 0), 100), ((i, "rows", 0), 100)] for i in range(NT)]

        def cost(todo):
            return sum(c for _, c in todo)

        def spread(todo, first, last):
            run, total = 0, cost(todo)
            for step, c in todo:
                SLOT_STEPS[int(first + (last - first) * run / total) + (step[1] == "rows")].append(step)
                run += c

        SLOT_STEPS = [[] for _ in range(SLOTS)]
        spread(SUMS[0], 0, 1)
        start, per_slot = 1, (cost(sum(SUMS[1:] + PICKS, []))) / (PICK_SLOTS - 1)
        for i in range(NT):
            end = start + cost(SUMS[i + 1] + PICKS[i]) / per_slot
            spread(PICKS[i], start, end)
            spread(SUMS[i + 1], start, end)
            start = end
        for todo in SLOT_STEPS:
            todo.sort(key=lambda step: (step[1] != "rows", 2 * step[0] - (step[1] == "sum")))

        GROUPS = NG * NT

        def regroups(s):
            i, at_ = divmod(s - ATTN_LAG, NG)
            i, pair = (i, 3) if at_ == 0 else (i + 1, at_ - 4)
            return (i, pair) if 0 <= i < NT and 0 <= pair < 4 and at_ != NG - 1 else None

        def score_bank(n):
            return bank[(0, 1, 4)[n % 3]]

        L_GLA, L_FFN0, L_SSM, L_FFN1, L_TOPK, L_INT0, L_LIN, L_INT1 = range(8)

        def chunk(a, c):
            return a[:, bass.ds(c * C, C)]

        block = ctx.enter_context(nc.Block())

        @block.sync
        def _(sp):
            sp.dma_start(x[:, :], d["xT"]).then_inc(x_loaded, 16)
            for s, names in LOADS.items():
                for n in names:
                    sp.dma_start(LOAD[n][:], d[n]).then_inc(s, 16)
                if s is s_gla:
                    sp.dma_start(gWq, d["gWq"]).then_inc(s, 16)
                    sp.dma_start(gWk, d["gWk"]).then_inc(s, 16)
            for n, dst in (("gate_i", gate_i), ("up_i", up_i), ("down_i", down_i)):
                sp.dma_start(dst[:], d[n]).then_inc(s_int, 16)

            sp.wait_ge(x_ready, 4 * L_TOPK + 4)
            for n, dst in (("WuqT", WuqT), ("WukT", WukT), ("WuvT", WuvT), ("Wout", Wout)):
                sp.dma_start(dst, d[n]).then_inc(t_w, 16)
            with sp.Fori(0, NCH) as c:
                sp.wait_ge(t_rot, c + 1)
                for k, n in enumerate(("cos_ql", "sin_ql", "cos_qg", "sin_qg")):
                    sp.dma_start(rope_tab[:, k, :], chunk(d[n], c)).then_inc(t_tab, 16)
                sp.dma_start(key_rope, chunk(d["key_rope"], c)).then_inc(t_tab, 16)
                sp.wait_ge(t_rowss, c + 1)
                sp.dma_start(key_table[bass.ds(c * C, C), :].rearrange("(b p) r -> p b r", p=P), rows)\
                    .then_inc(t_store_k, 16)
                sp.wait_ge(t_qlats, 2 * c + 2)
                for k in range(2):
                    sp.dma_start(chunk(q_lat[k * P:k * P + P, :], c), qt_sb[:, k, :]).then_inc(t_store_q, 16)
                sp.wait_ge(t_rot, c + 2)
                for k, n in enumerate("llgg"):
                    sp.dma_start(chunk(q_rot[n][k % 2], c), rot[:, k, :]).then_inc(t_store_q, 16)
            sp.wait_ge(t_store_q, STORES_Q * (NCH + 1))
            sp.wait_ge(t_store_k, STORES_K * (NCH + 1))
            sp.wait_ge(t_rot, NCH + 1)
            for i in range(NT):
                b = i % 2
                if i >= 1:
                    sp.wait_ge(a_q, 4 * i)
                half = DR // 2
                for dst, n in ((QL_in, "l"), (QG_in, "g")):
                    for r in range(4):
                        src = q_rot[n][r % 2][:, i * P:(i + 1) * P].rearrange("(h f) t -> f h t", f=half)
                        sp.dma_start(dst[r * half:(r + 1) * half], src).then_inc(q_loaded, 16)
                    src = q_lat[:, i * P:(i + 1) * P].rearrange("(h c) t -> c h t", c=DC)
                    sp.dma_start(dst[2 * DR:ROW], src).then_inc(q_loaded, 16)
                if i >= 2:
                    sp.wait_ge(a_pv, NG * (i - 1))
                for g in range(NG):
                    s0 = max(i * P + g * GQ - LW, 0)
                    sp.dma_start(Vloc[b][:, g, :], key_table[s0:s0 + WIN, 2 * DR:ROW]).then_inc(v_loaded[b], 16)

            sp.wait_ge(x_ready, 4 * L_LIN + 4)
            sp.dma_start(decay_row, d["decay_row"]).then_inc(l_in, 16)
            with sp.Fori(0, NCH) as c:
                sp.wait_ge(x_ready, 4 * L_INT1 + 5 + c)
                sp.dma_start(chunk(out, c), chunk(x, c)).then_inc(stored, 16)
            sp.wait_ge(stored, 16 * NCH)

        @block.gpsimd
        def _(pool):
            pool.wait_ge(t_store_k, STORES_K * (NCH + 1))
            pool.wait_ge(t_rot, NCH + 1)
            for i in range(NT):
                b = i % 2
                pool.wait_ge(i_idx, i + 1)
                if i >= 2:
                    pool.wait_ge(a_pv, NG * (i - 1))
                for q in range(P // 4):
                    pool.indirect_dma_start(
                        out=G[b][:, q, :], out_offset=None, in_=key_table,
                        in_offset=bass.IndirectOffsetOnAxis(ap=idx_T[:, i, q:q + 1], axis=0),
                    ).then_inc(gathered[b][q // 4], 16)

        @block.tensor
        def _(pe):
            def mm(out_, lhsT, rhs, start=True, stop=True, **kw):
                return pe.matmul(out_, lhsT, rhs, start=start, stop=stop, **kw)

            def layer_norm(k):
                with pe.Fori(0, 2) as r:
                    for u in range(2):
                        n = 4 * k + r * 2 + u
                        pe.wait_ge(x_ready, n + 1)
                        pe.wait_ge(ln_applied, LN0 + n - 1)
                        mm(bank[4 + u], center[:], chunk(x, r * 2 + u)).then_inc(ln_centered, 1)
                    for u in range(2):
                        pe.wait_ge(ln_squared, 4 * k + r * 2 + u + 1)
                        mm(bank[6 + u], mean_all[:], sq[:, u, :]).then_inc(ln_var, 1)

            def gla():
                pe.wait_ge(s_gla, N_GLA + 32)
                pe.wait_ge(ln_applied, LN0 + 4 * L_GLA + 4)
                with pe.Fori(0, NT) as i:
                    pe.wait_ge(g_xs, i + 1)
                    pe.wait_ge(g_out, i + 1)
                    mm(bank[0][0:16, 0:P], Wgk1[:], xs_t).then_inc(g_r, 1)
                    for h in range(GH):
                        mm(bank[2][:, h * P:h * P + P], gWq[:, h * GDK:(h + 1) * GDK], xs_t)
                        mm(bank[3][:, h * P:h * P + P], gWk[:, h * GDK:(h + 1) * GDK], xs_t)
                    mm(bank[7][:, 256:384], gWg[:], xs_t)
                    mm(bank[7][:, 384:512], xs_t, gWv[:]).then_inc(g_vg, 1)
                    pe.wait_ge(g_rs, i + 1)
                    for h in range(GH):
                        last = mm(bank[1][:, h * P:h * P + P], Wgk2[:, h * GDK:(h + 1) * GDK], r_sb)
                    last.then_inc(g_zqk, 1)
                    pe.wait_ge(g_qk, i + 1)
                    for h in range(GH):
                        last = mm(bank[5][:, h * P:h * P + P], kI[:, h, :], qg[:, h, :])
                    last.then_inc(g_A, 1)
                    for h in range(GH):
                        last = pe.transpose(bank[4][:, h * P:h * P + P], kI[:, h, :], ident[:])
                    last.then_inc(g_kT, 1)
                    pe.wait_ge(g_AT, i + 1)
                    pe.wait_ge(g_vts, i + 1)
                    for h in range(GH):
                        mm(bank[6][GDV * h:GDV * h + GDV, 0:P], vt[:, GDV * h:GDV * h + GDV], AT[:, h, :],
                           stop=False, tile_position=(0, GDV * h), skip_group_check=True)
                    for half in range(2):
                        lo_, hi_ = half * GCHUNK, (half + 1) * GCHUNK
                        pe.wait_ge(g_S, i * 2 + half + 1)
                        for h in range(GH):
                            last = mm(bank[6][GDV * h:GDV * h + GDV, lo_:hi_], S[:, GDV * h:GDV * h + GDV],
                                      qg[:, h, lo_:hi_], start=False, stop=True, tile_position=(0, GDV * h),
                                      skip_group_check=True)
                        if half == 1:
                            last.then_inc(g_o, 1)
                        if half == 0:
                            pe.wait_ge(g_kTs, i + 1)
                        for h in range(GH):
                            last = mm(bank[7][:, half * P + GDV * h:half * P + GDV * h + GDV],
                                      kIT[lo_:hi_, h, :], vt[lo_:hi_, GDV * h:GDV * h + GDV])
                        last.then_inc(g_dS, 1)
                with pe.Fori(0, NCH) as c:
                    pe.wait_ge(g_osq, c + 1)
                    mm(bank[0], mean_head[:], o_sq).then_inc(g_oms, 1)
                    pe.wait_ge(g_on, c + 1)
                    mm(bank[1], gWo[:], chunk(oT, c)).then_inc(g_y, 1)

            def ffn(layer, k):
                pe.wait_ge(s_ffn, N_FFN)
                with pe.Fori(0, NCH) as c:
                    n = 4 * k + c
                    pe.wait_ge(ln_applied, LN0 + 4 * layer + 1 + c)
                    pe.wait_ge(x_ready, 4 * layer + 4 + c)
                    for m in range(NM):
                        if m >= 2:
                            pe.wait_ge(f_gated, 4 * n + m - 1)
                        mm(bank[2 * (m % 2)], w1[:, m * P:m * P + P], chunk(xn, c))
                        mm(bank[2 * (m % 2) + 1], w2[:, m * P:m * P + P], chunk(xn, c)).then_inc(f_up, 1)
                    pe.wait_ge(f_gated, 4 * n + NM)
                    for m in range(NM):
                        for kk in range(NM):
                            last = mm(bank[m], h1[:, kk, m * P:m * P + P], fa[:, kk, :], kk == 0, kk == NM - 1)
                        last.then_inc(f_h1, 1)
                    for m in range(NM):
                        pe.wait_ge(f_g1, 4 * n + NM)
                        for kk in range(NM):
                            last = mm(bank[m], h2[:, kk, m * P:m * P + P], fb[:, kk, :], kk == 0, kk == NM - 1)
                        last.then_inc(f_h2, 1)
                    pe.wait_ge(f_g2, 4 * n + NM)
                    for kk in range(NM):
                        last = mm(bank[0], w3[:, kk, :], fa[:, kk, :], kk == 0, kk == NM - 1)
                    last.then_inc(f_down, 1)

            def ssm():
                pe.wait_ge(s_ssm, N_SSM)
                with pe.Fori(0, NCH) as c:
                    pe.wait_ge(ln_applied, LN0 + 4 * L_SSM + 1 + c)
                    pe.wait_ge(x_ready, 4 * L_SSM + 4 + c)
                    mm(bank[0][0:64, :], sBT[:], chunk(xn, c)).then_inc(ss_u, 1)
                    pe.wait_ge(ss_x, c + 1)
                    mm(bank[1], sCT[:], chunk(states, c)).then_inc(ss_y, 1)

            def topk_setup():
                pe.wait_ge(s_tk, N_TK)
                pe.wait_ge(t_w, 64)
                pe.wait_ge(x_ready, 4 * L_TOPK + 4)
                for h in range(NH):
                    last = mm(bank[0][0:DCQ, h * DC:(h + 1) * DC], WuqT[:, h, :], WukT[:, h, :])
                for h in range(NH):
                    last = mm(bank[1 + h // 4][0:DC, (h % 4) * P:(h % 4 + 1) * P], WuvT[:, h, :], Wout[:, h, :])
                last.then_inc(t_wm, 1)
                pe.wait_ge(t_wc, 3)
                pe.wait_ge(ln_applied, LN0 + 4 * L_TOPK + 4)
                with pe.Fori(0, NCH) as c:
                    pe.wait_ge(t_rot, c + 1)
                    mm(bank[0][0:DCQ, :], Wdq[:], chunk(xn, c)).then_inc(t_cq, 1)
                    mm(bank[1][0:ROW, :], Wkeys[:], chunk(xn, c)).then_inc(t_raw, 1)
                    mm(bank[2], Wiq[:, 0:P], chunk(xn, c))
                    mm(bank[3], Wiq[:, P:2 * P], chunk(xn, c))
                    mm(bank[4], Wik[:], chunk(xn, c)).then_inc(t_iq, 1)
                    pe.wait_ge(t_cqs, c + 1)
                    mm(bank[5], Wqr1[:], cq)
                    mm(bank[6], Wqr2[:], cq).then_inc(t_qp, 1)
                    mm(bank[7], Mq[:, 0:P], cq).then_inc(t_qlat, 1)
                    mm(bank[0], Mq[:, P:2 * P], cq).then_inc(t_qlat, 1)
                    pe.wait_ge(t_rawd, c + 1)
                    for j in range(4):
                        last = pe.transpose(bank[1][:, j * ROW:(j + 1) * ROW], raw[:, j * P:(j + 1) * P],
                                            ident[0:ROW, 0:ROW])
                    last.then_inc(t_rows, 1)

            bank5_read = [None]

            def bank5_free(reader):
                if bank5_read[0]:
                    pe.wait_ge(*bank5_read[0])
                bank5_read[0] = reader

            def index_scores(i, k):
                s0, w, h = index_units(i)[k]
                u = UNITS_BEFORE[i] + k
                if u >= 2:
                    pe.wait_ge(i_relu, u - 1)
                lo_ = 64 * (h % 2)
                mm(bank[6 + u % 2][:, 0:w], qi[lo_:lo_ + 64, h // 2, i * P:(i + 1) * P],
                   ki[lo_:lo_ + 64, s0:s0 + w]).then_inc(i_s, 1)

            def index_turn(i):
                pe.wait_ge(i_done, i + 1)
                bank5_free((i_idx, i + 1))
                for tq in range(4):
                    last = mm(bank[5][JG * tq:JG * tq + JG, 256:256 + P // 4], idx_f, ident[:, tq:P:4],
                              tile_position=(0, JG * tq), skip_group_check=True)
                last.then_inc(i_perm, 1)

            def rows_turn(n):
                pe.wait_ge(a_rot, n + 1)
                if n >= 2:
                    pe.wait_ge(a_gts, n - 1)
                for j in range(4):
                    last = pe.transpose(bank[2 + n % 2][0:ROW, j * P:(j + 1) * P], GR[n % 2][:, j, :], ident[:])
                last.then_inc(a_gt, 1)

            def scores(n):
                i, g = n // NG, n % NG
                pe.wait_ge(a_gts, n + 1)
                pe.wait_ge(a_q, 4 * i + g // 2 + 1)
                if n >= 3:
                    pe.wait_ge(a_otc, n - 2)
                s0 = max(i * P + g * GQ - LW, 0)
                sb_, w = score_bank(n), NH * QD
                mm(sb_[:, P:KEYS], QL[:, g, :], KL[:, s0:s0 + WIN])
                for j in range(4):
                    last = mm(sb_[j * w:(j + 1) * w, 0:P], QG[:, g, j * w:(j + 1) * w],
                              GT[n % 2][:, j * P:(j + 1) * P], tile_position=(0, j * w))
                last.then_inc(a_s, 1)

            def probs_turn(n):
                pe.wait_ge(a_pn, n + 1)
                pe.transpose(score_bank(n)[:, 0:P], Pr[n % 2][:, 0:P], ident[:])
                pe.transpose(score_bank(n)[0:WIN, P:2 * P], Pr[n % 2][:, P:KEYS], ident[:]).then_inc(a_pt, 1)

            def values(n):
                i, g = n // NG, n % NG
                b, w = i % 2, NH * QD
                if g == 0:
                    pe.wait_ge(v_loaded[b], 16 * NG * (i // 2 + 1))
                pe.wait_ge(a_pts, n + 1)
                o_ = score_bank(n)[0:DC, 2 * P:3 * P]
                mm(o_, Vloc[b][:, g, :], PTl[n % 2], True, False, skip_group_check=True)
                for j in range(4):
                    last = mm(o_[:, j * w:(j + 1) * w], G[b][:, g * 4 + j, 2 * DR:ROW], PTg[n % 2][:, j * w:(j + 1) * w],
                              False, True, skip_group_check=True)
                last.then_inc(a_pv, 1)

            def out_project(i):
                pe.wait_ge(a_otc, NG * (i + 1))
                bank5_free((a_x, i + 1))
                for h in range(NH):
                    last = mm(bank[5][:, 128:256], Muv[:, h, :], OT[i % 2][:, h, :], h == 0, h == NH - 1,
                              skip_group_check=True)
                last.then_inc(a_y, 1)

            def topk():
                pe.wait_ge(t_rot, NCH + 1)
                for s in range(SLOTS):
                    n = s - ATTN_LAG
                    if 0 <= n + 1 < GROUPS:
                        rows_turn(n + 1)
                    if 0 <= n < GROUPS:
                        scores(n)
                    if 0 <= n - 2 < GROUPS:
                        values(n - 2)
                    for i, what, k in SLOT_STEPS[s]:
                        if what == "sum":
                            index_scores(i, k)
                    if 0 <= n - 1 < GROUPS:
                        probs_turn(n - 1)
                    if 0 <= n - 2 < GROUPS and (n - 2) % NG == NG - 1:
                        out_project((n - 2) // NG)
                    for i, what, _ in SLOT_STEPS[s]:
                        if what == "turn":
                            index_turn(i)
                pe.wait_ge(a_x, NT)

            def int_ffn(layer, k):
                pe.wait_ge(n_w, 3)
                with pe.Fori(0, NCH) as c:
                    n = 4 * k + c
                    pe.wait_ge(ln_applied, LN0 + 4 * layer + 1 + c)
                    pe.wait_ge(x_ready, 4 * layer + 4 + c)
                    for m in range(NM2):
                        if m >= 2:
                            pe.wait_ge(n_gated, NM2 * n + m - 1)
                        mm(bank[2 * (m % 2)], gate_w[:, m * P:m * P + P], chunk(xn, c))
                        mm(bank[2 * (m % 2) + 1], up_w[:, m * P:m * P + P], chunk(xn, c)).then_inc(n_up, 1)
                    pe.wait_ge(n_gated, NM2 * n + NM2)
                    for m in range(NM2):
                        last = mm(bank[0], down_w[:, m * P:m * P + P], ia[:, m, :], m == 0, m == NM2 - 1)
                    last.then_inc(n_down, 1)

            def linear_attention():
                pe.wait_ge(s_lin, N_LIN)
                pe.wait_ge(ln_applied, LN0 + 4 * L_LIN + 4)
                with pe.Fori(0, NCH) as c:
                    pe.wait_ge(l_KVa, c + 1)
                    mm(bank[0], lWqT[:], chunk(xn, c)).then_inc(l_q, 1)
                    pe.wait_ge(l_xs, c + 1)
                    for j in range(4):
                        if j >= 2:
                            pe.wait_ge(l_kvs, 4 * c + j - 1)
                        mm(bank[1 + j % 2][:, 0:2 * P], xs_c[:, j * P:(j + 1) * P], lWkvT[:], True, False)
                        mm(bank[1 + j % 2][:, 0:2 * P], ones_row[:], lbkv[:], False, True).then_inc(l_kv, 1)
                    pe.wait_ge(l_kvs, 4 * c + 4)
                    for j in range(4):
                        last = mm(bank[3][:, 0:P + 1], lk4[:, j, :], lv4[:, j, :], j == 0, j == 3)
                    last.then_inc(l_KV, 1)
                pe.wait_ge(l_W, 2)
                with pe.Fori(0, NCH) as c:
                    pe.wait_ge(x_ready, 4 * L_LIN + 4 + c)
                    mm(bank[0], KVm, chunk(qf, c))
                    mm(bank[1], Den, chunk(qf, c)).then_inc(l_nd, 1)
                    pe.wait_ge(l_o, c + 1)
                    mm(bank[2], lWoT[:], lo).then_inc(l_y, 1)

            pe.wait_ge(s_tab, N_TAB)
            layer_norm(L_GLA)
            gla()
            layer_norm(L_FFN0)
            ffn(L_FFN0, 0)
            layer_norm(L_SSM)
            ssm()
            layer_norm(L_FFN1)
            ffn(L_FFN1, 1)
            layer_norm(L_TOPK)
            topk_setup()
            topk()
            layer_norm(L_INT0)
            int_ffn(L_INT0, 0)
            layer_norm(L_LIN)
            linear_attention()
            layer_norm(L_INT1)
            int_ffn(L_INT1, 1)

        @block.scalar
        def _(act):
            steps = Steps(act, act_step)
            fn = nc.scalar.activation

            def layer_norm(k):
                with act.Fori(0, 2) as r:
                    for u in range(2):
                        act.wait_ge(ln_centered, 4 * k + r * 2 + u + 1)
                        fn(sq[:, u, :], bank[4 + u], ACT.Square).then_inc(ln_squared, 1)
                    for u in range(2):
                        act.wait_ge(ln_var, 4 * k + r * 2 + u + 1)
                        fn(sd[:, u, :], bank[6 + u], ACT.Sqrt, bias=eps_col).then_inc(ln_sd, 1)

            def softplus_neg_abs(dst, done, parts=P):
                steps.did(fn(dst, dst, ACT.Exp, scale=-1.0))
                fn(dst, dst, ACT.Ln, bias=one_col[0:parts]).then_inc(done, 1)

            def gla():
                with act.Fori(0, NT) as i:
                    steps.enter(i, 2)
                    act.wait_ge(g_r, i + 1)
                    fn(r_sb, bank[0][0:16, 0:P], ACT.Copy).then_inc(g_rs, 1)
                    act.wait_ge(g_zb, i + 1)
                    steps.did(fn(ab, zb, ACT.Abs))
                    softplus_neg_abs(ab, g_lnz)
                    act.wait_ge(g_vts, i + 1)
                    fn(eg, bank[7][:, 256:384], ACT.Exp, scale=-1.0).then_inc(g_eg, 1)
                    act.wait_ge(g_G, i + 1)
                    fn(eG, Gc, ACT.Exp, scale=1.0 / 16)
                    fn(emG, Gc, ACT.Exp, scale=-1.0 / 16).then_inc(g_exp, 1)
                    act.wait_ge(g_kT, i + 1)
                    fn(kIT, bank[4].rearrange("p (h d) -> p h d", h=GH), ACT.Copy).then_inc(g_kTs, 1)
                steps.leave(2, NT)
                act.wait_ge(g_out, NT + 1)
                with act.Fori(0, NCH) as c:
                    fn(o_sq, chunk(oT, c), ACT.Square).then_inc(g_osq, 1)
                    act.wait_ge(g_oms, c + 1)
                    fn(o_sd, bank[0], ACT.Sqrt, bias=eps_col).then_inc(g_osd, 1)

            def ffn(layer, k):
                act.wait_ge(s_ffn, N_FFN)
                act.wait_ge(x_ready, 4 * layer + 4)
                with act.Fori(0, NCH) as c:
                    n = 4 * k + c
                    for m in range(NM):
                        act.wait_ge(f_up, 4 * n + m + 1)
                        fn(fb[:, m, :], bank[2 * (m % 2)], ACT.Silu, scale=w1s[:, m:m + 1]).then_inc(f_silu, 1)
                    for m in range(NM):
                        act.wait_ge(f_h1, 4 * n + m + 1)
                        fn(fb[:, m, :], bank[m], ACT.Gelu, scale=h1s[:, m:m + 1]).then_inc(f_g1, 1)
                    for m in range(NM):
                        act.wait_ge(f_h2, 4 * n + m + 1)
                        fn(fa[:, m, :], bank[m], ACT.Gelu, scale=h2s[:, m:m + 1]).then_inc(f_g2, 1)

            def ssm():
                act.wait_ge(s_ssm, N_SSM)
                act.wait_ge(x_ready, 4 * L_SSM + 4)
                fn(a_exp, lam[:], ACT.Exp)
                fn(a_dt, log_dt[:], ACT.Exp).then_inc(ss_a, 1)
                act.wait_ge(ss_a, 2)
                fn(a_dec, a_neg, ACT.Exp, scale=-1.0).then_inc(ss_a, 1)

            def topk_setup():
                act.wait_ge(t_wm, 1)
                fn(Mq, bank[0][0:DCQ, 0:NH * DC], ACT.Copy).then_inc(t_wc, 1)
                for a in range(2):
                    fn(Muv[:, 4 * a:4 * a + 4, :], bank[1 + a][0:DC, :].rearrange("c (h d) -> c h d", h=4),
                       ACT.Copy).then_inc(t_wc, 1)
                with act.Fori(0, NCH) as c:
                    steps.enter(c, 4)
                    act.wait_ge(t_cq, c + 1)
                    fn(cq, bank[0][0:DCQ, :], ACT.Copy).then_inc(t_cqs, 1)
                    act.wait_ge(t_raw, c + 1)
                    steps.did(fn(k_abs, bank[1][0:2 * DR, :], ACT.Abs))
                    softplus_neg_abs(k_abs, t_kln, 2 * DR)
                    act.wait_ge(t_iq, c + 1)
                    fn(chunk(qi[:, 0, :], c), bank[2], ACT.Copy)
                    fn(chunk(qi[:, 1, :], c), bank[3], ACT.Copy)
                    fn(chunk(ki, c), bank[4], ACT.Copy).then_inc(t_iqs, 1)
                    act.wait_ge(t_qp, c + 1)
                    fn(q_abs[:, 0, :], bank[5], ACT.Abs)
                    steps.did(fn(q_abs[:, 1, :], bank[6], ACT.Abs))
                    softplus_neg_abs(q_abs, t_qln)
                    act.wait_ge(t_store_q, STORES_Q * (c + 1))
                    act.wait_ge(t_qlat, 2 * c + 1)
                    fn(qt_sb[:, 0, :], bank[7], ACT.Copy).then_inc(t_qlats, 1)
                    act.wait_ge(t_qlat, 2 * c + 2)
                    fn(qt_sb[:, 1, :], bank[0], ACT.Copy).then_inc(t_qlats, 1)
                    act.wait_ge(t_store_k, STORES_K * (c + 1))
                    act.wait_ge(t_rows, c + 1)
                    fn(rows, bank[1][:, 0:4 * ROW].rearrange("p (b r) -> p b r", b=4), ACT.Copy)\
                        .then_inc(t_rowss, 1)
                steps.leave(4, NCH)

            def index_relu(i, k):
                s0, w, h = index_units(i)[k]
                u = UNITS_BEFORE[i] + k
                act.wait_ge(i_s, u + 1)
                if u >= 4:
                    act.wait_ge(i_used, u - 3)
                fn(relu[:, u % 4, 0:w], bank[6 + u % 2][:, 0:w], ACT.Relu).then_inc(i_relu, 1)

            def queries_regroup(i, pair):
                if pair == 0:
                    act.wait_ge(q_loaded, 160 * (i + 1))
                if i >= 1:
                    act.wait_ge(a_s, NG * (i - 1) + 2 * pair + 2)
                for dst, src in ((QL, QL_in), (QG, QG_in)):
                    last = fn(dst[:, 2 * pair:2 * pair + 2, :].rearrange("r g (q h t) -> r (g q) h t", h=NH, t=QD),
                              src[:, :, 2 * GQ * pair:2 * GQ * (pair + 1)]
                              .rearrange("r h (q t) -> r q h t", t=QD), ACT.Copy)
                last.then_inc(a_q, 1)

            def rows_copy(n):
                act.wait_ge(a_gt, n + 1)
                if n >= 2:
                    act.wait_ge(a_s, n - 1)
                fn(GT[n % 2], bank[2 + n % 2][0:ROW, :], ACT.Copy).then_inc(a_gts, 1)

            def probs(n):
                act.wait_ge(a_max, n + 1)
                if n >= 2:
                    act.wait_ge(a_pt, n - 1)
                fn(Pr[n % 2], Sm[n % 2], ACT.Exp, scale=SCALE, bias=nb[:, n % 2:n % 2 + 1],
                   accum_out=ssum[:, n % 2:n % 2 + 1]).then_inc(a_exp_s, 1)

            def probs_copy(n):
                act.wait_ge(a_pt, n + 1)
                if n >= 2:
                    act.wait_ge(a_pv, n - 1)
                fn(PTl[n % 2], score_bank(n)[0:WIN, P:2 * P], ACT.Copy)
                fn(PTg[n % 2], score_bank(n)[:, 0:P], ACT.Copy).then_inc(a_pts, 1)

            def out_copy(n):
                i, g = n // NG, n % NG
                act.wait_ge(a_pv, n + 1)
                if n >= 2 * NG and g == 0:
                    act.wait_ge(a_y, i - 1)
                dst = OT[i % 2][:, :, g * GQ:(g + 1) * GQ].rearrange("c h (q t) -> c q h t", t=QD)
                fn(dst, score_bank(n)[0:DC, 2 * P:3 * P].rearrange("c (q h t) -> c q h t", h=NH, t=QD), ACT.Copy)\
                    .then_inc(a_otc, 1)

            def topk():
                act.wait_ge(t_rot, NCH + 1)
                act.wait_ge(t_store_q, STORES_Q * (NCH + 1))
                act.wait_ge(t_store_k, STORES_K * (NCH + 1))
                for s in range(SLOTS):
                    n = s - ATTN_LAG
                    if 0 <= n + 1 < GROUPS:
                        rows_copy(n + 1)
                    if 0 <= n - 2 < GROUPS:
                        out_copy(n - 2)
                    if regroups(s):
                        queries_regroup(*regroups(s))
                    for i, what, k in SLOT_STEPS[s]:
                        if what == "sum":
                            index_relu(i, k)
                    if 0 <= n - 1 < GROUPS:
                        probs_copy(n - 1)
                    if 0 <= n < GROUPS:
                        probs(n)

            def int_ffn(layer, k):
                act.wait_ge(x_ready, 4 * layer + 4)
                with act.Fori(0, NCH) as c:
                    n = 4 * k + c
                    for m in range(NM2):
                        act.wait_ge(n_up, NM2 * n + m + 1)
                        fn(ia[:, m, :], bank[2 * (m % 2)], ACT.Silu).then_inc(n_silu, 1)

            def linear_attention():
                act.wait_ge(x_ready, 4 * L_LIN + 4)
                with act.Fori(0, NCH) as c:
                    act.wait_ge(l_q, c + 1)
                    fn(lq, bank[0], ACT.Relu, bias=lbq[:]).then_inc(l_qr, 1)

            act.wait_ge(s_tab, N_TAB)
            layer_norm(L_GLA)
            gla()
            layer_norm(L_FFN0)
            ffn(L_FFN0, 0)
            layer_norm(L_SSM)
            ssm()
            layer_norm(L_FFN1)
            ffn(L_FFN1, 1)
            layer_norm(L_TOPK)
            topk_setup()
            topk()
            layer_norm(L_INT0)
            int_ffn(L_INT0, 0)
            layer_norm(L_LIN)
            linear_attention()
            layer_norm(L_INT1)
            int_ffn(L_INT1, 1)

        @block.vector
        def _(dve):
            v = nc.vector
            steps = Steps(dve, dve_step)

            def layer_norm(k):
                with dve.Fori(0, 2) as r:
                    steps.enter(r, 2)
                    for u in range(2):
                        dve.wait_ge(ln_sd, 4 * k + r * 2 + u + 1)
                        steps.did(v.reciprocal(sd[:, u, :], sd[:, u, :]))
                        v.tensor_tensor(chunk(xn, r * 2 + u), bank[4 + u], sd[:, u, :], ALU.mult)\
                            .then_inc(ln_applied, 1)
                steps.leave(2, 2)

            def heads(a, n=GH):
                return a.rearrange("p (h t) -> p h t", h=n)

            def gla():
                dve.wait_ge(s_gla, N_GLA + 32)
                v.memset(S, 0.0).then_inc(g_S, 1)
                with dve.Fori(0, NT) as i:
                    steps.enter(i, 5)
                    dve.wait_ge(ln_applied, LN0 + 4 * L_GLA + 4)
                    dve.wait_ge(g_vg, i + 1)
                    v.tensor_copy(xs_t, xn[:, bass.ds(i * P, P)]).then_inc(g_xs, 1)
                    dve.wait_ge(g_zqk, i + 1)
                    v.tensor_tensor(zb, heads(bank[1]), bgk2[:].unsqueeze(2).to_broadcast([P, GH, P]), ALU.add)\
                        .then_inc(g_zb, 1)
                    dve.wait_ge(g_vg, i + 2)
                    v.tensor_copy(vt, bank[7][:, 384:512]).then_inc(g_vts, 1)
                    dve.wait_ge(g_lnz, i + 1)
                    dve.wait_ge(g_zb, i + 1)
                    steps.did(v.scalar_tensor_tensor(zb, zb, 0.0, ab, ALU.min, ALU.subtract))
                    v.tensor_tensor_scan(Gc.rearrange("p h t -> p (h t)"), scan_keep[:],
                                         zb.rearrange("p h t -> p (h t)"), 0.0, ALU.mult, ALU.add)\
                        .then_inc(g_G, 1)
                    dve.wait_ge(g_exp, i + 1)
                    v.scalar_tensor_tensor(qg, heads(bank[2]), GDK ** -0.5, eG, ALU.mult, ALU.mult)
                    v.tensor_tensor(kI, heads(bank[3]), emG, ALU.mult).then_inc(g_qk, 1)
                    dve.wait_ge(g_eg, i + 1)
                    steps.did(v.tensor_scalar(egr, eg, 1.0, None, ALU.add))
                    steps.did(v.reciprocal(egr, egr))
                    v.tensor_tensor(gate[:, bass.ds(i * P, P)], bank[7][:, 256:384], egr, ALU.mult)
                    dve.wait_ge(g_A, i + 1)
                    v.tensor_tensor(AT, heads(bank[5]), gla_mask[:].unsqueeze(1).to_broadcast([P, GH, P]),
                                    ALU.mult).then_inc(g_AT, 1)
                    for half in range(2):
                        dve.wait_ge(g_dS, 2 * i + half + 1)
                        dve.wait_ge(g_S, 2 * i + half + 1)
                        steps.did(v.tensor_tensor(S_in, S, bank[7][:, half * P:half * P + P], ALU.add))
                        end = (half + 1) * GCHUNK - 1
                        v.tensor_tensor(heads(S), heads(S_in), eG[:, :, end:end + 1].to_broadcast([P, GH, GDV]),
                                        ALU.mult).then_inc(g_S, 1)
                    dve.wait_ge(g_o, i + 1)
                    v.tensor_copy(oT[:, bass.ds(i * P, P)], bank[6][:, 0:P]).then_inc(g_out, 1)
                steps.leave(5, NT)
                with dve.Fori(0, NCH) as c:
                    steps.enter(c, 2)
                    dve.wait_ge(g_osd, c + 1)
                    steps.did(v.reciprocal(o_sd, o_sd))
                    steps.did(v.tensor_tensor(chunk(oT, c), chunk(oT, c), o_sd, ALU.mult))
                    v.scalar_tensor_tensor(chunk(oT, c), chunk(oT, c), gnw[:], chunk(gate, c), ALU.mult, ALU.mult)\
                        .then_inc(g_on, 1)
                    dve.wait_ge(g_y, c + 1)
                    v.tensor_tensor(chunk(x, c), chunk(x, c), bank[1], ALU.add).then_inc(x_ready, 1)
                steps.leave(2, NCH)

            def ffn(layer, k):
                dve.wait_ge(s_ffn, N_FFN)
                with dve.Fori(0, NCH) as c:
                    n = 4 * k + c
                    for m in range(NM):
                        dve.wait_ge(f_silu, 4 * n + m + 1)
                        v.scalar_tensor_tensor(fa[:, m, :], bank[2 * (m % 2) + 1], w2s[:, m:m + 1], fb[:, m, :],
                                               ALU.mult, ALU.mult).then_inc(f_gated, 1)
                    dve.wait_ge(f_down, n + 1)
                    v.scalar_tensor_tensor(chunk(x, c), bank[0], w3s[:], chunk(x, c), ALU.mult, ALU.add)\
                        .then_inc(x_ready, 1)

            def ssm():
                dve.wait_ge(s_ssm, N_SSM)
                dve.wait_ge(ss_a, 1)
                v.tensor_tensor(a_neg, a_exp, a_dt, ALU.mult).then_inc(ss_a, 1)
                steps.did(v.memset(keep, 1.0))
                dve.wait_ge(ss_a, 3)
                steps.did(v.tensor_scalar(keep, keep, a_dec, None, ALU.mult))
                steps.did(v.memset(carry, 0.0))
                steps.leave(3, 1)
                with dve.Fori(0, NCH) as c:
                    steps.enter(c, 2)
                    dve.wait_ge(ss_u, c + 1)
                    v.tensor_tensor_scan(chunk(states, c), keep, bank[0][0:64, :], carry, ALU.mult, ALU.add)\
                        .then_inc(ss_x, 1)
                    dve.wait_ge(ss_x, c + 1)
                    steps.did(v.tensor_copy(carry, states[:, bass.ds(c * C + C - 1, 1)]))
                    dve.wait_ge(ln_applied, LN0 + 4 * L_SSM + 4)
                    steps.did(v.scalar_tensor_tensor(chunk(x, c), chunk(xn, c), sD[:], chunk(x, c),
                                                     ALU.mult, ALU.add))
                    dve.wait_ge(ss_y, c + 1)
                    v.tensor_tensor(chunk(x, c), chunk(x, c), bank[1], ALU.add).then_inc(x_ready, 1)
                steps.leave(2, NCH)

            def topk_setup():
                with dve.Fori(0, NCH) as c:
                    steps.enter(c, 13)
                    dve.wait_ge(t_kln, c + 1)
                    v.scalar_tensor_tensor(raw[0:2 * DR, :], bank[1][0:2 * DR, :], 0.0, k_abs, ALU.max, ALU.add)
                    v.tensor_copy(raw[2 * DR:ROW, :], bank[1][2 * DR:ROW, :]).then_inc(t_rawd, 1)
                    dve.wait_ge(t_rawd, c + 1)
                    dve.wait_ge(t_tab, 80 * (c + 1))
                    v.tensor_tensor(chunk(KL[0:2 * DR, :], c), raw[0:2 * DR, :], key_rope, ALU.mult)
                    v.tensor_copy(chunk(KL[2 * DR:ROW, :], c), raw[2 * DR:ROW, :])
                    dve.wait_ge(t_qln, c + 1)
                    steps.did(v.scalar_tensor_tensor(mu[:, 0, :], bank[5], 0.0, q_abs[:, 0, :], ALU.max, ALU.add))
                    steps.did(v.scalar_tensor_tensor(mu[:, 1, :], bank[6], 0.0, q_abs[:, 1, :], ALU.max, ALU.add))
                    dve.wait_ge(t_store_q, STORES_Q * (c + 1))
                    for k in range(2):
                        cos, sin = rope_tab[:, 2 * k, :], rope_tab[:, 2 * k + 1, :]
                        for b, (f0, f1, op) in enumerate(((cos, sin, ALU.subtract), (sin, cos, ALU.add))):
                            steps.did(v.tensor_tensor(rot_t[:, 0, :], mu[:, 0, :], f0, ALU.mult))
                            steps.did(v.tensor_tensor(rot_t[:, 1, :], mu[:, 1, :], f1, ALU.mult))
                            if k == 1 and b == 1:
                                dve.wait_ge(t_iqs, c + 1)
                                dve.wait_ge(t_qlats, 2 * c + 2)
                                dve.wait_ge(t_rowss, c + 1)
                            last = v.tensor_tensor(rot[:, 2 * k + b, :], rot_t[:, 0, :], rot_t[:, 1, :], op)
                            if k == 1 and b == 1:
                                last.then_inc(t_rot, 1)
                                dve.wait_ge(t_rot, c + 2)
                            else:
                                steps.did(last)
                steps.leave(13, NCH)

            def pick(i, what, k):
                W = index_width(i)
                sc = I_s[:, i % 2, 0:W]
                best = top8[:, 8 * (k % N_ROUNDS):8 * (k % N_ROUNDS) + 8]
                if what == "sum":
                    s0, w, h = index_units(i)[k]
                    u = UNITS_BEFORE[i] + k
                    dve.wait_ge(i_relu, u + 1)
                    r_, s_ = relu[:, u % 4, 0:w], sc[:, s0:s0 + w]
                    if h == 0:
                        ins = v.tensor_scalar(s_, r_, iw[:, 0:1], None, ALU.mult)
                    else:
                        dve.wait_ge(i_used, u)
                        ins = v.scalar_tensor_tensor(s_, r_, iw[:, h:h + 1], s_, ALU.mult, ALU.add)
                    ins.then_inc(i_used, 1)
                elif what == "mask":
                    dve.wait_ge(i_used, UNITS_BEFORE[i + 1])
                    if i == 0:
                        steps.did(v.tensor_tensor(sc, sc, index_mask_first[:], ALU.add))
                    else:
                        steps.did(v.tensor_tensor(sc[:, W - P:W], sc[:, W - P:W], index_mask[:], ALU.add))
                elif what == "max":
                    steps.did(v.max(best, sc))
                elif what == "index":
                    steps.did(v.max_index(idx_u[:, 8 * k:8 * k + 8], best, sc))
                elif what == "drop":
                    steps.did(v.match_replace(sc, best, sc, TAKEN))
                elif what == "turn":
                    if i >= 1:
                        dve.wait_ge(i_perm, i)
                    v.tensor_copy(idx_f, idx_u[:]).then_inc(i_done, 1)
                    dve.wait_ge(i_done, i + 1)
                else:
                    dve.wait_ge(i_perm, i + 1)
                    v.tensor_copy(idx_T[:, i, :], bank[5][:, 256:256 + P // 4]).then_inc(i_idx, 1)

            def rows_rotate(n):
                i, g = n // NG, n % NG
                dve.wait_ge(gathered[i % 2][g], 64 * (i // 2 + 1))
                if n >= 2:
                    dve.wait_ge(a_gt, n - 1)
                v.tensor_tensor(GR[n % 2], G[i % 2][:, 4 * g:4 * g + 4, :],
                                rank_rope[:].unsqueeze(1).to_broadcast([P, 4, ROW]), ALU.mult).then_inc(a_rot, 1)

            def row_max(n):
                i, g = n // NG, n % NG
                b = n % 2
                dve.wait_ge(a_s, n + 1)
                if n >= 2:
                    dve.wait_ge(a_exp_s, n - 1)
                mask = score_mask_first if i * P + g * GQ < LW else score_mask
                steps.did(v.tensor_tensor_reduce(out=Sm[b], in0=score_bank(n)[:, 0:KEYS], in1=mask[:], scale=1.0,
                                                 scalar=LOWEST, op0=ALU.add, op1=ALU.max,
                                                 accum_out=mx[:, b:b + 1]))
                v.tensor_scalar(nb[:, b:b + 1], mx[:, b:b + 1], -SCALE, None, ALU.mult).then_inc(a_max, 1)

            def probs_norm(n):
                b = n % 2
                dve.wait_ge(a_exp_s, n + 1)
                steps.did(v.reciprocal(rsum[:, b:b + 1], ssum[:, b:b + 1]))
                v.tensor_scalar(Pr[b], Pr[b], rsum[:, b:b + 1], None, ALU.mult).then_inc(a_pn, 1)

            def add_tile(i):
                dve.wait_ge(a_y, i + 1)
                xt = x[:, i * P:(i + 1) * P]
                v.tensor_tensor(xt, xt, bank[5][:, 128:256], ALU.add).then_inc(a_x, 1)
                if i % 4 == 3:
                    dve.wait_ge(a_x, i + 1)
                    v.engine_nop().then_inc(x_ready, 1)

            def topk():
                dve.wait_ge(s_tk, N_TK)
                dve.wait_ge(t_store_q, STORES_Q * (NCH + 1))
                dve.wait_ge(t_store_k, STORES_K * (NCH + 1))
                for s in range(SLOTS):
                    n = s - ATTN_LAG
                    if 0 <= n + 2 < GROUPS:
                        rows_rotate(n + 2)
                    if 0 <= n - 1 < GROUPS:
                        probs_norm(n - 1)
                    if 0 <= n - 3 < GROUPS and (n - 3) % NG == NG - 1:
                        add_tile((n - 3) // NG)
                    todo = list(SLOT_STEPS[s])
                    while todo and todo[0][1] != "sum":
                        pick(*todo.pop(0))
                    if 0 <= n < GROUPS:
                        row_max(n)
                    for step in todo:
                        pick(*step)
                steps.leave(steps.k, 1)

            def int_weights():
                dve.wait_ge(s_int, 48)
                for dst, src in ((gate_w, gate_i), (up_w, up_i), (down_w, down_i)):
                    v.tensor_scalar(dst[:], src[:], float(np.float32(1.0 / 127.0)), None, ALU.mult)\
                        .then_inc(n_w, 1)

            def int_ffn(layer, k):
                with dve.Fori(0, NCH) as c:
                    n = 4 * k + c
                    for m in range(NM2):
                        dve.wait_ge(n_silu, NM2 * n + m + 1)
                        v.tensor_tensor(ia[:, m, :], ia[:, m, :], bank[2 * (m % 2) + 1], ALU.mult)\
                            .then_inc(n_gated, 1)
                    dve.wait_ge(n_down, n + 1)
                    v.tensor_tensor(chunk(x, c), chunk(x, c), bank[0], ALU.add).then_inc(x_ready, 1)

            def linear_attention():
                dve.wait_ge(s_lin, N_LIN)
                dve.wait_ge(ln_applied, LN0 + 4 * L_LIN + 4)
                steps.did(v.memset(KV, 0.0))
                steps.did(v.memset(lv4, 1.0))
                steps.leave(2, 1)
                dve.wait_ge(l_in, 16)
                with dve.Fori(0, NCH) as c:
                    v.tensor_copy(xs_c, chunk(xn, c)).then_inc(l_xs, 1)
                    dve.wait_ge(l_qr, c + 1)
                    v.tensor_tensor(chunk(qf, c), lq, chunk(decay_row, c), ALU.mult)
                    for j in range(4):
                        dve.wait_ge(l_kv, 4 * c + j + 1)
                        kv = bank[1 + j % 2]
                        v.tensor_scalar(lk4[:, j, :], kv[:, 0:P], 0.0, decay_col[:, bass.ds(4 * c + j, 1)],
                                        ALU.max, ALU.mult)
                        v.tensor_copy(lv4[:, j, 0:P], kv[:, P:2 * P]).then_inc(l_kvs, 1)
                    dve.wait_ge(l_KV, c + 1)
                    v.tensor_tensor(KV, KV, bank[3][:, 0:P + 1], ALU.add).then_inc(l_KVa, 1)
                    dve.wait_ge(l_KVa, c + 2)
                v.tensor_tensor(KVm, KV[:, 0:P], same_head[:], ALU.mult).then_inc(l_W, 1)
                v.tensor_scalar(Den, same_head[:], KV[:, P:P + 1], None, ALU.mult).then_inc(l_W, 1)
                with dve.Fori(0, NCH) as c:
                    steps.enter(c, 2)
                    dve.wait_ge(l_nd, c + 1)
                    steps.did(v.tensor_scalar(den, bank[1], EPS_LIN, None, ALU.add))
                    steps.did(v.reciprocal(rden, den))
                    v.tensor_tensor(lo, bank[0], rden, ALU.mult).then_inc(l_o, 1)
                    dve.wait_ge(l_y, c + 1)
                    v.scalar_tensor_tensor(chunk(x, c), bank[2], lbo[:], chunk(x, c), ALU.add, ALU.add)\
                        .then_inc(x_ready, 1)
                steps.leave(2, NCH)

            v.engine_nop().then_inc(ln_applied, LN0)
            for s, free in ((g_out, 1), (g_vg, 1), (t_rot, 1), (t_store_k, STORES_K), (t_store_q, STORES_Q),
                            (l_KVa, 1)):
                v.engine_nop().then_inc(s, free)
            dve.wait_ge(x_loaded, 16)
            v.engine_nop().then_inc(x_ready, 4)
            int_weights()
            layer_norm(L_GLA)
            gla()
            layer_norm(L_FFN0)
            ffn(L_FFN0, 0)
            layer_norm(L_SSM)
            ssm()
            layer_norm(L_FFN1)
            ffn(L_FFN1, 1)
            layer_norm(L_TOPK)
            topk_setup()
            topk()
            layer_norm(L_INT0)
            int_ffn(L_INT0, 0)
            layer_norm(L_LIN)
            linear_attention()
            layer_norm(L_INT1)
            int_ffn(L_INT1, 1)


def lay_out(i):
    A, B, F, K, L, N = "L0_attn_a_", "L0_attn_b_", "L0_ffn_", "L1_attn_a_", "L1_attn_b_", "L1_ffn_"

    def fold(w):
        return w.reshape(-1, P, w.shape[1]).transpose(1, 0, 2)

    def col(w):
        return w.reshape(-1, P).T

    d = {"xT": i[A + "x"][0].T}
    for n in ("Wq", "Wk", "Wv", "Wg", "Wo"):
        d["g" + n] = i[A + n]
    d["Wgk1"], d["Wgk2"], d["bgk2"] = i[A + "Wgk1"], i[A + "Wgk2"], col(i[A + "bgk2"])
    d["gnw"] = np.tile(i[A + "gnw"], GH)[:, None]
    d["lam"] = i[B + "Lambda"][:, None]
    d["log_dt"] = np.tile(i[B + "log_dt"], 64)[:, None]
    d["sBT"], d["sCT"], d["sD"] = i[B + "B"].T, i[B + "C"].T, i[B + "D"][:, None]
    d["w1"], d["w2"] = i[F + "w1_w"].T, i[F + "w2_w"].T
    for n in ("h1", "h2", "w3"):
        d[n] = fold(i[F + n + "_w"].T)
    for n in ("w1", "w2", "h1", "h2", "w3"):
        d[n + "s"] = col(i[F + n + "_s"])
    half = DR // 2
    kr = i[K + "W_kr"]
    d["Wkeys"] = np.concatenate([kr, kr[:, half:], kr[:, :half], i[K + "W_dkv"]], axis=1)
    d["Wdq"] = i[K + "W_dq"]
    qr = i[K + "W_qr"].reshape(DCQ, NH, DR)
    d["Wqr1"], d["Wqr2"] = qr[:, :, :half].reshape(DCQ, P), qr[:, :, half:].reshape(DCQ, P)
    for n, w in (("WuqT", "W_uq"), ("WukT", "W_uk"), ("WuvT", "W_uv")):
        d[n] = i[K + w].reshape(-1, NH, DH).transpose(2, 1, 0)
    d["Wout"] = i[K + "W_out"].reshape(NH, DH, P).transpose(1, 0, 2)
    d["Wiq"] = i[K + "idx_wq"]
    d["Wik"] = np.concatenate([i[K + "idx_wk"]] * 2, axis=1)
    d["iw"] = np.tile(i[K + "idx_w"][None, :], (P, 1))
    d["lWqT"], d["lWoT"] = i[L + "W_q"].T, i[L + "W_o"].T
    d["lWkvT"] = np.concatenate([i[L + "W_k"].T, i[L + "W_v"].T], axis=1)
    d["lbkv"] = np.concatenate([i[L + "b_k"], i[L + "b_v"]])[None, :]
    d["lbq"], d["lbo"] = i[L + "b_q"][:, None], i[L + "b_o"][:, None]
    d["gate_i"], d["up_i"] = i[N + "w_gate"].T, i[N + "w_up"].T
    d["down_i"] = fold(i[N + "w_down"].T).reshape(P, HID2)
    return d


def kernel(**inputs):
    import concourse.bacc as bacc
    from concourse.bass_utils import run_bass_kernel_spmd

    nc = bacc.Bacc("TRN2", target_bir_lowering=False, num_devices=1)
    arrays = {n: np.ascontiguousarray(a) for n, a in
              {**lay_out({n: np.asarray(a) for n, a in inputs.items()}), **shape_tables()}.items()}
    aps = {n: nc.dram_tensor("in_" + n, a.shape, mybir.dt.from_np(a.dtype), kind="ExternalInput").ap()
           for n, a in arrays.items()}
    out = nc.dram_tensor("out", (P, T), F32, kind="ExternalOutput").ap()
    hybrid_kernel(nc, aps, out)
    r = run_bass_kernel_spmd(nc, [{"in_" + n: a for n, a in arrays.items()}], core_ids=[0])
    return np.ascontiguousarray(r.results[0]["out"].T)[None]
```

```python
from contextlib import ExitStack

import numpy as np

import concourse.bass as bass
from concourse import mybir

F32 = mybir.dt.float32
F32R = mybir.dt.float32r
I32 = mybir.dt.int32
U32 = mybir.dt.uint32
ALU = mybir.AluOpType
ACT = mybir.ActivationFunctionType

P = 128
T = 2048
C = 512
NCH = T // C
NT = T // P
EPS_LN = 1e-5
LN0 = 2
STORES_K, STORES_L, STORES_Q = 16, 32, 32
EPS_LIN = 1e-6
GH, GDK, GDV, GCHUNK = 4, 128, 32, 64
NH, DR, DC, DCQ, DH = 8, 32, 32, 64, 64
NIH = 4
KTOP, LW = 96, 64
JG = KTOP - LW
EARLY = 2
ROW = 2 * DR + DC
SCALE = (DH + DR) ** -0.5
GQ = 16
NG = P // GQ
FIXED = LW
WIN = LW + GQ
QD = P // JG
KEYS = P + WIN
NEG = -1e30
LOWEST = -3e38
TAKEN = -3.3e38
HID = 512
NM = HID // P
HID2 = 384
NM2 = HID2 // P
LH, LDK = 16, 8
INT_SCALE = float(np.float32(1.0 / 127.0))


def shape_tables():
    f32 = np.float32
    t = {}
    t["ident"] = np.eye(P, dtype=f32)
    t["center"] = (np.eye(P) - 1.0 / P).astype(f32)
    t["mean_col"] = np.full((P, 1), 1.0 / P, f32)
    t["ones"] = np.ones((P, P), f32)
    same = np.arange(P)[:, None] // GDV == np.arange(P)[None, :] // GDV
    t["mean_head"] = (same / GDV).astype(f32)
    t["head_cols"] = (np.arange(P)[:, None] // LDK == np.arange(LH)[None, :]).astype(f32)
    t["same_head"] = (np.arange(P)[:, None] // LDK == np.arange(P)[None, :] // LDK).astype(f32)
    j, i = np.arange(P)[:, None], np.arange(P)[None, :]
    t["gla_mask"] = ((j <= i) & (j // GCHUNK == i // GCHUNK)).astype(f32)
    t["scan_keep"] = np.tile((np.arange(C) % GCHUNK != 0).astype(f32), (P, 1))
    cols = np.zeros((P, 4), f32)
    cols[:, 0] = EPS_LN
    cols[:, 1] = 1.0
    t["cols"] = cols
    half = DR // 2
    theta = 1.0 / 10000.0 ** (2.0 * np.arange(half) / DR)
    pos = np.arange(T)
    q_g = theta[:, None] * pos[None, :]
    q_l = theta[:, None] * (pos + np.maximum(pos - (LW - 1), 0))[None, :]
    for name, a in (("qg", q_g), ("ql", q_l)):
        t["cos_" + name] = np.tile(np.cos(a), (NH, 1)).astype(f32)
        t["sin_" + name] = np.tile(np.sin(a), (NH, 1)).astype(f32)
    c, s = np.cos(q_g), np.sin(q_g)
    t["key_rope"] = np.concatenate([c, c, -s, s]).astype(f32)
    a = (LW + np.arange(JG))[:, None] * theta[None, :]
    row = np.concatenate([np.cos(a), np.cos(a), -np.sin(a), np.sin(a), np.ones((JG, DC))], axis=1)
    t["rank_rope"] = np.tile(row, (P // JG, 1)).astype(f32)
    r = np.arange(P)
    tq, q = r % QD, r // (NH * QD) * QD + r % QD
    own = (np.arange(P) // JG)[None, :] == tq[:, None]
    x = np.arange(WIN)[None, :]
    near = (x >= 1 + q[:, None]) & (x <= LW + q[:, None])
    first = np.broadcast_to(x < LW, (P, WIN))
    t["score_mask"] = np.where(np.concatenate([own, near], 1), 0, NEG).astype(f32)
    t["score_mask_first"] = np.where(np.concatenate([own, first], 1), 0, NEG).astype(f32)
    p, s = np.arange(P)[:, None], np.arange(KTOP)[None, :]
    past, local = s <= p - LW, (s <= p) & (s > p - LW)
    local = local | ((p < LW) & (s < LW))
    t["index_mask_first"] = np.where(local, LOWEST, np.where(past, 0, NEG)).astype(f32)
    t["index_mask"] = np.where(np.arange(P)[None, :] <= p, 0, LOWEST).astype(f32)
    dec = np.exp(-np.arange(T, dtype=f32) / f32(T)).astype(f32)
    t["decay_row"] = np.broadcast_to(dec, (P, T))
    t["decay_col"] = dec.reshape(NT, P).T
    t["ones_row"] = np.ones((1, P), f32)
    return t


class Steps:

    def __init__(self, eng, sem):
        self.eng, self.sem, self.base, self.loop, self.k = eng, sem, 0, 0, 0

    def enter(self, i, per):
        self.loop, self.k = i * per, 0

    def leave(self, per, times):
        assert self.k == per, (self.k, per)
        self.base, self.loop, self.k = self.base + per * times, 0, 0

    def did(self, ins):
        self.k += 1
        ins.then_inc(self.sem, 1)
        self.eng.wait_ge(self.sem, self.base + self.loop + self.k)


def hybrid_kernel(nc, d, out):
    with ExitStack() as ctx:
        def sem(name):
            return ctx.enter_context(nc.semaphore(name))

        def sb(name, shape, dt=F32):
            return ctx.enter_context(nc.sbuf_tensor(name, shape, dt))

        def dram(name, shape):
            return nc.dram_tensor(name, shape, F32, kind="Internal").ap()

        bank2 = [ctx.enter_context(nc.psum_tensor(f"bank{2 * i}_{2 * i + 1}", [P, 2 * C], F32)) for i in range(4)]
        bank = [bank2[i // 2][:, (i % 2) * C:(i % 2) * C + C] for i in range(8)]

        x = sb("x", [P, T])
        xn = sb("xn", [P, T])
        LOAD = {}

        def load(name, dt=F32):
            LOAD[name] = sb(name, list(d[name].shape), dt)
            return LOAD[name]

        ident, center, mean_col = (load(n) for n in ("ident", "center", "mean_col"))
        ones, mean_head = load("ones"), load("mean_head")
        head_cols = load("head_cols")
        same_head, gla_mask, scan_keep, cols = load("same_head"), load("gla_mask"), load("scan_keep"), load("cols")
        rank_rope, ones_row = load("rank_rope"), load("ones_row")
        score_mask, score_mask_first = load("score_mask"), load("score_mask_first")
        index_mask, index_mask_first, decay_col = load("index_mask"), load("index_mask_first"), load("decay_col")
        eps_col, one_col = cols[:, 0:1], cols[:, 1:2]
        gWv, gWg, gWo, Wgk1 = (load(n) for n in ("gWv", "gWg", "gWo", "Wgk1"))
        bgk2, gnw = load("bgk2"), load("gnw")
        lam, log_dt, sBT, sCT, sD = (load(n) for n in ("lam", "log_dt", "sBT", "sCT", "sD"))
        early_offset = (nc.sbuf_base + 31) // 32 * 32
        h1, h2, w1, w2, w3, Wgk2 = (load(n) for n in ("h1", "h2", "w1", "w2", "w3", "Wgk2"))
        assert nc.sbuf_base - early_offset == 4 * 3 * T
        w1s, w2s, h1s, h2s, w3s = (load(n) for n in ("w1s", "w2s", "h1s", "h2s", "w3s"))
        Wkeys, Wdq, Wqr1, Wqr2 = (load(n) for n in ("Wkeys", "Wdq", "Wqr1", "Wqr2"))
        Wiq, Wik, iw = (load(n) for n in ("Wiq", "Wik", "iw"))
        lWqT, lWkvT, lWoT, lbq, lbkv, lbo = (load(n) for n in ("lWqT", "lWkvT", "lWoT", "lbq", "lbkv", "lbo"))
        gate_w, up_w, down_w = (sb(n, [P, HID2], F32R) for n in ("gate_w", "up_w", "down_w"))

        ARENA_0, ARENA_LO, ARENA_HI = 3 * T, 25664, 5760
        sq, sd_col, inv_diag = sb("ln_sq", [P, 2, C]), sb("ln_sd", [P, 2, C // P]), sb("ln_diag", [P, 2, C])
        arena_offset = nc.sbuf_base
        arenas = [sb("arena_0", [P, ARENA_0]), sb("arena_lo", [P, ARENA_LO - ARENA_0]), sb("arena_hi", [P, ARENA_HI])]
        assert nc.sbuf_base - arena_offset == 4 * (ARENA_LO + ARENA_HI)
        at = [0]

        def part(*shape, parts=P):
            n = int(np.prod(shape))
            k = (at[0] >= ARENA_0) + (at[0] >= ARENA_LO)
            a0 = at[0] - (0, ARENA_0, ARENA_LO)[k]
            assert a0 + n <= (ARENA_0, ARENA_LO - ARENA_0, ARENA_HI)[k], (at[0], n)
            v = arenas[k][0:parts, a0:a0 + n]
            at[0] += n
            if len(shape) == 2:
                v = v.rearrange("p (a b) -> p a b", a=shape[0])
            return v

        def over(name, shape, dt=F32, parts=P):
            v = nc.alloc_sbuf_tensor_at(name, [parts, *shape], dt, offset=arena_offset + 4 * at[0])
            at[0] += int(np.prod(shape))
            assert at[0] <= ARENA_LO + ARENA_HI
            return v[:]

        LAYER = at[0]
        oT = part(T)
        eG = [part(GH, P) for _ in range(2)]
        qg = [part(GH, P) for _ in range(2)]
        emG, kI, kIT, AT = (part(GH, P) for _ in range(4))
        at[0] = ARENA_0
        gWq, gWk = part(GH * GDK), part(GH * GDK)
        xs_t, r_sb = part(P), part(C, parts=16)
        neg_bgk2 = part(GH)
        G_all, relu_z = part(GH, T), part(GH, T)
        vt = [part(P) for _ in range(2)]
        S, S_in = [part(P) for _ in range(2)], part(P)
        gate = relu_z[:, 0, :]
        o_sq, o_sd = (relu_z[:, k, 0:2 * C].rearrange("p (a b) -> p a b", a=2) for k in (1, 2))
        at[0] = ARENA_LO
        w1r, w2r, w3r = over("w1r", [HID], F32R), over("w2r", [HID], F32R), over("w3r", [NM, P], F32R)
        h1r, h2r = over("h1r", [NM, HID], F32R), over("h2r", [NM, HID], F32R)
        at[0] = LAYER
        x_hi, x_lo = (over("ffn_x_" + n, [2, C], F32R) for n in ("hi", "lo"))
        a_hi, a_lo = (over("ffn_a_" + n, [2 * NM, C], F32R) for n in ("hi", "lo"))
        b_hi, b_lo = (over("ffn_b_" + n, [2 * NM, C], F32R) for n in ("hi", "lo"))
        f_silu_sb, f_full = over("ffn_silu_out", [2, C]), over("ffn_full", [4, C])
        a_exp, a_dt, a_neg, a_dec, carry = (over("ssm_" + n, [8], parts=64)[:, 0:1] for n in
                                            ("exp_lam", "dt", "neg_log", "decay", "carry"))
        keep, states = over("ssm_keep", [C], parts=64), over("ssm_state_sb", [T], parts=64)
        at[0] = LAYER
        q_split = [over("index_q0", [T], F32R), over("index_q1", [T], F32R)]
        k_hi = over("index_k_hi", [T], F32R)
        q_split += [nc.alloc_sbuf_tensor_at(f"index_q{2 + k}", [P, T], F32R, offset=early_offset + 4 * k * T)[:]
                    for k in range(2)]
        k_lo = nc.alloc_sbuf_tensor_at("index_k_lo", [P, T], F32R, offset=early_offset + 4 * 2 * T)[:]
        KL = part(T, parts=ROW)
        Muv = part(NH, P, parts=DC)
        TOPK = at[0]
        WuqT, WukT = part(NH, DCQ, parts=DH), part(NH, DC, parts=DH)
        WuvT, Wout = part(NH, DC, parts=DH), part(NH, P, parts=DH)
        Mq = part(NH * DC, parts=DCQ)
        ROPE = at[0]
        rope_tab = [part(4, C) for _ in range(NCH)]
        cq, raw = [part(C, parts=DCQ) for _ in range(2)], [part(C, parts=ROW) for _ in range(2)]
        k_abs = part(C, parts=2 * DR)
        q_abs, mu = part(2, C), [part(2, C) for _ in range(2)]
        at[0] = TOPK
        rot_t, rot_tg = part(2, C), part(2, C)
        at[0] = ARENA_LO
        rot, qt_sb, key_rope, rows = part(4, C), part(2, C), part(T, parts=2 * DR), part(4, ROW)
        at[0] = TOPK
        relu, PTg = part(4, C), [part(P) for _ in range(2)]
        at[0] = ROPE
        G = [part(P // QD, ROW) for _ in range(2)]
        assert P // QD * ROW <= EARLY * 4 * C and 2 * (P // QD) * ROW <= (EARLY + 1) * 4 * C
        QL_in, QG_in = part(NH, P, parts=ROW), part(NH, P, parts=ROW)
        top8, idx_f, I_s = part(JG), part(JG), part(2, T)
        QL = part(NG, P, parts=ROW)
        Vloc = [part(NG, DC, parts=WIN) for _ in range(2)]
        PTl = [part(P, parts=WIN) for _ in range(2)]
        QG = part(NG, P, parts=ROW)
        GR = [part(4, ROW) for _ in range(2)]
        GT = [part(C, parts=ROW) for _ in range(2)]
        Sm = [part(KEYS) for _ in range(2)]
        Pr = [part(KEYS) for _ in range(2)]
        mx, nb, ssum, rsum = (part(2) for _ in range(4))
        OT = [part(NH, P, parts=DC) for _ in range(2)]
        early_I_s, early_relu = sq[:, :, 0:EARLY * P], inv_diag[:].rearrange("p u (b w) -> p (u b) w", w=EARLY * P)
        early_top8, early_idx_f = sq[:, 0, C - JG:C], sq[:, 1, C - JG:C]
        at[0] = ARENA_LO
        decay_row = part(T)
        at[0] = ARENA_0
        qf, lq = part(T), part(2, C)
        lk, lv = [part(4, P) for _ in range(2)], [part(4, P + 1) for _ in range(2)]
        k_sum, head_sums, KVm = part(1), part(LH), part(P)
        den, rden = part(2, 4 * LH), part(2, 4 * LH)
        num, lo = part(2, C), part(2, C)
        rden_cols = [part(4 * LH, LDK) for _ in range(2)]
        gate_i, up_i, down_i = (sb(n, [P, HID2], I32) for n in ("gate_i", "up_i", "down_i"))
        idx_u = sb("idx_u", [P, JG], U32)
        idx_T = sb("idx_T", [P, NT, P // 4], U32)

        key_table = dram("key_table", (T, ROW))
        q_rot = {n: dram("q_" + n, (2, P, T)) for n in ("l", "g")}
        q_lat = dram("q_lat", (NH * DC, T))

        (s_tab, s_gla, s_ssm, s_ffn, s_tk, s_lin, s_int) = (
            sem("loaded_" + n) for n in ("tables", "gla", "ssm", "ffn", "topk", "lin", "int"))
        x_loaded, x_ready = sem("x_loaded"), sem("x_ready")
        ln_centered, ln_squared, ln_var, ln_sd, ln_diag, ln_inv, ln_applied = (
            sem("ln_" + n) for n in ("centered", "squared", "var", "sd", "diagonal", "inverse_spread", "applied"))
        dve_step, act_step, pool_step = sem("dve_step"), sem("act_step"), sem("pool_step")

        LOADS = {
            s_tab: ["ident", "center", "mean_col", "ones", "cols"],
            s_gla: ["gWv", "gWg", "gWo", "Wgk1", "Wgk2", "bgk2", "gnw", "mean_head", "gla_mask", "scan_keep"],
            s_ffn: ["w1", "w2", "h1", "h2", "w3", "w1s", "w2s", "h1s", "h2s", "w3s"],
            s_ssm: ["lam", "log_dt", "sBT", "sCT", "sD"],
            s_tk: ["Wkeys", "Wdq", "Wqr1", "Wqr2", "Wiq", "Wik", "iw", "rank_rope", "score_mask",
                   "score_mask_first", "index_mask", "index_mask_first"],
            s_lin: ["lWqT", "lWkvT", "lWoT", "lbq", "lbkv", "lbo", "same_head", "head_cols", "decay_col", "ones_row"],
        }
        assert {n for v in LOADS.values() for n in v} == set(LOAD)
        N_TAB, N_GLA, N_FFN, N_SSM, N_TK, N_LIN = (16 * len(v) for v in LOADS.values())

        (g_nb, g_r, g_rs, g_z, g_rect, g_ln, g_G, g_xs, g_v, g_vts, g_proj, g_exp, g_qk, g_A, g_AT, g_kT, g_kTs,
         g_dS, g_S, g_Su, g_o, g_out, g_gp, g_gate, g_osq, g_oms, g_osd, g_on, g_y) = (
            sem("gla_" + n) for n in (
                "neg_bias", "lowrank", "lowrank_copied", "gate_logits", "logits_read", "gate_log", "cumulated",
                "tile_staged", "v_projected", "v_copied", "qk_projected", "decays", "qk_scaled", "scores",
                "scores_masked", "k_turned", "k_turned_copied", "state_add", "state_ready", "first_state_used",
                "read_out", "read_out_copied", "gate_projected", "gate_ready", "squared", "mean_sq", "rms",
                "normed", "projected_out"))
        (f_w, f_x_hi, f_x, f_up, f_silu, f_gated, f_gated_hi, f_a, f_hid, f_gelu, f_lo, f_down) = (
            sem("ffn_" + n) for n in (
                "weights_rounded", "x_hi", "x_split", "up", "silu", "gated", "gated_hi", "gated_split", "hidden",
                "gelu", "gelu_split", "down"))
        ss_a, ss_u, ss_x, ss_y = (sem("ssm_" + n) for n in ("decay_ready", "inputs", "states", "outputs"))
        (t_w, t_wm, t_wc, t_cq, t_cqs, t_raw, t_ln, t_rawd, t_rows, t_rowss, t_iq, t_iqh, t_iqs, t_qp,
         t_mu, t_rot, t_rotg, t_qlat, t_qlats) = (
            sem("topk_" + n) for n in (
                "weights", "merged", "merged_copied", "cq", "cq_copied", "raw_keys", "softplus_log",
                "keys_ready", "key_rows", "key_rows_copied", "index_proj", "index_rounded", "index_split",
                "query_proj", "queries_positive", "rotated_window", "rotated_picked", "q_latent", "q_latent_copied"))
        t_tab = [sem(f"topk_rope_tables{c}") for c in range(NCH)]
        t_store_k, t_store_l, t_store_q, t_store_g = (
            sem("topk_" + n + "_stored") for n in ("keys", "latents", "window_queries", "picked_queries"))
        (i_s, i_relu, i_used, i_done, i_perm, i_idx) = (
            sem("index_" + n) for n in ("scores", "relu", "relu_used", "picked", "permuted", "ready"))
        fixed_rows = sem("fixed_rows")
        gathered = [[sem(f"gathered{b}_{g}") for g in range(NG)] for b in range(2)]
        q_loaded, a_q = sem("queries_loaded"), sem("queries_regrouped")
        v_loaded = [sem(f"local_values_loaded{b}") for b in range(2)]
        (a_rot, a_gt, a_gts, a_s, a_max, a_exp_s, a_pt, a_pts, a_pv, a_rsum, a_pn, a_otc, a_y, a_x) = (
            sem("attn_" + n) for n in (
                "rows_rotated", "rows_turned", "rows_turned_copied", "scores", "max", "probs", "probs_turned",
                "probs_copied", "values", "sum_inverted", "probs_normed", "out_copied", "projected",
                "added"))
        (l_q, l_qr, l_qf, l_kv, l_lk, l_lv, l_KV, l_W, l_nd, l_num, l_rden, l_cols, l_rt, l_o, l_y) = (
            sem("lin_" + n) for n in (
                "q", "q_relu", "q_features", "kv", "k_features", "values", "keys_x_values", "weights_ready", "num_den",
                "num_copied", "den_inverse", "den_columns", "den_spread", "normed", "projected"))
        (n_w, n_x_hi, n_x, n_up, n_silu, n_gated, n_gated_hi, n_a, n_down) = (
            sem("int_" + n) for n in ("weights_ready", "x_hi", "x_split", "up", "silu", "gated", "gated_hi",
                                      "gated_split", "down"))
        stored = sem("stored")

        ATTN_LAG = NG - 1
        PICK_SLOTS = NG * NT - 10
        SLOTS = NG * NT + ATTN_LAG + 4

        def index_width(i):
            return KTOP if i == 0 else i * P + P - LW

        def index_units(i):
            W = index_width(i)
            return [(s0, min(C, W - s0), h) for s0 in range(0, W, C) for h in range(NIH)]

        UNITS_BEFORE = [sum(len(index_units(k)) for k in range(i)) for i in range(NT + 1)]
        N_ROUNDS = JG // 8

        SUMS = [[((i, "sum", u), w + 60) for u, (_, w, _) in enumerate(index_units(i))] for i in range(NT)] + [[]]
        PICKS = [[((i, "mask", 0), 190)] +
                 [((i, what, r), index_width(i) + 60) for r in range(N_ROUNDS) for what in ("max", "index", "drop")
                  if (what, r) != ("drop", N_ROUNDS - 1)] +
                 [((i, "turn", 0), 100), ((i, "rows", 0), 100)] for i in range(NT)]

        def cost(todo):
            return sum(c for _, c in todo)

        def spread(todo, first, last):
            run, total = 0, cost(todo)
            for step, c in todo:
                SLOT_STEPS[int(first + (last - first) * run / total) + (step[1] == "rows")].append(step)
                run += c

        SLOT_STEPS = [[] for _ in range(SLOTS)]
        spread(SUMS[EARLY], 0, 1)
        start, per_slot = 1, (cost(sum(SUMS[EARLY + 1:] + PICKS[EARLY:], []))) / (PICK_SLOTS - 1)
        for i in range(EARLY, NT):
            end = start + cost(SUMS[i + 1] + PICKS[i]) / per_slot
            spread(PICKS[i], start, end)
            spread(SUMS[i + 1], start, end)
            start = end
        for todo in SLOT_STEPS:
            todo.sort(key=lambda step: (step[1] != "rows", 2 * step[0] - (step[1] == "sum")))

        GROUPS = NG * NT

        def regroups(s):
            i, at_ = divmod(s - ATTN_LAG, NG)
            i, pair = (i, 3) if at_ == 0 else (i + 1, at_ - 4)
            return (i, pair) if 0 <= i < NT and 0 <= pair < 4 and at_ != NG - 1 else None

        def score_bank(n):
            return bank[(0, 1, 4)[n % 3]]

        def turned_rows(i):
            return bank[5][:, 256:256 + P // QD] if i >= EARLY else bank[7][:, 4 * ROW:4 * ROW + P // QD]

        INDEX_BANKS = (2, 3, 4, 7, 2)

        L_GLA, L_FFN0, L_SSM, L_FFN1, L_TOPK, L_INT0, L_LIN, L_INT1 = range(8)

        def chunk(a, c):
            return a[:, bass.ds(c * C, C)]

        block = ctx.enter_context(nc.Block())

        @block.sync
        def _(sp):
            sp.dma_start(x[:, :], d["xT"]).then_inc(x_loaded, 16)
            for s, names in LOADS.items():
                for n in names:
                    sp.dma_start(LOAD[n][:], d[n]).then_inc(s, 16)
                if s is s_gla:
                    sp.dma_start(gWq, d["gWq"]).then_inc(s, 16)
                    sp.dma_start(gWk, d["gWk"]).then_inc(s, 16)
            for n, dst in (("gate_i", gate_i), ("up_i", up_i), ("down_i", down_i)):
                sp.dma_start(dst[:], d[n]).then_inc(s_int, 16)

            sp.wait_ge(x_ready, 4 * L_TOPK + 4)
            for n, dst in (("WuqT", WuqT), ("WukT", WukT), ("WuvT", WuvT), ("Wout", Wout)):
                sp.dma_start(dst, d[n]).then_inc(t_w, 16)
            for c in range(NCH):
                for k, n in enumerate(("cos_ql", "sin_ql", "cos_qg", "sin_qg")):
                    sp.dma_start(rope_tab[c][:, k, :], d[n][:, c * C:(c + 1) * C]).then_inc(t_tab[c], 16)
                sp.dma_start(key_rope[:, c * C:(c + 1) * C], d["key_rope"][:, c * C:(c + 1) * C]).then_inc(t_tab[c], 16)
            def first_rows():
                sp.wait_ge(t_store_k, STORES_K * (EARLY + 1))
                sp.wait_ge(t_rot, EARLY + 1)
                sp.wait_ge(t_rotg, EARLY + 1)
                for tq in range(QD):
                    sp.dma_start(G[0][tq * JG:(tq + 1) * JG, 0:FIXED // QD, :],
                                 key_table[LW:KTOP, :].unsqueeze(1).to_broadcast([JG, FIXED // QD, ROW]))\
                        .then_inc(fixed_rows, 16)

            for c in range(NCH):
                if c == EARLY:
                    first_rows()
                for rotated, stored_, k0, n in ((t_rot, t_store_q, 0, "l"), (t_rotg, t_store_g, 2, "g")):
                    sp.wait_ge(rotated, c + 2)
                    for k in range(2):
                        sp.dma_start(q_rot[n][k][:, c * C:(c + 1) * C], rot[:, k0 + k, :]).then_inc(stored_, 16)
                sp.wait_ge(t_rowss, c + 2)
                sp.dma_start(key_table[c * C:(c + 1) * C, :].rearrange("(b p) r -> p b r", p=P), rows)\
                    .then_inc(t_store_k, 16)
                sp.wait_ge(t_qlats, 2 * c + 2)
                for k in range(2):
                    sp.dma_start(q_lat[k * P:k * P + P, c * C:(c + 1) * C], qt_sb[:, k, :]).then_inc(t_store_l, 16)
            sp.wait_ge(t_store_q, STORES_Q * (NCH + 1))
            sp.wait_ge(t_store_g, STORES_Q * (NCH + 1))
            sp.wait_ge(t_store_l, STORES_L * (NCH + 1))
            sp.wait_ge(t_store_k, STORES_K * (NCH + 1))
            for i in range(NT):
                b = i % 2
                if i >= 1:
                    sp.wait_ge(a_q, 4 * i)
                half = DR // 2
                for dst, n in ((QL_in, "l"), (QG_in, "g")):
                    for r in range(4):
                        src = q_rot[n][r % 2][:, i * P:(i + 1) * P].rearrange("(h f) t -> f h t", f=half)
                        sp.dma_start(dst[r * half:(r + 1) * half], src).then_inc(q_loaded, 16)
                    src = q_lat[:, i * P:(i + 1) * P].rearrange("(h c) t -> c h t", c=DC)
                    sp.dma_start(dst[2 * DR:ROW], src).then_inc(q_loaded, 16)
                if i >= 2:
                    sp.wait_ge(a_pv, NG * (i - 1))
                for g in range(NG):
                    s0 = max(i * P + g * GQ - LW, 0)
                    sp.dma_start(Vloc[b][:, g, :], key_table[s0:s0 + WIN, 2 * DR:ROW]).then_inc(v_loaded[b], 16)

            sp.wait_ge(x_ready, 4 * L_INT0 + 4)
            sp.wait_ge(s_lin, N_LIN)
            sp.dma_start(decay_row, d["decay_row"]).then_inc(s_lin, 16)
            with sp.Fori(0, NCH) as c:
                sp.wait_ge(x_ready, 4 * L_INT1 + 5 + c)
                sp.dma_start(chunk(out, c), chunk(x, c)).then_inc(stored, 16)
            sp.wait_ge(stored, 16 * NCH)

        @block.gpsimd
        def _(pool):
            steps = Steps(pool, pool_step)
            pool.wait_ge(s_ffn, N_FFN)
            for dst, src in ((w1r, w1), (w2r, w2), (h1r, h1), (h2r, h2), (w3r, w3)):
                pool.tensor_copy(dst[:], src[:]).then_inc(f_w, 1)
            pool.wait_ge(s_int, 48)
            for dst, src in ((gate_w, gate_i), (up_w, up_i), (down_w, down_i)):
                pool.tensor_copy(dst[:], src[:]).then_inc(n_w, 1)

            def gather(i):
                b = i % 2
                pool.wait_ge(i_idx, i + 1)
                for q in range(FIXED // QD if i == 0 else 0, P // QD):
                    if i >= 2 and q % (GQ // QD) == 0:
                        pool.wait_ge(a_pv, NG * (i - 2) + q // (GQ // QD) + 1)
                    pool.indirect_dma_start(
                        out=G[b][:, q, :], out_offset=None, in_=key_table[0:index_width(i), :],
                        in_offset=bass.IndirectOffsetOnAxis(ap=idx_T[:, i, q:q + 1], axis=0),
                    ).then_inc(gathered[b][q // (GQ // QD)], 16)

            pool.wait_ge(x_ready, 4 * L_TOPK + 4)
            for c in range(NCH):
                pool.wait_ge(t_mu, c + 2)
                pool.wait_ge(t_tab[c], 80)
                pool.wait_ge(t_store_g, STORES_Q * (c + 1))
                cos, sin = rope_tab[c][:, 2, :], rope_tab[c][:, 3, :]
                for b, (f0, f1, op) in enumerate(((cos, sin, ALU.subtract), (sin, cos, ALU.add))):
                    steps.did(pool.tensor_tensor(rot_tg[:, 0, :], mu[c % 2][:, 0, :], f0, ALU.mult))
                    steps.did(pool.tensor_tensor(rot_tg[:, 1, :], mu[c % 2][:, 1, :], f1, ALU.mult))
                    last = pool.tensor_tensor(rot[:, 2 + b, :], rot_tg[:, 0, :], rot_tg[:, 1, :], op)
                    if b == 0:
                        steps.did(last)
                last.then_inc(t_rotg, 1)
                pool.wait_ge(t_rotg, c + 2)
                if c == EARLY:
                    pool.wait_ge(t_store_k, STORES_K * (EARLY + 1))
                    pool.wait_ge(t_rot, EARLY + 1)
                    gather(0)
            pool.wait_ge(t_rot, EARLY + 2)
            gather(1)
            pool.wait_ge(t_store_k, STORES_K * (NCH + 1))
            for i in range(EARLY, NT):
                gather(i)

        @block.tensor
        def _(pe):
            def mm(out_, lhsT, rhs, start=True, stop=True, **kw):
                return pe.matmul(out_, lhsT, rhs, start=start, stop=stop, **kw)

            def ln_center(k, r):
                for u in range(2):
                    n = 4 * k + r * 2 + u
                    pe.wait_ge(x_ready, n + 1)
                    pe.wait_ge(ln_applied, LN0 + n - 1)
                    mm(bank[4 + u], center[:], x[:, (r * 2 + u) * C:(r * 2 + u + 1) * C]).then_inc(ln_centered, 1)

            def ln_mean(k, r):
                for u in range(2):
                    pe.wait_ge(ln_squared, 4 * k + r * 2 + u + 1)
                    for j in range(C // P):
                        last = mm(bank[6 + u][:, j:j + 1], sq[:, u, j * P:(j + 1) * P], mean_col[:])
                    last.then_inc(ln_var, 1)

            def ln_spread(k, r):
                for u in range(2):
                    pe.wait_ge(ln_diag, 4 * k + r * 2 + u + 1)
                    mm(bank[6 + u], ones[:], inv_diag[:, u, :]).then_inc(ln_inv, 1)

            def layer_norm(k, pairs=(0, 1)):
                for r in pairs:
                    ln_center(k, r)
                    ln_mean(k, r)
                    ln_spread(k, r)

            def gla():
                pe.wait_ge(s_gla, N_GLA + 32)
                with pe.Fori(0, NCH) as c:
                    pe.wait_ge(ln_applied, LN0 + 4 * L_GLA + 1 + c)
                    pe.wait_ge(g_rect, GH * c + 1)
                    mm(bank[0][0:16, :], Wgk1[:], chunk(xn, c)).then_inc(g_r, 1)
                    pe.wait_ge(g_rs, c + 1)
                    for h in range(GH):
                        pe.wait_ge(g_rect, GH * c + h + 1)
                        mm(bank[h], Wgk2[:, h * GDK:(h + 1) * GDK], r_sb).then_inc(g_z, 1)
                pe.wait_ge(g_rect, GH * NCH + GH)

                def project(n, what, first=False):
                    tokens = xn[:, bass.ds(n * P, P)]
                    if what == "keys":
                        pe.wait_ge(g_xs, n + 1)
                        if not first:
                            pe.wait_ge(g_vts, n)
                        mm(bank[2][:, 0:P], xs_t, gWv[:]).then_inc(g_v, 1)
                    if not first:
                        pe.wait_ge(g_qk, 2 * n - 1 if what == "keys" else 2 * n)
                    o_, w = (bank[1], gWk) if what == "keys" else (bank[0], gWq)
                    for h in range(GH):
                        last = mm(o_[:, h * P:h * P + P], w[:, h * GDK:(h + 1) * GDK], tokens)
                    last.then_inc(g_proj, 1)

                def tile(i, u, first=False, last_tile=False):
                    pe.wait_ge(g_qk, 2 * i + 1)
                    for h in range(GH):
                        last = pe.transpose(bank[4][:, h * P:h * P + P], kI[:, h, :], ident[:])
                    last.then_inc(g_kT, 1)
                    pe.wait_ge(g_qk, 2 * i + 2)
                    for h in range(GH):
                        last = mm(bank[5][:, h * P:h * P + P], kI[:, h, :], qg[u][:, h, :])
                    last.then_inc(g_A, 1)
                    if not last_tile:
                        project(i + 1, "keys")
                    pe.wait_ge(g_kTs, i + 1)
                    pe.wait_ge(g_vts, i + 1)
                    pe.wait_ge(g_S, 2 * i + 1)
                    for half in range(2):
                        lo_, hi_ = half * GCHUNK, (half + 1) * GCHUNK
                        for h in range(GH):
                            last = mm(bank[6 + half][:, GDV * h:GDV * h + GDV],
                                      kIT[lo_:hi_, h, :], vt[u][lo_:hi_, GDV * h:GDV * h + GDV])
                    last.then_inc(g_dS, 1)
                    pe.wait_ge(g_AT, i + 1)
                    if not first:
                        pe.wait_ge(g_out, i)
                    for h in range(GH):
                        mm(bank[3][GDV * h:GDV * h + GDV, 0:P], vt[u][:, GDV * h:GDV * h + GDV], AT[:, h, :],
                           stop=False, tile_position=(0, GDV * h), skip_group_check=True)
                    for half in range(2):
                        lo_, hi_ = half * GCHUNK, (half + 1) * GCHUNK
                        if half == 1:
                            if not last_tile:
                                project(i + 1, "queries")
                            pe.wait_ge(g_S, 2 * i + 2)
                        for h in range(GH):
                            last = mm(bank[3][GDV * h:GDV * h + GDV, lo_:hi_], S[half][:, GDV * h:GDV * h + GDV],
                                      qg[u][:, h, lo_:hi_], start=False, stop=True, tile_position=(0, GDV * h),
                                      skip_group_check=True)
                        last.then_inc(g_Su if half == 0 else g_o, 1)

                project(0, "keys", first=True)
                project(0, "queries", first=True)
                tile(0, 0, first=True)
                with pe.Fori(0, NT // 2 - 1) as r:
                    for u in (1, 0):
                        tile(2 * r + 2 - u, u)
                tile(NT - 1, 1, last_tile=True)
                with pe.Fori(0, 2) as r:
                    for u in range(2):
                        c = 2 * r + u
                        pe.wait_ge(g_gate, c + 1)
                        mm(bank[u], gWg[:], chunk(xn, c)).then_inc(g_gp, 1)
                with pe.Fori(0, 2) as r:
                    for u in range(2):
                        pe.wait_ge(g_osq, 2 * r + u + 1)
                        mm(bank[2 + u], mean_head[:], o_sq[:, u, :]).then_inc(g_oms, 1)
                    for u in range(2):
                        pe.wait_ge(g_on, 2 * r + u + 1)
                        mm(bank[u], gWo[:], chunk(oT, 2 * r + u)).then_inc(g_y, 1)

            def ffn(layer, k):
                pe.wait_ge(f_w, 5)
                for r in range(2):
                    R = 2 * k + r
                    pe.wait_ge(x_ready, 4 * layer + 4 + 2 * r)
                    for u in range(2):
                        pe.wait_ge(f_x, 2 * R + u + 1)
                        for m in range(NM):
                            j = u * NM + m
                            if j >= 2:
                                pe.wait_ge(f_gated, 8 * R + j - 1)
                            for o_, w in ((bank[2 * (j % 2)], w1r), (bank[2 * (j % 2) + 1], w2r)):
                                mm(o_, w[:, m * P:m * P + P], x_hi[:, u, :], True, False)
                                last = mm(o_, w[:, m * P:m * P + P], x_lo[:, u, :], False, True)
                            last.then_inc(f_up, 1)
                    for stage, (w, hi, lo) in enumerate(((h1r, a_hi, a_lo), (h2r, b_hi, b_lo))):
                        for u in range(2):
                            for m in range(NM):
                                q = 8 * stage + 4 * u + m
                                if q < 4:
                                    pe.wait_ge(f_gated, 8 * R + 7 + m // 2)
                                else:
                                    pe.wait_ge(f_gelu, 16 * R + q - 3)
                                for kk in range(NM):
                                    if m == 0 and stage == 0:
                                        pe.wait_ge(f_a, 8 * R + u * NM + kk + 1)
                                    elif m == 0:
                                        pe.wait_ge(f_lo, 16 * R + u * NM + kk + 1)
                                    wt = w[:, kk, m * P:m * P + P]
                                    mm(bank[m], wt, hi[:, u * NM + kk, :], kk == 0, False)
                                    last = mm(bank[m], wt, lo[:, u * NM + kk, :], False, kk == NM - 1)
                                last.then_inc(f_hid, 1)
                            next_layer, next_r = (layer, 1) if r == 0 else (layer + 1, 0)
                            if stage == 0:
                                (ln_center if u == 0 else ln_mean)(next_layer, next_r)
                            elif u == 0:
                                ln_spread(next_layer, next_r)
                    for u in range(2):
                        pe.wait_ge(f_gelu, 16 * R + 13 + u)
                        for kk in range(NM):
                            pe.wait_ge(f_lo, 16 * R + 8 + u * NM + kk + 1)
                            mm(bank[u], w3r[:, kk, :], a_hi[:, u * NM + kk, :], kk == 0, False)
                            last = mm(bank[u], w3r[:, kk, :], a_lo[:, u * NM + kk, :], False, kk == NM - 1)
                        last.then_inc(f_down, 1)

            def ssm():
                pe.wait_ge(s_ssm, N_SSM)
                with pe.Fori(0, NCH) as c:
                    pe.wait_ge(ln_applied, LN0 + 4 * L_SSM + 1 + c)
                    pe.wait_ge(x_ready, 4 * L_SSM + 4 + c)
                    mm(bank[0][0:64, :], sBT[:], chunk(xn, c)).then_inc(ss_u, 1)
                    pe.wait_ge(ss_x, c + 1)
                    mm(bank[1], sCT[:], chunk(states, c)).then_inc(ss_y, 1)

            def topk_setup():
                pe.wait_ge(s_tk, N_TK)
                pe.wait_ge(t_w, 64)
                pe.wait_ge(x_ready, 4 * L_TOPK + 4)
                for h in range(NH):
                    last = mm(bank[0][0:DCQ, h * DC:(h + 1) * DC], WuqT[:, h, :], WukT[:, h, :])
                for h in range(NH):
                    last = mm(bank[1 + h // 4][0:DC, (h % 4) * P:(h % 4 + 1) * P], WuvT[:, h, :], Wout[:, h, :])
                last.then_inc(t_wm, 1)
                pe.wait_ge(t_wc, 3)
                pe.wait_ge(ln_applied, LN0 + 4 * L_TOPK + 4)

                def front(c):
                    at_ = slice(c * C, (c + 1) * C)
                    if c >= 1:
                        pe.wait_ge(t_cqs, c)
                        pe.wait_ge(t_rawd, c)
                        pe.wait_ge(t_mu, c + 1)
                    if 2 <= c < EARLY + 2:
                        pe.wait_ge(i_relu, UNITS_BEFORE[c - 1])
                    mm(bank[0][0:DCQ, :], Wdq[:], xn[:, at_]).then_inc(t_cq, 1)
                    mm(bank[1][0:ROW, :], Wkeys[:], xn[:, at_]).then_inc(t_raw, 1)
                    pe.wait_ge(t_cqs, c + 1)
                    mm(bank[5], Wqr1[:], cq[c % 2])
                    mm(bank[6], Wqr2[:], cq[c % 2]).then_inc(t_qp, 1)

                def index(c):
                    for h in range(NIH):
                        if c >= 1:
                            pe.wait_ge(*((t_iqs, 5 * c), (t_qlats, 2 * c - 1), (t_qlats, 2 * c), (t_rowss, c + 1))[h])
                        if h == NIH - 1 and 1 <= c <= EARLY:
                            pe.wait_ge(i_relu, UNITS_BEFORE[c])
                        if h == NIH - 1 and 2 <= c <= EARLY + 1:
                            pe.wait_ge(i_idx, c - 1)
                        mm(bank[INDEX_BANKS[h]], Wiq[:, h * P:(h + 1) * P], xn[:, c * C:(c + 1) * C]).then_inc(t_iq, 1)

                def back(c):
                    pe.wait_ge(t_iqs, 5 * c + 1)
                    mm(bank[INDEX_BANKS[NIH]], Wik[:], xn[:, c * C:(c + 1) * C]).then_inc(t_iq, 1)
                    pe.wait_ge(t_iqs, 5 * c + 2)
                    mm(bank[3], Mq[:, 0:P], cq[c % 2]).then_inc(t_qlat, 1)
                    pe.wait_ge(t_iqs, 5 * c + 3)
                    mm(bank[4], Mq[:, P:2 * P], cq[c % 2]).then_inc(t_qlat, 1)
                    pe.wait_ge(t_iqs, 5 * c + 4)
                    pe.wait_ge(t_rawd, c + 1)
                    for j in range(4):
                        last = pe.transpose(bank[7][:, j * ROW:(j + 1) * ROW], raw[c % 2][:, j * P:(j + 1) * P],
                                            ident[0:ROW, 0:ROW])
                    last.then_inc(t_rows, 1)

                def early(c):
                    if 1 <= c <= EARLY:
                        pe.wait_ge(t_rowss, c + 2)
                        index_turn(c - 1)
                    if c < EARLY:
                        pe.wait_ge(t_iqs, 5 * c + 5)
                        pe.wait_ge(t_mu, c + 3)
                        pe.wait_ge(t_rowss, c + 2)
                        if c >= 1:
                            pe.wait_ge(i_idx, c)
                        for k in range(len(index_units(c))):
                            index_scores(c, k)

                front(0)
                for c in range(NCH):
                    if c + 1 < NCH:
                        front(c + 1)
                    index(c)
                    back(c)
                    early(c)

            bank5_read = [None]

            def bank5_free(reader):
                if bank5_read[0]:
                    pe.wait_ge(*bank5_read[0])
                bank5_read[0] = reader

            def index_scores(i, k):
                s0, w, h = index_units(i)[k]
                u = UNITS_BEFORE[i] + k
                if u >= 2:
                    pe.wait_ge(i_relu, u - 1)
                q = q_split[h][:, i * P:(i + 1) * P]
                mm(bank[6 + u % 2][:, 0:w], q, k_hi[:, s0:s0 + w], True, False)
                mm(bank[6 + u % 2][:, 0:w], q, k_lo[:, s0:s0 + w], False, True).then_inc(i_s, 1)

            def index_turn(i):
                pe.wait_ge(i_done, i + 1)
                if i >= EARLY:
                    bank5_free((i_idx, i + 1))
                src = idx_f if i >= EARLY else early_idx_f
                for tq in range(4):
                    last = mm(turned_rows(i)[JG * tq:JG * tq + JG, :], src, ident[:, tq:P:4],
                              tile_position=(0, JG * tq), skip_group_check=True)
                last.then_inc(i_perm, 1)

            def rows_turn(n):
                pe.wait_ge(a_rot, n + 1)
                if n >= 2:
                    pe.wait_ge(a_gts, n - 1)
                for j in range(4):
                    last = pe.transpose(bank[2 + n % 2][0:ROW, j * P:(j + 1) * P], GR[n % 2][:, j, :], ident[:])
                last.then_inc(a_gt, 1)

            def scores(n):
                i, g = n // NG, n % NG
                pe.wait_ge(a_gts, n + 1)
                pe.wait_ge(a_q, 4 * i + g // 2 + 1)
                if n >= 3:
                    pe.wait_ge(a_otc, n - 2)
                s0 = max(i * P + g * GQ - LW, 0)
                sb_, w = score_bank(n), NH * QD
                mm(sb_[:, P:KEYS], QL[:, g, :], KL[:, s0:s0 + WIN])
                for j in range(4):
                    last = mm(sb_[j * w:(j + 1) * w, 0:P], QG[:, g, j * w:(j + 1) * w],
                              GT[n % 2][:, j * P:(j + 1) * P], tile_position=(0, j * w))
                last.then_inc(a_s, 1)

            def probs_turn(n):
                pe.wait_ge(a_pn, n + 1)
                pe.transpose(score_bank(n)[:, 0:P], Pr[n % 2][:, 0:P], ident[:])
                pe.transpose(score_bank(n)[0:WIN, P:2 * P], Pr[n % 2][:, P:KEYS], ident[:]).then_inc(a_pt, 1)

            def values(n):
                i, g = n // NG, n % NG
                b, w = i % 2, NH * QD
                if g == 0:
                    pe.wait_ge(v_loaded[b], 16 * NG * (i // 2 + 1))
                pe.wait_ge(a_pts, n + 1)
                o_ = score_bank(n)[0:DC, 2 * P:3 * P]
                mm(o_, Vloc[b][:, g, :], PTl[n % 2], True, False, skip_group_check=True)
                for j in range(4):
                    last = mm(o_[:, j * w:(j + 1) * w], G[b][:, g * 4 + j, 2 * DR:ROW],
                              PTg[n % 2][:, j * w:(j + 1) * w], False, True, skip_group_check=True)
                last.then_inc(a_pv, 1)

            def out_project(i):
                pe.wait_ge(a_otc, NG * (i + 1))
                bank5_free((a_x, i + 1))
                for h in range(NH):
                    last = mm(bank[5][:, 128:256], Muv[:, h, :], OT[i % 2][:, h, :], h == 0, h == NH - 1,
                              skip_group_check=True)
                last.then_inc(a_y, 1)

            def topk():
                pe.wait_ge(t_iqs, 5 * NCH)
                pe.wait_ge(t_mu, NCH + 1)
                pe.wait_ge(t_rot, NCH + 1)
                pe.wait_ge(t_rotg, NCH + 1)
                pe.wait_ge(t_rowss, NCH + 1)
                for s in range(SLOTS):
                    n = s - ATTN_LAG
                    if 0 <= n + 1 < GROUPS:
                        rows_turn(n + 1)
                    if 0 <= n < GROUPS:
                        scores(n)
                    if 0 <= n - 2 < GROUPS:
                        values(n - 2)
                    for i, what, k in SLOT_STEPS[s]:
                        if what == "sum":
                            index_scores(i, k)
                    if 0 <= n - 1 < GROUPS:
                        probs_turn(n - 1)
                    if 0 <= n - 2 < GROUPS and (n - 2) % NG == NG - 1:
                        out_project((n - 2) // NG)
                    for i, what, _ in SLOT_STEPS[s]:
                        if what == "turn":
                            index_turn(i)
                pe.wait_ge(a_x, NT)

            def int_ffn(layer, k):
                pe.wait_ge(n_w, 3)
                for r in range(2):
                    R = 2 * k + r
                    ahead = (layer, 1) if r == 0 else (layer + 1, 0) if layer == L_INT0 else None
                    pe.wait_ge(x_ready, 4 * layer + 4 + 2 * r)
                    for u in range(2):
                        pe.wait_ge(n_x, 2 * R + u + 1)
                        for m in range(NM2):
                            j = u * NM2 + m
                            if j >= 2:
                                pe.wait_ge(n_gated, 2 * NM2 * R + j - 1)
                            for o_, w in ((bank[2 * (j % 2)], gate_w), (bank[2 * (j % 2) + 1], up_w)):
                                mm(o_, w[:, m * P:m * P + P], x_hi[:, u, :], True, False)
                                last = mm(o_, w[:, m * P:m * P + P], x_lo[:, u, :], False, True)
                            last.then_inc(n_up, 1)
                        if ahead:
                            (ln_center if u == 0 else ln_mean)(*ahead)
                    pe.wait_ge(n_gated, 2 * NM2 * R + 5)
                    for u in range(2):
                        for kk in range(NM2):
                            pe.wait_ge(n_a, 2 * NM2 * R + u * NM2 + kk + 1)
                            w = down_w[:, kk * P:kk * P + P]
                            mm(bank[u], w, a_hi[:, u * NM2 + kk, :], kk == 0, False)
                            last = mm(bank[u], w, a_lo[:, u * NM2 + kk, :], False, kk == NM2 - 1)
                        last.then_inc(n_down, 1)
                        if u == 0 and ahead:
                            ln_spread(*ahead)

            def linear_attention():
                pe.wait_ge(s_lin, N_LIN)

                def keys_x_values(c):
                    for j in range(4):
                        if j % 2 == 0:
                            pe.wait_ge(l_lk, 2 * c + j // 2 + 1)
                            pe.wait_ge(l_lv, 2 * c + j // 2 + 1)
                        last = mm(bank[3][:, 0:P + 1], lk[c % 2][:, j, :], lv[c % 2][:, j, :],
                                  c == 0 and j == 0, c == NCH - 1 and j == 3)
                    last.then_inc(l_KV, 1)

                ln_center(L_LIN, 1)
                for c in range(NCH):
                    pe.wait_ge(ln_applied, LN0 + 4 * L_LIN + 1 + c)
                    if c >= 1:
                        pe.wait_ge(l_qr, c)
                    mm(bank[0], lWqT[:], xn[:, c * C:(c + 1) * C]).then_inc(l_q, 1)
                    for half in range(2):
                        if c >= 1:
                            pe.wait_ge(l_lk, 2 * c + half - 1)
                            pe.wait_ge(l_lv, 2 * c + half - 1)
                        for j in range(2):
                            o_ = bank[1 + half][:, 2 * P * j:2 * P * (j + 1)]
                            t0 = c * C + (2 * half + j) * P
                            mm(o_, xn[:, t0:t0 + P], lWkvT[:], True, False, skip_group_check=True)
                            last = mm(o_, ones_row[:], lbkv[:], False, True, skip_group_check=True)
                        last.then_inc(l_kv, 1)
                    if c >= 1:
                        keys_x_values(c - 1)
                    if c == 0:
                        ln_mean(L_LIN, 1)
                        ln_spread(L_LIN, 1)
                keys_x_values(NCH - 1)
                pe.wait_ge(l_W, 1)
                for r in range(2):
                    pe.wait_ge(x_ready, 4 * L_LIN + 4 + 2 * r)
                    for u in range(2):
                        c = 2 * r + u
                        mm(bank[u], KVm, qf[:, c * C:(c + 1) * C])
                        for j in range(4):
                            last = mm(bank[2 + u][:, j * LH:(j + 1) * LH], qf[:, c * C + j * P:c * C + (j + 1) * P],
                                      head_sums)
                        last.then_inc(l_nd, 1)
                    if r == 1:
                        ln_center(L_INT1, 0)
                        ln_mean(L_INT1, 0)
                    for u in range(2):
                        pe.wait_ge(l_cols, 2 * r + u + 1)
                        cols_ = rden_cols[u].rearrange("p a b -> p (a b)")
                        for j in range(4):
                            last = pe.transpose(bank[2 + u][:, j * P:(j + 1) * P], cols_[:, j * P:(j + 1) * P],
                                                ident[:])
                        last.then_inc(l_rt, 1)
                    if r == 1:
                        ln_spread(L_INT1, 0)
                    for u in range(2):
                        pe.wait_ge(l_o, 2 * r + u + 1)
                        mm(bank[u], lWoT[:], lo[:, u, :]).then_inc(l_y, 1)

            pe.wait_ge(s_tab, N_TAB)
            layer_norm(L_GLA)
            gla()
            layer_norm(L_FFN0, pairs=(0,))
            ffn(L_FFN0, 0)
            layer_norm(L_SSM, pairs=(1,))
            ssm()
            layer_norm(L_FFN1, pairs=(0,))
            ffn(L_FFN1, 1)
            layer_norm(L_TOPK, pairs=(1,))
            topk_setup()
            topk()
            layer_norm(L_INT0, pairs=(0,))
            int_ffn(L_INT0, 0)
            linear_attention()
            int_ffn(L_INT1, 1)

        @block.scalar
        def _(act):
            steps = Steps(act, act_step)
            fn = nc.scalar.activation

            def ln_square(k, r):
                for u in range(2):
                    act.wait_ge(ln_centered, 4 * k + r * 2 + u + 1)
                    fn(sq[:, u, :], bank[4 + u], ACT.Square).then_inc(ln_squared, 1)
                    fn(xn[:, (2 * r + u) * C:(2 * r + u + 1) * C], bank[4 + u], ACT.Copy)

            def ln_sqrt(k, r):
                for u in range(2):
                    act.wait_ge(ln_var, 4 * k + r * 2 + u + 1)
                    fn(sd_col[:, u, :], bank[6 + u][:, 0:C // P], ACT.Sqrt, bias=eps_col).then_inc(ln_sd, 1)

            def layer_norm(k, pairs=(0, 1)):
                for r in pairs:
                    ln_square(k, r)
                    ln_sqrt(k, r)

            def gla():
                act.wait_ge(g_nb, 1)
                for c in range(NCH):
                    act.wait_ge(g_r, c + 1)
                    fn(r_sb, bank[0][0:16, :], ACT.Copy).then_inc(g_rs, 1)
                    for h in range(GH):
                        act.wait_ge(g_z, GH * c + h + 1)
                        fn(chunk(G_all[:, h, :], c), bank[h], ACT.Abs, bias=bgk2[:, h:h + 1])
                        fn(chunk(relu_z[:, h, :], c), bank[h], ACT.Relu, scale=-1.0, bias=neg_bgk2[:, h:h + 1])\
                            .then_inc(g_rect, 1)
                    act.wait_ge(g_rect, GH * (c + 2))
                    g = G_all[:, :, bass.ds(c * C, C)]
                    steps.did(fn(g, g, ACT.Exp, scale=-1.0))
                steps.leave(NCH, 1)
                for c in range(NCH):
                    g = G_all[:, :, bass.ds(c * C, C)]
                    fn(g, g, ACT.Ln, bias=one_col).then_inc(g_ln, 1)

                def prepare(n, u, first=False):
                    if not first:
                        act.wait_ge(g_S, 2 * n - 1)
                        act.wait_ge(g_qk, 2 * n - 1)
                    act.wait_ge(g_G, NT)
                    fn(eG[u], G_all[:, :, bass.ds(n * P, P)], ACT.Exp, scale=-1.0 / 16)
                    fn(emG, G_all[:, :, bass.ds(n * P, P)], ACT.Exp, scale=1.0 / 16).then_inc(g_exp, 1)

                def values_copy(n, u):
                    act.wait_ge(g_v, n + 1)
                    fn(vt[u], bank[2][:, 0:P], ACT.Copy).then_inc(g_vts, 1)

                def tile(i, u, first=False, last_tile=False):
                    if not last_tile:
                        prepare(i + 1, 1 - u)
                    act.wait_ge(g_kT, i + 1)
                    if not first:
                        act.wait_ge(g_dS, i)
                    fn(kIT, bank[4].rearrange("p (h d) -> p h d", h=GH), ACT.Copy).then_inc(g_kTs, 1)
                    if not last_tile:
                        values_copy(i + 1, 1 - u)

                prepare(0, 0, first=True)
                values_copy(0, 0)
                tile(0, 0, first=True)
                with act.Fori(0, NT // 2 - 1) as r:
                    for u in (1, 0):
                        tile(2 * r + 2 - u, u)
                tile(NT - 1, 1, last_tile=True)
                for c in range(NCH):
                    act.wait_ge(g_gp, c + 1)
                    fn(chunk(gate, c), bank[c % 2], ACT.Silu).then_inc(g_gate, 1)
                act.wait_ge(g_out, NT)
                with act.Fori(0, 2) as r:
                    for u in range(2):
                        fn(o_sq[:, u, :], chunk(oT, 2 * r + u), ACT.Square).then_inc(g_osq, 1)
                    for u in range(2):
                        act.wait_ge(g_oms, 2 * r + u + 1)
                        fn(o_sd[:, u, :], bank[2 + u], ACT.Sqrt, bias=eps_col).then_inc(g_osd, 1)

            def ffn(layer, k):
                act.wait_ge(x_ready, 4 * layer + 4)

                def x_round(r):
                    for u in range(2):
                        c = 2 * r + u
                        act.wait_ge(ln_applied, LN0 + 4 * layer + c + 1)
                        if 2 * k + r > 0:
                            act.wait_ge(f_up, 8 * (2 * k + r))
                        fn(x_hi[:, u, :], xn[:, c * C:(c + 1) * C], ACT.Copy).then_inc(f_x_hi, 1)

                x_round(0)
                for r in range(2):
                    R = 2 * k + r

                    def gated_round(j):
                        act.wait_ge(f_gated, 8 * R + j + 1)
                        if R > 0 and j % NM == 0:
                            act.wait_ge(f_down, 2 * R)
                        fn(a_hi[:, j, :], f_full[:, j % 4, :], ACT.Copy).then_inc(f_gated_hi, 1)

                    for j in range(2 * NM):
                        act.wait_ge(f_up, 8 * R + j + 1)
                        if j >= 2:
                            act.wait_ge(f_gated, 8 * R + j - 1)
                        fn(f_silu_sb[:, j % 2, :], bank[2 * (j % 2)], ACT.Silu, scale=w1s[:, j % NM:j % NM + 1])\
                            .then_inc(f_silu, 1)
                        if j >= 1:
                            gated_round(j - 1)
                    gated_round(2 * NM - 1)
                    for stage, (hi, sc) in enumerate(((b_hi, h1s), (a_hi, h2s))):
                        for u in range(2):
                            for m in range(NM):
                                q = 8 * stage + 4 * u + m
                                act.wait_ge(f_hid, 16 * R + q + 1)
                                if q >= 4:
                                    act.wait_ge(f_lo, 16 * R + q - 3)
                                else:
                                    act.wait_ge(f_a, 8 * R + 5 + m)
                                if stage == 0 and R > 0 and m == 0:
                                    act.wait_ge(f_hid, 16 * R)
                                if stage == 1 and m == 0:
                                    act.wait_ge(f_hid, 16 * R + 4 * u + 4)
                                fn(f_full[:, q % 4, :], bank[m], ACT.Gelu, scale=sc[:, m:m + 1])
                                fn(hi[:, u * NM + m, :], bank[m], ACT.Gelu, scale=sc[:, m:m + 1])\
                                    .then_inc(f_gelu, 1)
                            if stage == 0:
                                next_layer, next_r = (layer, 1) if r == 0 else (layer + 1, 0)
                                (ln_square if u == 0 else ln_sqrt)(next_layer, next_r)
                        if stage == 1 and r == 0:
                            x_round(1)

            def ssm():
                act.wait_ge(s_ssm, N_SSM)
                act.wait_ge(x_ready, 4 * L_SSM + 4)
                fn(a_exp, lam[:], ACT.Exp)
                fn(a_dt, log_dt[:], ACT.Exp).then_inc(ss_a, 1)
                act.wait_ge(ss_a, 2)
                fn(a_dec, a_neg, ACT.Exp, scale=-1.0).then_inc(ss_a, 1)

            def topk_setup():
                act.wait_ge(t_wm, 1)
                fn(Mq, bank[0][0:DCQ, 0:NH * DC], ACT.Copy).then_inc(t_wc, 1)
                for a in range(2):
                    fn(Muv[:, 4 * a:4 * a + 4, :], bank[1 + a][0:DC, :].rearrange("c (h d) -> c h d", h=4),
                       ACT.Copy).then_inc(t_wc, 1)

                def front(c):
                    act.wait_ge(t_cq, c + 1)
                    fn(cq[c % 2], bank[0][0:DCQ, :], ACT.Copy).then_inc(t_cqs, 1)
                    act.wait_ge(t_raw, c + 1)
                    fn(k_abs, bank[1][0:2 * DR, :], ACT.Abs)
                    act.wait_ge(t_qp, c + 1)
                    fn(q_abs[:, 0, :], bank[5], ACT.Abs)
                    steps.did(fn(q_abs[:, 1, :], bank[6], ACT.Abs))
                    fn(k_abs, k_abs, ACT.Exp, scale=-1.0)
                    steps.did(fn(q_abs, q_abs, ACT.Exp, scale=-1.0))
                    fn(k_abs, k_abs, ACT.Ln, bias=one_col[0:2 * DR]).then_inc(t_ln, 1)
                    fn(q_abs, q_abs, ACT.Ln, bias=one_col).then_inc(t_ln, 1)

                def index_round(c, h):
                    act.wait_ge(t_iq, 5 * c + h + 1)
                    dst = q_split[h] if h < NIH else k_hi
                    fn(dst[:, c * C:(c + 1) * C], bank[INDEX_BANKS[h]], ACT.Copy).then_inc(t_iqh, 1)

                def index(c):
                    for h in range(NIH):
                        index_round(c, h)

                def back(c):
                    index_round(c, NIH)
                    act.wait_ge(t_store_l, STORES_L * (c + 1))
                    act.wait_ge(t_qlat, 2 * c + 1)
                    fn(qt_sb[:, 0, :], bank[3], ACT.Copy).then_inc(t_qlats, 1)
                    act.wait_ge(t_qlat, 2 * c + 2)
                    fn(qt_sb[:, 1, :], bank[4], ACT.Copy).then_inc(t_qlats, 1)
                    act.wait_ge(t_store_k, STORES_K * (c + 1))
                    act.wait_ge(t_rows, c + 1)
                    fn(rows, bank[7][:, 0:4 * ROW].rearrange("p (b r) -> p b r", b=4), ACT.Copy)\
                        .then_inc(t_rowss, 1)

                front(0)
                for c in range(NCH):
                    if c + 1 < NCH:
                        front(c + 1)
                    index(c)
                    back(c)
                    if c < EARLY:
                        for k in range(len(index_units(c))):
                            index_relu(c, k)
                steps.leave(2 * NCH, 1)

            def index_relu(i, k):
                s0, w, h = index_units(i)[k]
                u = UNITS_BEFORE[i] + k
                act.wait_ge(i_s, u + 1)
                if u >= 4:
                    act.wait_ge(i_used, u - 3)
                relu_ = relu if i >= EARLY else early_relu
                fn(relu_[:, u % 4, 0:w], bank[6 + u % 2][:, 0:w], ACT.Relu).then_inc(i_relu, 1)

            def queries_regroup(i, pair):
                if pair == 0:
                    act.wait_ge(q_loaded, 160 * (i + 1))
                if i >= 1:
                    act.wait_ge(a_s, NG * (i - 1) + 2 * pair + 2)
                for dst, src in ((QL, QL_in), (QG, QG_in)):
                    last = fn(dst[:, 2 * pair:2 * pair + 2, :].rearrange("r g (q h t) -> r (g q) h t", h=NH, t=QD),
                              src[:, :, 2 * GQ * pair:2 * GQ * (pair + 1)]
                              .rearrange("r h (q t) -> r q h t", t=QD), ACT.Copy)
                last.then_inc(a_q, 1)

            def rows_copy(n):
                act.wait_ge(a_gt, n + 1)
                if n >= 2:
                    act.wait_ge(a_s, n - 1)
                fn(GT[n % 2], bank[2 + n % 2][0:ROW, :], ACT.Copy).then_inc(a_gts, 1)

            def probs(n):
                act.wait_ge(a_max, n + 1)
                if n >= 2:
                    act.wait_ge(a_pt, n - 1)
                fn(Pr[n % 2], Sm[n % 2], ACT.Exp, scale=SCALE, bias=nb[:, n % 2:n % 2 + 1],
                   accum_out=ssum[:, n % 2:n % 2 + 1]).then_inc(a_exp_s, 1)

            def probs_norm(n):
                act.wait_ge(a_rsum, n + 1)
                fn(Pr[n % 2], Pr[n % 2], ACT.Copy, scale=rsum[:, n % 2:n % 2 + 1]).then_inc(a_pn, 1)

            def probs_copy(n):
                act.wait_ge(a_pt, n + 1)
                if n >= 2:
                    act.wait_ge(a_pv, n - 1)
                fn(PTl[n % 2], score_bank(n)[0:WIN, P:2 * P], ACT.Copy)
                fn(PTg[n % 2], score_bank(n)[:, 0:P], ACT.Copy).then_inc(a_pts, 1)

            def out_copy(n):
                i, g = n // NG, n % NG
                act.wait_ge(a_pv, n + 1)
                if n >= 2 * NG and g == 0:
                    act.wait_ge(a_y, i - 1)
                dst = OT[i % 2][:, :, g * GQ:(g + 1) * GQ].rearrange("c h (q t) -> c q h t", t=QD)
                fn(dst, score_bank(n)[0:DC, 2 * P:3 * P].rearrange("c (q h t) -> c q h t", h=NH, t=QD), ACT.Copy)\
                    .then_inc(a_otc, 1)

            def topk():
                act.wait_ge(t_rot, NCH + 1)
                act.wait_ge(t_rotg, NCH + 1)
                for s in range(SLOTS):
                    n = s - ATTN_LAG
                    if n == -4:
                        act.wait_ge(t_store_l, STORES_L * (NCH + 1))
                        act.wait_ge(t_store_q, STORES_Q * (NCH + 1))
                        act.wait_ge(t_store_g, STORES_Q * (NCH + 1))
                        act.wait_ge(t_store_k, STORES_K * (NCH + 1))
                    if 0 <= n + 1 < GROUPS:
                        rows_copy(n + 1)
                    if 0 <= n - 1 < GROUPS:
                        probs_norm(n - 1)
                    if 0 <= n - 2 < GROUPS:
                        out_copy(n - 2)
                    if regroups(s):
                        queries_regroup(*regroups(s))
                    for i, what, k in SLOT_STEPS[s]:
                        if what == "sum":
                            index_relu(i, k)
                    if 0 <= n - 1 < GROUPS:
                        probs_copy(n - 1)
                    if 0 <= n < GROUPS:
                        probs(n)

            def int_ffn(layer, k):
                act.wait_ge(x_ready, 4 * layer + 4)

                def x_round(r):
                    for u in range(2):
                        c = 2 * r + u
                        act.wait_ge(ln_applied, LN0 + 4 * layer + c + 1)
                        if 2 * k + r > 0:
                            act.wait_ge(n_up, 2 * NM2 * (2 * k + r))
                        fn(x_hi[:, u, :], xn[:, c * C:(c + 1) * C], ACT.Copy).then_inc(n_x_hi, 1)

                x_round(0)
                for r in range(2):
                    R = 2 * k + r
                    ahead = (layer, 1) if r == 0 else (layer + 1, 0) if layer == L_INT0 else None

                    def gated_round(j):
                        act.wait_ge(n_gated, 2 * NM2 * R + j + 1)
                        if R > 0 and j % NM2 == 0:
                            act.wait_ge(n_down, 2 * R)
                        fn(a_hi[:, j, :], f_full[:, j % 4, :], ACT.Copy).then_inc(n_gated_hi, 1)

                    for j in range(2 * NM2):
                        act.wait_ge(n_up, 2 * NM2 * R + j + 1)
                        if 2 * NM2 * R + j >= 2:
                            act.wait_ge(n_gated, 2 * NM2 * R + j - 1)
                        fn(f_silu_sb[:, j % 2, :], bank[2 * (j % 2)], ACT.Silu, scale=INT_SCALE).then_inc(n_silu, 1)
                        if j >= 1:
                            gated_round(j - 1)
                        if j == 3 and ahead:
                            ln_square(*ahead)
                    gated_round(2 * NM2 - 1)
                    if ahead:
                        ln_sqrt(*ahead)
                    if r == 0:
                        x_round(1)

            def linear_attention():
                act.wait_ge(x_ready, 4 * L_LIN + 4)
                act.wait_ge(s_lin, N_LIN)
                ln_square(L_LIN, 1)
                for c in range(NCH):
                    act.wait_ge(l_q, c + 1)
                    if c >= 2:
                        act.wait_ge(l_qf, c - 1)
                    fn(lq[:, c % 2, :], bank[0], ACT.Relu, bias=lbq[:]).then_inc(l_qr, 1)
                    for half in range(2):
                        act.wait_ge(l_kv, 2 * c + half + 1)
                        if c >= 2:
                            act.wait_ge(l_KV, c - 1)
                        for j in range(2):
                            n = 4 * c + 2 * half + j
                            last = fn(lk[c % 2][:, 2 * half + j, :], bank[1 + half][:, 2 * P * j:2 * P * j + P],
                                      ACT.Relu, scale=decay_col[:, n:n + 1])
                        last.then_inc(l_lk, 1)
                    if c == 0:
                        ln_sqrt(L_LIN, 1)
                for r in range(2):
                    for u in range(2):
                        act.wait_ge(l_nd, 2 * r + u + 1)
                        if r == 1:
                            act.wait_ge(l_o, u + 1)
                        fn(num[:, u, :], bank[u], ACT.Copy).then_inc(l_num, 1)
                    if r == 1:
                        ln_square(L_INT1, 0)
                    for u in range(2):
                        act.wait_ge(l_rden, 2 * r + u + 1)
                        if r == 1:
                            act.wait_ge(l_rt, u + 1)
                        fn(rden_cols[u], rden[:, u, :].unsqueeze(2).to_broadcast([P, 4 * LH, LDK]), ACT.Copy)\
                            .then_inc(l_cols, 1)
                    if r == 1:
                        ln_sqrt(L_INT1, 0)

            act.wait_ge(s_tab, N_TAB)
            layer_norm(L_GLA)
            gla()
            layer_norm(L_FFN0, pairs=(0,))
            ffn(L_FFN0, 0)
            layer_norm(L_SSM, pairs=(1,))
            ssm()
            layer_norm(L_FFN1, pairs=(0,))
            ffn(L_FFN1, 1)
            layer_norm(L_TOPK, pairs=(1,))
            topk_setup()
            topk()
            layer_norm(L_INT0, pairs=(0,))
            int_ffn(L_INT0, 0)
            linear_attention()
            int_ffn(L_INT1, 1)

        @block.vector
        def _(dve):
            v = nc.vector
            steps = Steps(dve, dve_step)

            def ln_invert(k, r):
                for u in range(2):
                    dve.wait_ge(ln_sd, 4 * k + r * 2 + u + 1)
                    steps.did(v.reciprocal(sd_col[:, u, :], sd_col[:, u, :]))
                    v.tensor_tensor(inv_diag[:, u, :].rearrange("p (j t) -> p j t", t=P),
                                    ident[:].unsqueeze(1).to_broadcast([P, C // P, P]),
                                    sd_col[:, u, :].unsqueeze(2).to_broadcast([P, C // P, P]), ALU.mult)\
                        .then_inc(ln_diag, 1)

            def ln_apply(k, r):
                for u in range(2):
                    c = 2 * r + u
                    dve.wait_ge(ln_inv, 4 * k + c + 1)
                    v.tensor_tensor(xn[:, c * C:(c + 1) * C], xn[:, c * C:(c + 1) * C], bank[6 + u], ALU.mult)\
                        .then_inc(ln_applied, 1)

            def layer_norm(k, pairs=(0, 1)):
                for r in pairs:
                    ln_invert(k, r)
                    ln_apply(k, r)
                steps.leave(steps.k, 1)

            def heads(a, n=GH):
                return a.rearrange("p (h t) -> p h t", h=n)

            def gla():
                dve.wait_ge(s_gla, N_GLA + 32)
                v.tensor_scalar(neg_bgk2, bgk2[:], -1.0, None, ALU.mult).then_inc(g_nb, 1)
                v.memset(S[0], 0.0).then_inc(g_S, 1)
                with dve.Fori(0, NCH) as c:
                    steps.enter(c, 1)
                    dve.wait_ge(g_ln, c + 1)
                    g, z = (a[:, :, bass.ds(c * C, C)] for a in (G_all, relu_z))
                    steps.did(v.tensor_tensor(z, z, g, ALU.add))
                    for h in range(GH):
                        last = v.tensor_tensor_scan(chunk(G_all[:, h, :], c), scan_keep[:], chunk(relu_z[:, h, :], c),
                                                    0.0, ALU.mult, ALU.add)
                    last.then_inc(g_G, C // P)
                steps.leave(1, NCH)

                def scale_k(n):
                    dve.wait_ge(g_exp, n + 1)
                    dve.wait_ge(g_proj, 2 * n + 1)
                    v.tensor_tensor(kI, heads(bank[1]), emG, ALU.mult).then_inc(g_qk, 1)

                def scale_q(n, u):
                    dve.wait_ge(g_proj, 2 * n + 2)
                    v.scalar_tensor_tensor(qg[u], heads(bank[0]), GDK ** -0.5, eG[u], ALU.mult, ALU.mult)\
                        .then_inc(g_qk, 1)

                def stage(n):
                    v.tensor_copy(xs_t, xn[:, bass.ds(n * P, P)]).then_inc(g_xs, 1)

                def read_out(n):
                    dve.wait_ge(g_o, n + 1)
                    v.tensor_copy(oT[:, bass.ds(n * P, P)], bank[3][:, 0:P]).then_inc(g_out, 1)

                def tile(i, u, first=False, last_tile=False):
                    if not last_tile:
                        dve.wait_ge(g_v, i + 1)
                        stage(i + 1)
                    dve.wait_ge(g_A, i + 1)
                    if not first:
                        dve.wait_ge(g_o, i)
                    v.tensor_tensor(AT, heads(bank[5]), gla_mask[:].unsqueeze(1).to_broadcast([P, GH, P]),
                                    ALU.mult).then_inc(g_AT, 1)
                    if not first:
                        read_out(i - 1)
                    if not last_tile:
                        scale_k(i + 1)
                    dve.wait_ge(g_dS, i + 1)
                    for half in range(2):
                        dve.wait_ge(g_S, 2 * i + half + 1)
                        steps.did(v.tensor_tensor(S_in, S[half], bank[6 + half][:, 0:P], ALU.add))
                        if half == 1:
                            dve.wait_ge(g_Su, i + 1)
                        end = (half + 1) * GCHUNK - 1
                        v.tensor_tensor(heads(S[1 - half]), heads(S_in),
                                        eG[u][:, :, end:end + 1].to_broadcast([P, GH, GDV]), ALU.mult)\
                            .then_inc(g_S, 1)
                    if not last_tile:
                        scale_q(i + 1, 1 - u)

                stage(0)
                scale_k(0)
                scale_q(0, 0)
                steps.enter(0, 2)
                tile(0, 0, first=True)
                steps.leave(2, 1)
                with dve.Fori(0, NT // 2 - 1) as r:
                    steps.enter(r, 4)
                    for u in (1, 0):
                        tile(2 * r + 2 - u, u)
                steps.leave(4, NT // 2 - 1)
                tile(NT - 1, 1, last_tile=True)
                steps.leave(2, 1)
                read_out(NT - 1)
                with dve.Fori(0, 2) as r:
                    steps.enter(r, 4)
                    for u in range(2):
                        c = 2 * r + u
                        dve.wait_ge(g_osd, c + 1)
                        steps.did(v.reciprocal(o_sd[:, u, :], o_sd[:, u, :]))
                        steps.did(v.tensor_tensor(chunk(oT, c), chunk(oT, c), o_sd[:, u, :], ALU.mult))
                        dve.wait_ge(g_gate, c + 3)
                        v.scalar_tensor_tensor(chunk(oT, c), chunk(oT, c), gnw[:], chunk(gate, c), ALU.mult, ALU.mult)\
                            .then_inc(g_on, 1)
                    for u in range(2):
                        c = 2 * r + u
                        dve.wait_ge(g_y, c + 1)
                        v.tensor_tensor(chunk(x, c), chunk(x, c), bank[u], ALU.add).then_inc(x_ready, 1)
                steps.leave(4, 2)

            def ffn(layer, k):
                dve.wait_ge(s_ffn, N_FFN)

                def x_rest(r):
                    for u in range(2):
                        c = 2 * r + u
                        dve.wait_ge(f_x_hi, 4 * k + c + 1)
                        v.tensor_tensor(x_lo[:, u, :], xn[:, c * C:(c + 1) * C], x_hi[:, u, :], ALU.subtract)\
                            .then_inc(f_x, 1)

                x_rest(0)
                for r in range(2):
                    R = 2 * k + r

                    def gated_rest(j):
                        dve.wait_ge(f_gated_hi, 8 * R + j + 1)
                        v.tensor_tensor(a_lo[:, j, :], f_full[:, j % 4, :], a_hi[:, j, :], ALU.subtract)\
                            .then_inc(f_a, 1)

                    for j in range(2 * NM):
                        m = j % NM
                        dve.wait_ge(f_silu, 8 * R + j + 1)
                        if j >= 4:
                            dve.wait_ge(f_a, 8 * R + j - 3)
                        elif R > 0:
                            dve.wait_ge(f_lo, 16 * R)
                        v.scalar_tensor_tensor(f_full[:, j % 4, :], bank[2 * (j % 2) + 1], w2s[:, m:m + 1],
                                               f_silu_sb[:, j % 2, :], ALU.mult, ALU.mult).then_inc(f_gated, 1)
                        if j >= 1:
                            gated_rest(j - 1)
                    gated_rest(2 * NM - 1)
                    for q in range(4 * NM):
                        hi, lo = (b_hi, b_lo) if q < 2 * NM else (a_hi, a_lo)
                        dve.wait_ge(f_gelu, 16 * R + q + 1)
                        v.tensor_tensor(lo[:, q % 8, :], f_full[:, q % 4, :], hi[:, q % 8, :], ALU.subtract)\
                            .then_inc(f_lo, 1)
                        next_layer, next_r = (layer, 1) if r == 0 else (layer + 1, 0)
                        if q == 7:
                            ln_invert(next_layer, next_r)
                        elif q == 11:
                            ln_apply(next_layer, next_r)
                    if r == 0:
                        x_rest(1)
                    for u in range(2):
                        c = 2 * r + u
                        dve.wait_ge(f_down, 2 * R + u + 1)
                        v.scalar_tensor_tensor(x[:, c * C:(c + 1) * C], bank[u], w3s[:], x[:, c * C:(c + 1) * C],
                                               ALU.mult, ALU.add).then_inc(x_ready, 1)
                steps.leave(steps.k, 1)

            def ssm():
                dve.wait_ge(s_ssm, N_SSM)
                dve.wait_ge(ss_a, 1)
                v.tensor_tensor(a_neg, a_exp, a_dt, ALU.mult).then_inc(ss_a, 1)
                steps.did(v.memset(keep, 1.0))
                dve.wait_ge(ss_a, 3)
                steps.did(v.tensor_scalar(keep, keep, a_dec, None, ALU.mult))
                steps.did(v.memset(carry, 0.0))
                steps.leave(3, 1)
                with dve.Fori(0, NCH) as c:
                    steps.enter(c, 2)
                    dve.wait_ge(ss_u, c + 1)
                    v.tensor_tensor_scan(chunk(states, c), keep, bank[0][0:64, :], carry, ALU.mult, ALU.add)\
                        .then_inc(ss_x, 1)
                    dve.wait_ge(ss_x, c + 1)
                    steps.did(v.tensor_copy(carry, states[:, bass.ds(c * C + C - 1, 1)]))
                    dve.wait_ge(ln_applied, LN0 + 4 * L_SSM + 4)
                    steps.did(v.scalar_tensor_tensor(chunk(x, c), chunk(xn, c), sD[:], chunk(x, c),
                                                     ALU.mult, ALU.add))
                    dve.wait_ge(ss_y, c + 1)
                    v.tensor_tensor(chunk(x, c), chunk(x, c), bank[1], ALU.add).then_inc(x_ready, 1)
                steps.leave(2, NCH)

            def topk_setup():
                dve.wait_ge(s_tk, N_TK)

                def front(c):
                    at_, raw_, mu_ = slice(c * C, (c + 1) * C), raw[c % 2], mu[c % 2]
                    dve.wait_ge(t_ln, 2 * c + 1)
                    if c >= 2:
                        dve.wait_ge(t_rows, c - 1)
                        dve.wait_ge(t_rotg, c)
                    v.scalar_tensor_tensor(raw_[0:2 * DR, :], bank[1][0:2 * DR, :], 0.0, k_abs, ALU.max, ALU.add)
                    v.tensor_copy(raw_[2 * DR:ROW, :], bank[1][2 * DR:ROW, :]).then_inc(t_rawd, 1)
                    dve.wait_ge(t_ln, 2 * c + 2)
                    v.scalar_tensor_tensor(mu_[:, 0, :], bank[5], 0.0, q_abs[:, 0, :], ALU.max, ALU.add)
                    v.scalar_tensor_tensor(mu_[:, 1, :], bank[6], 0.0, q_abs[:, 1, :], ALU.max, ALU.add)\
                        .then_inc(t_mu, 1)
                    dve.wait_ge(t_mu, c + 2)
                    dve.wait_ge(t_rawd, c + 1)
                    dve.wait_ge(t_tab[c], 80)
                    v.tensor_tensor(KL[0:2 * DR, at_], raw_[0:2 * DR, :], key_rope[:, at_], ALU.mult)
                    v.tensor_copy(KL[2 * DR:ROW, at_], raw_[2 * DR:ROW, :])

                def index_rest(c, h):
                    dve.wait_ge(t_iqh, 5 * c + h + 1)
                    at_ = slice(c * C, (c + 1) * C)
                    part_, hi, lo = (slice(64, P), q_split[h], q_split[h]) if h < NIH else (slice(0, P), k_hi, k_lo)
                    v.tensor_tensor(lo[part_, at_], bank[INDEX_BANKS[h]][part_, :], hi[part_, at_], ALU.subtract)\
                        .then_inc(t_iqs, 1)

                def rotate(c):
                    at_, mu_ = slice(c * C, (c + 1) * C), mu[c % 2]
                    dve.wait_ge(t_store_q, STORES_Q * (c + 1))
                    cos, sin = rope_tab[c][:, 0, :], rope_tab[c][:, 1, :]
                    for b, (f0, f1, op) in enumerate(((cos, sin, ALU.subtract), (sin, cos, ALU.add))):
                        steps.did(v.tensor_tensor(rot_t[:, 0, :], mu_[:, 0, :], f0, ALU.mult))
                        steps.did(v.tensor_tensor(rot_t[:, 1, :], mu_[:, 1, :], f1, ALU.mult))
                        last = v.tensor_tensor(rot[:, b, :], rot_t[:, 0, :], rot_t[:, 1, :], op)
                        if b == 0:
                            steps.did(last)
                    last.then_inc(t_rot, 1)
                    dve.wait_ge(t_rot, c + 2)

                front(0)
                for c in range(NCH):
                    rotate(c)
                    if c + 1 < NCH:
                        front(c + 1)
                    for h in range(NIH + 1):
                        index_rest(c, h)
                    if 1 <= c <= EARLY:
                        pick(c - 1, "rows", 0)
                    if c < EARLY:
                        for step, _ in SUMS[c] + PICKS[c][:-1]:
                            pick(*step)
                steps.leave(steps.k, 1)

            def pick(i, what, k):
                W = index_width(i)
                is_early = i < EARLY
                sc = (early_I_s if is_early else I_s)[:, i % 2, 0:W]
                best = (early_top8 if is_early else top8)[:, 8 * (k % N_ROUNDS):8 * (k % N_ROUNDS) + 8]
                if what == "sum":
                    s0, w, h = index_units(i)[k]
                    u = UNITS_BEFORE[i] + k
                    dve.wait_ge(i_relu, u + 1)
                    r_, s_ = (early_relu if is_early else relu)[:, u % 4, 0:w], sc[:, s0:s0 + w]
                    if h == 0:
                        ins = v.tensor_scalar(s_, r_, iw[:, 0:1], None, ALU.mult)
                    else:
                        dve.wait_ge(i_used, u)
                        ins = v.scalar_tensor_tensor(s_, r_, iw[:, h:h + 1], s_, ALU.mult, ALU.add)
                    ins.then_inc(i_used, 1)
                elif what == "mask":
                    dve.wait_ge(i_used, UNITS_BEFORE[i + 1])
                    if i == 0:
                        steps.did(v.tensor_tensor(sc, sc, index_mask_first[:], ALU.add))
                    else:
                        steps.did(v.tensor_tensor(sc[:, W - P:W], sc[:, W - P:W], index_mask[:], ALU.add))
                elif what == "max":
                    steps.did(v.max(best, sc))
                elif what == "index":
                    steps.did(v.max_index(idx_u[:, 8 * k:8 * k + 8], best, sc))
                elif what == "drop":
                    steps.did(v.match_replace(sc, best, sc, TAKEN))
                elif what == "turn":
                    if i >= 1:
                        dve.wait_ge(i_perm, i)
                    v.tensor_copy(early_idx_f if is_early else idx_f, idx_u[:]).then_inc(i_done, 1)
                    dve.wait_ge(i_done, i + 1)
                else:
                    dve.wait_ge(i_perm, i + 1)
                    v.tensor_copy(idx_T[:, i, :], turned_rows(i)).then_inc(i_idx, 1)

            def rows_rotate(n):
                i, g = n // NG, n % NG
                if n < FIXED // GQ:
                    dve.wait_ge(fixed_rows, 16 * QD)
                else:
                    gathers = i // 2 + (i % 2 == 1 or g >= FIXED // GQ)
                    dve.wait_ge(gathered[i % 2][g], 16 * GQ // QD * gathers)
                if n >= 2:
                    dve.wait_ge(a_gt, n - 1)
                v.tensor_tensor(GR[n % 2], G[i % 2][:, 4 * g:4 * g + 4, :],
                                rank_rope[:].unsqueeze(1).to_broadcast([P, 4, ROW]), ALU.mult).then_inc(a_rot, 1)

            def row_max(n):
                i, g = n // NG, n % NG
                b = n % 2
                dve.wait_ge(a_s, n + 1)
                if n >= 2:
                    dve.wait_ge(a_exp_s, n - 1)
                mask = score_mask_first if i * P + g * GQ < LW else score_mask
                steps.did(v.tensor_tensor_reduce(out=Sm[b], in0=score_bank(n)[:, 0:KEYS], in1=mask[:], scale=1.0,
                                                 scalar=LOWEST, op0=ALU.add, op1=ALU.max,
                                                 accum_out=mx[:, b:b + 1]))
                v.tensor_scalar(nb[:, b:b + 1], mx[:, b:b + 1], -SCALE, None, ALU.mult).then_inc(a_max, 1)

            def sum_invert(n):
                b = n % 2
                dve.wait_ge(a_exp_s, n + 1)
                v.reciprocal(rsum[:, b:b + 1], ssum[:, b:b + 1]).then_inc(a_rsum, 1)

            def add_tile(i):
                dve.wait_ge(a_y, i + 1)
                xt = x[:, i * P:(i + 1) * P]
                v.tensor_tensor(xt, xt, bank[5][:, 128:256], ALU.add).then_inc(a_x, 1)
                if i % 4 == 3:
                    dve.wait_ge(a_x, i + 1)
                    v.engine_nop().then_inc(x_ready, 1)

            def topk():
                dve.wait_ge(t_rowss, NCH + 1)
                dve.wait_ge(t_rotg, NCH + 1)
                for s in range(SLOTS):
                    n = s - ATTN_LAG
                    if n == -2:
                        dve.wait_ge(t_store_q, STORES_Q * (NCH + 1))
                        dve.wait_ge(t_store_g, STORES_Q * (NCH + 1))
                        dve.wait_ge(t_store_l, STORES_L * (NCH + 1))
                        dve.wait_ge(t_store_k, STORES_K * (NCH + 1))
                    if 0 <= n + 2 < GROUPS:
                        rows_rotate(n + 2)
                    if 0 <= n - 1 < GROUPS:
                        sum_invert(n - 1)
                    if 0 <= n - 3 < GROUPS and (n - 3) % NG == NG - 1:
                        add_tile((n - 3) // NG)
                    todo = list(SLOT_STEPS[s])
                    while todo and todo[0][1] != "sum":
                        pick(*todo.pop(0))
                    if 0 <= n < GROUPS:
                        row_max(n)
                    for step in todo:
                        pick(*step)
                steps.leave(steps.k, 1)

            def int_ffn(layer, k):
                def x_rest(r):
                    for u in range(2):
                        c = 2 * r + u
                        dve.wait_ge(n_x_hi, 4 * k + c + 1)
                        v.tensor_tensor(x_lo[:, u, :], xn[:, c * C:(c + 1) * C], x_hi[:, u, :], ALU.subtract)\
                            .then_inc(n_x, 1)

                x_rest(0)
                for r in range(2):
                    R = 2 * k + r
                    ahead = (layer, 1) if r == 0 else (layer + 1, 0) if layer == L_INT0 else None

                    def gated_rest(j):
                        dve.wait_ge(n_gated_hi, 2 * NM2 * R + j + 1)
                        v.tensor_tensor(a_lo[:, j, :], f_full[:, j % 4, :], a_hi[:, j, :], ALU.subtract)\
                            .then_inc(n_a, 1)

                    for j in range(2 * NM2):
                        dve.wait_ge(n_silu, 2 * NM2 * R + j + 1)
                        if 2 * NM2 * R + j >= 4:
                            dve.wait_ge(n_a, 2 * NM2 * R + (j - 3 if j >= 4 else 0))
                        v.scalar_tensor_tensor(f_full[:, j % 4, :], bank[2 * (j % 2) + 1], INT_SCALE,
                                               f_silu_sb[:, j % 2, :], ALU.mult, ALU.mult).then_inc(n_gated, 1)
                        if j >= 1:
                            gated_rest(j - 1)
                    gated_rest(2 * NM2 - 1)
                    if ahead:
                        ln_invert(*ahead)
                    for u in range(2):
                        c = 2 * r + u
                        dve.wait_ge(n_down, 2 * R + u + 1)
                        v.scalar_tensor_tensor(x[:, c * C:(c + 1) * C], bank[u], INT_SCALE, x[:, c * C:(c + 1) * C],
                                               ALU.mult, ALU.add).then_inc(x_ready, 1)
                        if u == 0 and ahead:
                            ln_apply(*ahead)
                    if r == 0:
                        x_rest(1)
                steps.leave(steps.k, 1)

            def linear_attention():
                dve.wait_ge(s_lin, N_LIN)
                for b in range(2):
                    steps.did(v.memset(lv[b], 1.0))
                dve.wait_ge(s_lin, N_LIN + 16)
                for c in range(NCH):
                    dve.wait_ge(l_qr, c + 1)
                    v.tensor_tensor(qf[:, c * C:(c + 1) * C], lq[:, c % 2, :], decay_row[:, c * C:(c + 1) * C],
                                    ALU.mult).then_inc(l_qf, 1)
                    for half in range(2):
                        dve.wait_ge(l_lk, 2 * c + half + 1)
                        if c >= 2:
                            dve.wait_ge(l_KV, c - 1)
                        v.tensor_copy(lv[c % 2][:, 2 * half:2 * half + 2, 0:P],
                                      bank[1 + half].rearrange("p (j a) -> p j a", j=2)[:, :, P:2 * P])\
                            .then_inc(l_lv, 1)
                    if c == 0:
                        ln_invert(L_LIN, 1)
                        ln_apply(L_LIN, 1)
                dve.wait_ge(l_KV, NCH)
                steps.did(v.tensor_copy(k_sum, bank[3][:, P:P + 1]))
                v.tensor_scalar(head_sums, head_cols[:], k_sum, None, ALU.mult)
                v.tensor_tensor(KVm, bank[3][:, 0:P], same_head[:], ALU.mult).then_inc(l_W, 1)
                for r in range(2):
                    for u in range(2):
                        dve.wait_ge(l_nd, 2 * r + u + 1)
                        if r == 1:
                            dve.wait_ge(l_cols, u + 1)
                        steps.did(v.tensor_scalar(den[:, u, :], bank[2 + u][:, 0:4 * LH], EPS_LIN, None, ALU.add))
                        v.reciprocal(rden[:, u, :], den[:, u, :]).then_inc(l_rden, 1)
                    if r == 1:
                        ln_invert(L_INT1, 0)
                    for u in range(2):
                        dve.wait_ge(l_rt, 2 * r + u + 1)
                        dve.wait_ge(l_num, 2 * r + u + 1)
                        if r == 1:
                            dve.wait_ge(l_y, u + 1)
                        v.tensor_tensor(lo[:, u, :], num[:, u, :], bank[2 + u], ALU.mult).then_inc(l_o, 1)
                    if r == 1:
                        ln_apply(L_INT1, 0)
                    for u in range(2):
                        c = 2 * r + u
                        dve.wait_ge(l_y, 2 * r + u + 1)
                        v.scalar_tensor_tensor(x[:, c * C:(c + 1) * C], bank[u], lbo[:], x[:, c * C:(c + 1) * C],
                                               ALU.add, ALU.add).then_inc(x_ready, 1)
                steps.leave(steps.k, 1)

            v.engine_nop().then_inc(ln_applied, LN0)
            for s, free in ((g_rect, GH), (g_gate, 2), (t_mu, 1), (t_rot, 1), (t_rotg, 1), (t_rowss, 1),
                            (t_store_k, STORES_K), (t_store_l, STORES_L), (t_store_q, STORES_Q), (t_store_g, STORES_Q)):
                v.engine_nop().then_inc(s, free)
            dve.wait_ge(x_loaded, 16)
            v.engine_nop().then_inc(x_ready, 4)
            layer_norm(L_GLA)
            gla()
            layer_norm(L_FFN0, pairs=(0,))
            ffn(L_FFN0, 0)
            layer_norm(L_SSM, pairs=(1,))
            ssm()
            layer_norm(L_FFN1, pairs=(0,))
            ffn(L_FFN1, 1)
            layer_norm(L_TOPK, pairs=(1,))
            topk_setup()
            topk()
            layer_norm(L_INT0, pairs=(0,))
            int_ffn(L_INT0, 0)
            linear_attention()
            int_ffn(L_INT1, 1)


def lay_out(i):
    A, B, F, K, L, N = "L0_attn_a_", "L0_attn_b_", "L0_ffn_", "L1_attn_a_", "L1_attn_b_", "L1_ffn_"

    def fold(w):
        return w.reshape(-1, P, w.shape[1]).transpose(1, 0, 2)

    def col(w):
        return w.reshape(-1, P).T

    d = {"xT": i[A + "x"][0].T}
    for n in ("Wq", "Wk", "Wv", "Wg", "Wo"):
        d["g" + n] = i[A + n]
    d["Wgk1"], d["Wgk2"], d["bgk2"] = i[A + "Wgk1"], i[A + "Wgk2"], col(i[A + "bgk2"])
    d["gnw"] = np.tile(i[A + "gnw"], GH)[:, None]
    d["lam"] = i[B + "Lambda"][:, None]
    d["log_dt"] = np.tile(i[B + "log_dt"], 64)[:, None]
    d["sBT"], d["sCT"], d["sD"] = i[B + "B"].T, i[B + "C"].T, i[B + "D"][:, None]
    d["w1"], d["w2"] = i[F + "w1_w"].T, i[F + "w2_w"].T
    for n in ("h1", "h2", "w3"):
        d[n] = fold(i[F + n + "_w"].T)
    for n in ("w1", "w2", "h1", "h2", "w3"):
        d[n + "s"] = col(i[F + n + "_s"])
    half = DR // 2
    kr = i[K + "W_kr"]
    d["Wkeys"] = np.concatenate([kr, kr[:, half:], kr[:, :half], i[K + "W_dkv"]], axis=1)
    d["Wdq"] = i[K + "W_dq"]
    qr = i[K + "W_qr"].reshape(DCQ, NH, DR)
    d["Wqr1"], d["Wqr2"] = qr[:, :, :half].reshape(DCQ, P), qr[:, :, half:].reshape(DCQ, P)
    for n, w in (("WuqT", "W_uq"), ("WukT", "W_uk"), ("WuvT", "W_uv")):
        d[n] = i[K + w].reshape(-1, NH, DH).transpose(2, 1, 0)
    d["Wout"] = i[K + "W_out"].reshape(NH, DH, P).transpose(1, 0, 2)
    d["Wiq"] = np.tile(i[K + "idx_wq"].reshape(-1, NIH, 1, DH), (1, 1, 2, 1)).reshape(-1, 2 * NIH * DH)
    d["Wik"] = np.concatenate([i[K + "idx_wk"]] * 2, axis=1)
    d["iw"] = np.tile(i[K + "idx_w"][None, :], (P, 1))
    d["lWqT"], d["lWoT"] = i[L + "W_q"].T, i[L + "W_o"].T
    d["lWkvT"] = np.concatenate([i[L + "W_k"].T, i[L + "W_v"].T], axis=1)
    d["lbkv"] = np.concatenate([i[L + "b_k"], i[L + "b_v"]])[None, :]
    d["lbq"], d["lbo"] = i[L + "b_q"][:, None], i[L + "b_o"][:, None]
    d["gate_i"], d["up_i"] = i[N + "w_gate"].T, i[N + "w_up"].T
    d["down_i"] = fold(i[N + "w_down"].T).reshape(P, HID2)
    return d


def kernel(**inputs):
    import concourse.bacc as bacc
    from concourse.bass_utils import run_bass_kernel_spmd

    nc = bacc.Bacc("TRN2", target_bir_lowering=False, num_devices=1)
    arrays = {n: np.ascontiguousarray(a) for n, a in
              {**lay_out({n: np.asarray(a) for n, a in inputs.items()}), **shape_tables()}.items()}
    aps = {n: nc.dram_tensor("in_" + n, a.shape, mybir.dt.from_np(a.dtype), kind="ExternalInput").ap()
           for n, a in arrays.items()}
    out = nc.dram_tensor("out", (P, T), F32, kind="ExternalOutput").ap()
    hybrid_kernel(nc, aps, out)
    r = run_bass_kernel_spmd(nc, [{"in_" + n: a for n, a in arrays.items()}], core_ids=[0])
    return np.ascontiguousarray(r.results[0]["out"].T)[None]
```
